# Optimizing a Trainium2 kernel written in Bass

```python
import numpy as np
import jax
import jax.numpy as jnp

def _softmax(x, axis=-1):
    return jax.nn.softmax(x, axis=axis)

def _gelu(x):
    return jax.nn.gelu(x, approximate=True)

def _silu(x):
    return jax.nn.silu(x)

def _sigmoid(x):
    return jax.nn.sigmoid(x)

def _layernorm(x, axis=-1, eps=1e-05):
    m = jnp.mean(x, axis=axis, keepdims=True)
    v = jnp.var(x, axis=axis, keepdims=True)
    return (x - m) / jnp.sqrt(v + eps)

def _scatter_add(tgt, idx, src, axis=0):
    return tgt.at[idx].add(src)

def _segment_sum(src, seg, n):
    return jax.ops.segment_sum(src, seg, n)
kernel_name = 'mk_prb_d1_jaxref_r8_84eb24'

def setup_inputs(seed: int=0):
    np.random.seed(seed)
    _w = jnp.asarray

    def _L0_attn_setup():
        import jax, jax.numpy as jnp
        import numpy as np
        HIDDEN = 256
        NUM_HEADS = 16
        HEAD_DIM = HIDDEN // NUM_HEADS
        HARMONICS = 64

        def _holo_params(key, in_features, out_features, harmonics):
            kb, kp = jax.random.split(key)
            basis = jax.random.normal(kb, (harmonics, in_features), dtype=jnp.float32)
            basis = basis / jnp.linalg.norm(basis, axis=1, keepdims=True)
            phase = jax.random.normal(kp, (out_features, harmonics), dtype=jnp.float32) * 0.1
            amp = jnp.ones((out_features, harmonics), dtype=jnp.float32) / np.sqrt(harmonics).astype(np.float32)
            return (basis, phase, amp)

        def _holo_linear(x, basis, phase, amp):
            resonance = jnp.einsum('bsd,hd->bsh', x, basis)
            w = amp * jnp.cos(phase)
            return jnp.einsum('bsh,oh->bso', resonance, w)
        key = jax.random.key(seed)
        ks = jax.random.split(key, 5)
        hidden_states = jax.random.normal(ks[0], (2, 256, HIDDEN), dtype=jnp.float32)
        inp = {'hidden_states': hidden_states}
        for name, k in zip(('q', 'k', 'v', 'o'), ks[1:]):
            basis, phase, amp = _holo_params(k, HIDDEN, HIDDEN, HARMONICS)
            inp[f'basis_{name}'] = basis
            inp[f'phase_{name}'] = phase
            inp[f'amp_{name}'] = amp
        return inp
    _L0_attn_in = _L0_attn_setup()

    def _L0_ffn_setup():
        import jax, jax.numpy as jnp
        import numpy as np
        B, S, H = (2, 256, 256)
        E, K, F = (32, 4, 176)
        FS = 704
        EPS = 1e-06
        CAP = 128
        key = jax.random.key(seed)
        ks = jax.random.split(key, 10)
        s = 0.02
        return {'hidden_states': jax.random.normal(ks[0], (B, S, H), jnp.float32), 'w_norm': 1.0 + 0.02 * jax.random.normal(ks[1], (H,), jnp.float32), 'w_router': s * jax.random.normal(ks[2], (H, E), jnp.float32), 'w_gate': s * jax.random.normal(ks[3], (E, H, F), jnp.float32), 'w_up': s * jax.random.normal(ks[4], (E, H, F), jnp.float32), 'w_down': s * jax.random.normal(ks[5], (E, F, H), jnp.float32), 'sw_gate': s * jax.random.normal(ks[6], (H, FS), jnp.float32), 'sw_up': s * jax.random.normal(ks[7], (H, FS), jnp.float32), 'sw_down': s * jax.random.normal(ks[8], (FS, H), jnp.float32), 'w_shared_gate': s * jax.random.normal(ks[9], (H, 1), jnp.float32)}
    _L0_ffn_in = _L0_ffn_setup()
    _d = {'L0_attn_hidden_states': _L0_attn_in['hidden_states'], 'L0_attn_basis_q': _L0_attn_in['basis_q'], 'L0_attn_phase_q': _L0_attn_in['phase_q'], 'L0_attn_amp_q': _L0_attn_in['amp_q'], 'L0_attn_basis_k': _L0_attn_in['basis_k'], 'L0_attn_phase_k': _L0_attn_in['phase_k'], 'L0_attn_amp_k': _L0_attn_in['amp_k'], 'L0_attn_basis_v': _L0_attn_in['basis_v'], 'L0_attn_phase_v': _L0_attn_in['phase_v'], 'L0_attn_amp_v': _L0_attn_in['amp_v'], 'L0_attn_basis_o': _L0_attn_in['basis_o'], 'L0_attn_phase_o': _L0_attn_in['phase_o'], 'L0_attn_amp_o': _L0_attn_in['amp_o'], 'L0_ffn_w_norm': _L0_ffn_in['w_norm'], 'L0_ffn_w_router': _L0_ffn_in['w_router'], 'L0_ffn_w_gate': _L0_ffn_in['w_gate'], 'L0_ffn_w_up': _L0_ffn_in['w_up'], 'L0_ffn_w_down': _L0_ffn_in['w_down'], 'L0_ffn_sw_gate': _L0_ffn_in['sw_gate'], 'L0_ffn_sw_up': _L0_ffn_in['sw_up'], 'L0_ffn_sw_down': _L0_ffn_in['sw_down'], 'L0_ffn_w_shared_gate': _L0_ffn_in['w_shared_gate']}
    _x0 = _d['L0_attn_hidden_states']
    _d['L0_attn_hidden_states'] = jax.random.normal(jax.random.fold_in(jax.random.key(seed), 1), (2, 1024, 256), dtype=_x0.dtype)
    del _x0
    return _d

def reference(L0_attn_hidden_states, L0_attn_basis_q, L0_attn_phase_q, L0_attn_amp_q, L0_attn_basis_k, L0_attn_phase_k, L0_attn_amp_k, L0_attn_basis_v, L0_attn_phase_v, L0_attn_amp_v, L0_attn_basis_o, L0_attn_phase_o, L0_attn_amp_o, L0_ffn_w_norm, L0_ffn_w_router, L0_ffn_w_gate, L0_ffn_w_up, L0_ffn_w_down, L0_ffn_sw_gate, L0_ffn_sw_up, L0_ffn_sw_down, L0_ffn_w_shared_gate):

    def _L0_attn_ref(hidden_states, basis_q, phase_q, amp_q, basis_k, phase_k, amp_k, basis_v, phase_v, amp_v, basis_o, phase_o, amp_o):
        import jax, jax.numpy as jnp
        import numpy as np
        HIDDEN = 256
        NUM_HEADS = 16
        HEAD_DIM = HIDDEN // NUM_HEADS
        HARMONICS = 64

        def _holo_params(key, in_features, out_features, harmonics):
            kb, kp = jax.random.split(key)
            basis = jax.random.normal(kb, (harmonics, in_features), dtype=jnp.float32)
            basis = basis / jnp.linalg.norm(basis, axis=1, keepdims=True)
            phase = jax.random.normal(kp, (out_features, harmonics), dtype=jnp.float32) * 0.1
            amp = jnp.ones((out_features, harmonics), dtype=jnp.float32) / np.sqrt(harmonics).astype(np.float32)
            return (basis, phase, amp)

        def _holo_linear(x, basis, phase, amp):
            resonance = jnp.einsum('bsd,hd->bsh', x, basis)
            w = amp * jnp.cos(phase)
            return jnp.einsum('bsh,oh->bso', resonance, w)
        bsz, seq_len, _ = hidden_states.shape
        q = _holo_linear(hidden_states, basis_q, phase_q, amp_q)
        k = _holo_linear(hidden_states, basis_k, phase_k, amp_k)
        v = _holo_linear(hidden_states, basis_v, phase_v, amp_v)
        q = q.reshape(bsz, seq_len, NUM_HEADS, HEAD_DIM).transpose(0, 2, 1, 3)
        k = k.reshape(bsz, seq_len, NUM_HEADS, HEAD_DIM).transpose(0, 2, 1, 3)
        v = v.reshape(bsz, seq_len, NUM_HEADS, HEAD_DIM).transpose(0, 2, 1, 3)
        scale = 1.0 / np.sqrt(HEAD_DIM).astype(np.float32)
        scores = jnp.einsum('bhqd,bhkd->bhqk', q, k) * scale
        attn = jax.nn.softmax(scores, axis=-1)
        out = jnp.einsum('bhqk,bhkd->bhqd', attn, v)
        out = out.transpose(0, 2, 1, 3).reshape(bsz, seq_len, HIDDEN)
        return _holo_linear(out, basis_o, phase_o, amp_o)

    def _L0_ffn_ref(hidden_states, w_norm, w_router, w_gate, w_up, w_down, sw_gate, sw_up, sw_down, w_shared_gate):
        import jax, jax.numpy as jnp
        import numpy as np
        B, S, H = (2, 256, 256)
        E, K, F = (32, 4, 176)
        FS = 704
        EPS = 1e-06
        CAP = 128
        inp = hidden_states
        xf = inp.astype(jnp.float32)
        var = jnp.mean(xf * xf, axis=-1, keepdims=True)
        x = (w_norm * (xf * jax.lax.rsqrt(var + EPS))).astype(inp.dtype)
        Bq, Sq, Hq = x.shape
        x = x.reshape(-1, Hq)
        T = Bq * Sq
        logits = x @ w_router
        probs = jax.nn.softmax(logits.astype(jnp.float32), axis=-1)
        w_topk, sel = jax.lax.top_k(probs, K)
        w_topk = w_topk.astype(x.dtype)
        flat_e = sel.reshape(-1)
        order = jnp.argsort(flat_e)
        sorted_e = flat_e[order]
        counts = jnp.zeros((E,), jnp.int32).at[flat_e].add(1)
        starts = jnp.cumsum(counts) - counts
        pos = jnp.arange(T * K) - starts[sorted_e]
        tok = order // K
        valid = pos < CAP
        dest = jnp.where(valid, pos, CAP)
        buf = jnp.zeros((E, CAP + 1, Hq), x.dtype).at[sorted_e, dest].set(x[tok])
        buf = buf[:, :CAP]
        g = jnp.einsum('ech,ehf->ecf', buf, w_gate)
        u = jnp.einsum('ech,ehf->ecf', buf, w_up)
        y = jnp.einsum('ecf,efh->ech', jax.nn.silu(g) * u, w_down)
        wv = w_topk.reshape(-1)[order] * valid.astype(x.dtype)
        gath = y[sorted_e, jnp.minimum(pos, CAP - 1)]
        out = jnp.zeros((T, Hq), x.dtype).at[tok].add(gath * wv[:, None])
        sh = jax.nn.silu(x @ sw_gate) * (x @ sw_up) @ sw_down
        sh = jax.nn.sigmoid(x @ w_shared_gate) * sh
        out = out + sh
        return inp + out.reshape(Bq, Sq, Hq)
    x = L0_attn_hidden_states
    xn = _layernorm(x, axis=-1)
    x = x + _L0_attn_ref(xn, L0_attn_basis_q, L0_attn_phase_q, L0_attn_amp_q, L0_attn_basis_k, L0_attn_phase_k, L0_attn_amp_k, L0_attn_basis_v, L0_attn_phase_v, L0_attn_amp_v, L0_attn_basis_o, L0_attn_phase_o, L0_attn_amp_o) + _L0_ffn_ref(xn, L0_ffn_w_norm, L0_ffn_w_router, L0_ffn_w_gate, L0_ffn_w_up, L0_ffn_w_down, L0_ffn_sw_gate, L0_ffn_sw_up, L0_ffn_sw_down, L0_ffn_w_shared_gate)
    return x

_drawn_inputs = setup_inputs


def setup_inputs(seed=0):
    import zlib

    import numpy as np

    out = dict(_drawn_inputs(seed))
    spreads = {'L0_attn_amp_q': (0.125, 0.6),
     'L0_attn_amp_k': (0.125, 0.6),
     'L0_attn_amp_v': (0.125, 0.6),
     'L0_attn_amp_o': (0.125, 0.6)}
    factors = {'L0_attn_phase_q': 64.0,
     'L0_attn_phase_k': 64.0,
     'L0_attn_phase_v': 64.0,
     'L0_attn_phase_o': 64.0,
     'L0_ffn_w_norm': 8.0,
     'L0_ffn_w_router': 8.0,
     'L0_ffn_w_gate': 8.0,
     'L0_ffn_w_up': 8.0,
     'L0_ffn_w_down': 8.0,
     'L0_ffn_sw_gate': 8.0,
     'L0_ffn_sw_up': 8.0,
     'L0_ffn_sw_down': 8.0,
     'L0_ffn_w_shared_gate': 8.0,
     'L0_attn_basis_q': 8.0,
     'L0_attn_basis_k': 8.0,
     'L0_attn_basis_v': 8.0,
     'L0_attn_basis_o': 8.0}
    for name, (base, spread) in spreads.items():
        noise = np.random.default_rng([zlib.crc32(name.encode()), seed]).standard_normal(out[name].shape)
        drawn = base * np.exp(spread * noise) if base else spread * noise
        out[name] = jnp.asarray(drawn.astype(out[name].dtype))
    for name, factor in factors.items():
        out[name] = (out[name] * factor).astype(out[name].dtype)
    return out
```

```python
from contextlib import ExitStack

import concourse.bass as bass
from concourse import mybir

FP32 = mybir.dt.float32
BF16 = mybir.dt.bfloat16
U32 = mybir.dt.uint32
ALU = mybir.AluOpType
ACT = mybir.ActivationFunctionType
AX = mybir.AxisListType

P = 128
BATCH, SEQ, HID = 2, 1024, 256
TOK = BATCH * SEQ
TILES = TOK // P
HC = HID // P
HEADS, HD, HARM = 16, 16, 64
GH = 4
HG = HEADS // GH
GROUPS = BATCH * HG
KT = SEQ // P
N = 512
QH = SEQ // N
STEPS = QH * KT
EXPERTS, TOPK, FF, CAP = 32, 4, 176, 128
SLOTS = EXPERTS * CAP
FS = 704
FCH = [118] * 5 + [114]
FOFF = [118 * i for i in range(6)]
FHALF = FF // 2
BLK = TOK // N
TPB = N // P
LN_EPS, RMS_EPS = 1e-5, 1e-6
SCALE = HD ** -0.5
TWO_PI_HI, TWO_PI_LO = 6.28125, 0.0019353071795864769
INV_TWO_PI = 0.15915494309189535
ROUND = 1.5 * 2.0 ** 23
PI = 3.1415925
PAIRS = [(0, 0), (0, 1), (0, 2), (1, 0), (1, 1), (2, 0)]
SROWS = HD * len(PAIRS)
KROWS = SROWS + 2
STACK_DMAS = 2 * len(PAIRS) + 1
BIAS_DMAS = 4
UNITS = GH * KT
MBANK = UNITS + 2


def build(nc, x, bq, pq, aq, bk, pk, ak, bv, pv, av, bo, po, ao, w_norm, w_router, w_gate, w_up,
          w_down, sw_gate, sw_up, sw_down, w_sg, out):
    ctx = ExitStack()
    with ctx:
        def sb(name, shape, dt=FP32):
            return ctx.enter_context(nc.sbuf_tensor(name, shape, dt))

        def sem(name):
            return ctx.enter_context(nc.semaphore(name))

        q_parts = nc.dram_tensor("q_parts", (GROUPS, 3, HD * GH, SEQ), BF16).ap()
        k_parts = nc.dram_tensor("k_parts", (GROUPS, 3, HD * GH, SEQ), BF16).ap()
        v_wide = nc.dram_tensor("v_wide", (GROUPS, SEQ, GH * 32), FP32).ap()
        slot_x = nc.dram_tensor("slot_x", (SLOTS, HID), FP32).ap()
        slot_y = nc.dram_tensor("slot_y", (SLOTS + 1, HID), FP32).ap()

        res = sb("res", [P, TILES, HID])
        wide = sb("wide", [P, GROUPS * SEQ])
        xn = wide[:, 0:TILES * HID].rearrange("p (t h) -> p t h", t=TILES)
        xnT = wide[:, TILES * HID:2 * TILES * HID].rearrange("p (c t) -> p c t", c=HC)
        attT = wide[:, :].rearrange("p (g t) -> p g t", g=GROUPS)
        xf = sb("xf", [P, TILES, HID])
        xfT = sb("xfT", [P, HC, TOK])
        q_mem = sb("q_mem", [P, 3 * GH * SEQ // 2])
        k_mem = sb("k_mem", [P, 3 * GH * SEQ // 2])
        q_stack = q_mem[:, :].bitcast(BF16).rearrange("p (b j t) -> p b j t", b=3, j=GH)
        k_stack = k_mem[:, :].bitcast(BF16).rearrange("p (b j t) -> p b j t", b=3, j=GH)
        v_stack = sb("v_stack", [P, 3, KT, GH, 32])
        prob = sb("prob", [P, 3, GH, N])
        sw_gu = sb("sw_gu", [P, HC, 2, FS])
        sw_dn = sb("sw_dn", [FCH[0], len(FCH), HID])
        ident = sb("ident", [P, P])
        ident_b = sb("ident_b", [P, P], BF16)
        before = sb("before", [P, P], BF16)
        ones_b = sb("ones_b", [P, P], BF16)
        bT = sb("bT", [P, 2, HC, P])
        wq = sb("wq", [P, HID])
        wk = sb("wk", [P, HID])
        wv = sb("wv", [P, HID])
        wo = sb("wo", [P, HID])
        boT = sb("boT", [P, HG, P])
        wr = sb("wr", [P, HC, EXPERTS + 1])
        rt = sb("rt", [P, 2, N])
        rvo = sb("rvo", [P, N])
        mx = sb("mx", [P, UNITS])
        nm = sb("nm", [P, 2, 2, 2, KT], BF16)
        nmT = sb("nmT", [32, 2, P], BF16)
        slot = sb("slot", [P, TOPK, TILES], U32)
        wsel = sb("wsel", [P, TOPK, TILES])
        sgate = sb("sgate", [P, TILES])
        small = sb("small", [P, 16, TILES])
        bn = sb("bn", [P, TILES, 6])
        mv = sb("mv", [P, TILES, 2])
        top8 = sb("top8", [P, TILES, 8])
        idx8 = sb("idx8", [P, TILES, 8], U32)
        idxf = sb("idxf", [P, TILES, 8])
        wn = sb("wn", [P, HID])
        iota_e = sb("iota_e", [P, EXPERTS])
        mask_b = sb("mask_b", [P, TILES, EXPERTS], BF16)
        eps = sb("eps", [P, 2])

        psum = ctx.enter_context(nc.psum_tensor("psum", [P, 8, N], FP32))

        probf = prob[:, :, :, :].rearrange("p a b c -> p (a b c)")
        zeros = probf[:, 0:2048]
        phase = probf[:, 2048:2560].rearrange("p (c m h) -> p c m h", c=2, m=4)
        amp = probf[:, 2560:3072].rearrange("p (c m h) -> p c m h", c=2, m=4)
        turn = probf[:, 3072:3584].rearrange("p (c m h) -> p c m h", c=2, m=4)
        ang = probf[:, 3584:4096].rearrange("p (c m h) -> p c m h", c=2, m=4)
        wmat = probf[:, 4096:4608].rearrange("p (c m h) -> p c m h", c=2, m=4)
        rem = probf[:, 4608:5632].rearrange("p (b n) -> p b n", b=2)
        bo_pad = probf[:, 5632:6144].rearrange("p (g j d) -> p g j d", g=HG, j=GH)
        basis = k_mem[:, 5120:5632].rearrange("p (s h) -> p s h", s=2)
        parts = q_mem[:, :].bitcast(BF16).rearrange("p (u s t) -> p u s t", u=4, s=3)
        v_stage = k_mem[:, 0:4096].rearrange("p (b t h d) -> p b t h d", b=4, t=2, h=HEADS)
        vsf = v_stack[:, :, :, :, :].rearrange("p a b c d -> p (a b c d)")
        probs = vsf[:, 0:512].rearrange("p (t e) -> p t e", t=TILES)
        onehot = vsf[:, 512:2560].rearrange("p (k t e) -> p k t e", k=TOPK, t=TILES)
        rtmp = vsf[:, 2560:3072].rearrange("p (t e) -> p t e", t=TILES)
        cum = k_mem[:, 4096:5120].rearrange("p (b t e) -> p b t e", b=2, t=TILES)
        pos = k_mem[:, 5632:6144].rearrange("p (t e) -> p t e", t=TILES)

        prologue(nc, sem, locals())
        attention(nc, sem, locals())
        experts(nc, sem, locals())
        shared(nc, sem, locals())


def prologue(nc, sem, v):
    (x, res, xn, xnT, xf, xfT, psum, ident, ident_b, before, ones_b, bT, wq, wk, wv, wo, boT, wr, rt, rvo) = (
        v["x"], v["res"], v["xn"], v["xnT"], v["xf"], v["xfT"], v["psum"], v["ident"], v["ident_b"], v["before"],
        v["ones_b"], v["bT"], v["wq"], v["wk"], v["wv"], v["wo"], v["boT"], v["wr"], v["rt"], v["rvo"])
    (zeros, phase, amp, turn, ang, wmat, rem, bo_pad, basis, parts, v_stage, probs, onehot, rtmp, cum, pos) = (
        v["zeros"], v["phase"], v["amp"], v["turn"], v["ang"], v["wmat"], v["rem"], v["bo_pad"], v["basis"],
        v["parts"], v["v_stage"], v["probs"], v["onehot"], v["rtmp"], v["cum"], v["pos"])
    (bn, mv, small, eps, wn, top8, idx8, idxf, iota_e, mask_b, slot, wsel, sgate, k_stack) = (
        v["bn"], v["mv"], v["small"], v["eps"], v["wn"], v["top8"], v["idx8"], v["idxf"], v["iota_e"],
        v["mask_b"], v["slot"], v["wsel"], v["sgate"], v["k_stack"])
    slot_x, slot_y, v_wide = v["slot_x"], v["slot_y"], v["v_wide"]

    x_in = [sem(f"x_in{i}") for i in range(BLK)]
    holo_in = sem("holo_in")
    vec_in = sem("vec_in")
    late_in = sem("late_in")
    zero_out = sem("zero_out")
    const_ok = sem("const_ok")
    pool_step = sem("pool_step")
    dve_step = sem("dve_step")
    var_ok = sem("var_ok")
    sqrt_ok = sem("sqrt_ok")
    xn_ok = sem("xn_ok")
    ms_ok = sem("ms_ok")
    xf_ok = sem("xf_ok")
    ang_ok = sem("ang_ok")
    sin_ok = sem("sin_ok")
    wmat_ok = sem("wmat_ok")
    wtr_ok = sem("wtr_ok")
    wT_ok = sem("wT_ok")
    tr_ok = sem("tr_ok")
    xnT_ok = sem("xnT_ok")
    xfT_ok = sem("xfT_ok")
    r_ok = sem("r_ok")
    rs_ok = sem("rs_ok")
    qk_ok = sem("qk_ok")
    hi_ok = sem("hi_ok")
    rem_ok = sem("rem_ok")
    mid_ok = sem("mid_ok")
    low_ok = sem("low_ok")
    part_out = [sem(f"part_out{u}") for u in range(4)]
    v_ok = sem("v_ok")
    vs_ok = sem("vs_ok")
    v_out = [sem(f"v_out{i}") for i in range(4)]
    logit_ok = sem("logit_ok")
    exp_in = sem("exp_in")
    exp_ok = sem("exp_ok")
    mask_ok = sem("mask_ok")
    count_ok = sem("count_ok")

    mats = [(v["pq"], v["aq"]), (v["pk"], v["ak"]), (v["pv"], v["av"]), (v["po"], v["ao"])]
    HOLO = 2 * len(mats) + 4
    VDMAS = 2

    with nc.Block() as block:
        @block.sync
        def _(sp):
            xr = x.rearrange("b s h -> (b s) h").rearrange("(t p) h -> p t h", p=P)
            for i in range(BLK):
                sp.dma_start(res[:, TPB * i:TPB * (i + 1), :], xr[:, TPB * i:TPB * (i + 1), :]).then_inc(x_in[i], 16)
            sp.wait_ge(const_ok, 5)
            for i in range(4):
                sp.dma_start(slot_x[1024 * i:1024 * (i + 1), :].rearrange("(p r) h -> p (r h)", p=P),
                             zeros).then_inc(zero_out, 16)
            sp.dma_start(slot_y[SLOTS:SLOTS + 1, :], zeros[0:1, 0:HID]).then_inc(zero_out, 16)
            sgu = v["sw_gu"]
            sp.dma_start(sgu[:, :, 0, :], v["sw_gate"].rearrange("(c p) f -> p c f", p=P)).then_inc(late_in, 16)
            sp.dma_start(sgu[:, :, 1, :], v["sw_up"].rearrange("(c p) f -> p c f", p=P)).then_inc(late_in, 16)
            for i, (o, n) in enumerate(zip(FOFF, FCH)):
                sp.dma_start(v["sw_dn"][0:n, i, :], v["sw_down"][o:o + n, :]).then_inc(late_in, 16)
            for b in range(BATCH):
                for u in range(4):
                    dst = (v["q_parts"], v["k_parts"])[u // 2]
                    sp.wait_ge(low_ok, 8 * b + 4 + u + 1)
                    for i in range(2):
                        sp.dma_start(dst[HG * b + 2 * (u % 2) + i, :, :, :].rearrange("s p t -> p s t"),
                                     parts[64 * i:64 * (i + 1), u, :, :]).then_inc(part_out[u], 16)
            for u in range(4):
                sp.wait_ge(part_out[u], 16 * 2 * BATCH)
            sp.wait_ge(zero_out, 16 * 5)
            sp.wait_ge(late_in, 16 * 8)

        @block.gpsimd
        def _(pool):
            pool.memset(ident[:, :], 0.0).then_inc(pool_step, 1)
            pool.memset(ident_b[:, :], 0.0).then_inc(pool_step, 1)
            pool.memset(before[:, :], 1.0).then_inc(pool_step, 1)
            pool.wait_ge(pool_step, 3)
            for m in (ident, ident_b):
                pool.affine_select(out=m[:, :], in_=m[:, :], compare_op=ALU.not_equal, fill=1.0, base=0,
                                   pattern=[[-1, P]], channel_multiplier=1).then_inc(const_ok, 1)
            pool.affine_select(out=before[:, :], in_=before[:, :], compare_op=ALU.is_gt, fill=0.0, base=0,
                               pattern=[[1, P]], channel_multiplier=-1).then_inc(const_ok, 1)
            pool.memset(ones_b[:, :], 1.0).then_inc(const_ok, 1)
            pool.memset(zeros, 0.0).then_inc(const_ok, 1)
            pool.iota(iota_e[:, :], pattern=[[1, EXPERTS]], base=0, channel_multiplier=0,
                      allow_small_or_imprecise_dtypes=True).then_inc(const_ok, 1)
            for b in range(BLK):
                pool.wait_ge(xn_ok, TPB * (b + 1))
                sl = slice(TPB * b, TPB * (b + 1))
                pool.tensor_tensor(res[:, sl, :], res[:, sl, :], xn[:, sl, :], ALU.add).then_inc(pool_step, 1)

        @block.scalar
        def _(act):
            act.dma_start(basis[0:64, 0, :], v["bq"]).then_inc(holo_in, 16)
            act.dma_start(basis[64:128, 0, :], v["bk"]).then_inc(holo_in, 16)
            act.dma_start(basis[0:64, 1, :], v["bv"]).then_inc(holo_in, 16)
            act.dma_start(basis[64:128, 1, :], v["bo"]).then_inc(holo_in, 16)
            for m, (ph, am) in enumerate(mats):
                act.dma_start(phase[:, :, m, :], ph.rearrange("(c p) h -> p c h", p=P)).then_inc(holo_in, 16)
                act.dma_start(amp[:, :, m, :], am.rearrange("(c p) h -> p c h", p=P)).then_inc(holo_in, 16)
            wn_src = v["w_norm"].rearrange("(a h) -> a h", a=1)
            act.dma_start(wn[:, :], wn_src.broadcast_to([P, HID])).then_inc(vec_in, 16)
            act.dma_start(wr[:, :, 0:EXPERTS], v["w_router"].rearrange("(c p) e -> p c e", p=P)).then_inc(vec_in, 16)
            with nc.allow_non_contiguous_dma(reason="one column of 256 weights"):
                act.dma_start(wr[:, :, EXPERTS:EXPERTS + 1],
                              v["w_sg"].rearrange("(c p) e -> p c e", p=P)).then_inc(vec_in, 16)
            act.wait_ge(ang_ok, 1)
            act.activation(wmat, ang, ACT.Sin).then_inc(sin_ok, 1)
            act.wait_ge(var_ok, 1)
            act.activation(small[:, 0, :], mv[:, :, 1], ACT.Sqrt, bias=eps[:, 0:1]).then_inc(sqrt_ok, 1)
            for t in range(TILES):
                act.wait_ge(xn_ok, t + 1)
                act.activation(xf[:, t, :], xn[:, t, :], ACT.Square, scale=1.0 / 16.0,
                               accum_out=small[:, 4, t:t + 1]).then_inc(ms_ok, 1)
            act.wait_ge(ms_ok, TILES)
            act.activation(small[:, 5, :], small[:, 4, :], ACT.Sqrt, bias=eps[:, 1:2]).then_inc(sqrt_ok, 1)
            for b in range(BLK):
                blk = slice(N * b, N * (b + 1))
                for c in range(HC):
                    act.wait_ge(tr_ok, 4 * b + c + 1)
                    act.copy(xnT[:, c, blk], psum[:, c, :]).then_inc(xnT_ok, 1)
                for i, dst in enumerate((rt[:, b % 2, :], rvo[:, :])):
                    act.wait_ge(r_ok, 2 * b + i + 1)
                    if i == 0 and b >= 2:
                        act.wait_ge(qk_ok, 4 * (b - 1))
                    if i == 1 and b >= 1:
                        act.wait_ge(v_ok, 2 * b)
                    act.copy(dst, psum[:, 4, :] if i == 0 else psum[:, 5, :]).then_inc(rs_ok, 1)
                for u in range(4):
                    n = 4 * b + u
                    half = slice(N * (b % 2), N * (b % 2 + 1))
                    act.wait_ge(qk_ok, n + 1)
                    if b >= 2:
                        act.wait_ge(part_out[u], 32)
                    act.copy(parts[:, u, 0, half], psum[:, 6 + u % 2, :]).then_inc(hi_ok, 1)
                    act.wait_ge(rem_ok, n + 1)
                    act.copy(parts[:, u, 1, half], rem[:, n % 2, :]).then_inc(mid_ok, 1)
                for i in range(2):
                    n = 2 * b + i
                    act.wait_ge(v_ok, n + 1)
                    act.wait_ge(dve_step, 1)
                    if n >= 4:
                        act.wait_ge(v_out[n % 4], VDMAS * 16 * (n // 4))
                    act.copy(v_stage[:, n % 4, :, :, 0:HD],
                             psum[:, 4 + i, :].rearrange("p (t h d) -> p t h d", t=2, h=HEADS)).then_inc(vs_ok, 1)
                    act.wait_ge(vs_ok, n + 1)
                    for t in range(2):
                        tile = 2 * n + t
                        row = P * (tile % KT)
                        act.dma_start(v_wide[HG * (tile // KT):HG * (tile // KT + 1), row:row + P, :].rearrange("g p n -> p g n"),
                                      v_stage[:, n % 4, t, :, :].rearrange("p (g j) d -> p g (j d)", g=HG)).then_inc(v_out[n % 4], 16)
            act.wait_ge(exp_in, 1)
            act.activation(probs, probs, ACT.Exp).then_inc(exp_ok, 1)
            act.activation(small[:, 10, :], small[:, 9, :], ACT.Tanh, scale=0.5).then_inc(exp_ok, 1)
            for i in range(4):
                act.wait_ge(v_out[i], VDMAS * 16 * 2)

        @block.tensor
        def _(pe):
            pe.wait_ge(const_ok, 2)
            pe.wait_ge(holo_in, 16 * HOLO - 16 * 0)
            for s in range(2):
                for c in range(HC):
                    last = pe.transpose(psum[:, 0, P * (2 * s + c):P * (2 * s + c + 1)],
                                        basis[:, s, P * c:P * (c + 1)], ident[:, :])
            last.then_inc(wtr_ok, 1)
            pe.wait_ge(wmat_ok, 2)
            for s in range(2):
                for c in range(HC):
                    last = pe.transpose(psum[:, 1, P * (2 * s + c):P * (2 * s + c + 1)],
                                        wmat[:, c, 2 * s:2 * s + 2, :], ident[:, :])
            last.then_inc(wtr_ok, 1)
            for g in range(HG):
                last = pe.transpose(psum[:, 2, P * g:P * (g + 1)], bo_pad[:, g, :, :], ident[:, :])
            last.then_inc(wtr_ok, 1)
            pe.wait_ge(wT_ok, 6)
            for b in range(BLK):
                blk = slice(N * b, N * (b + 1))
                for src, ok, free, bank in ((xn, xn_ok, xnT_ok, 0), (xf, xf_ok, xfT_ok, 2)):
                    pe.wait_ge(ok, TPB * (b + 1))
                    for c in range(HC):
                        if b:
                            pe.wait_ge(free, 2 * (b - 1) + c + 1)
                        for t in range(TPB):
                            last = pe.transpose(psum[:, bank + c, P * t:P * (t + 1)],
                                                src[:, TPB * b + t, P * c:P * (c + 1)], ident[:, :])
                        last.then_inc(tr_ok, 1)
                pe.wait_ge(xnT_ok, 2 * (b + 1))
                for s in range(2):
                    if b:
                        pe.wait_ge(vs_ok, 2 * (b - 1) + s + 1)
                    for c in range(HC):
                        last = pe.matmul(psum[:, 4 + s, :], bT[:, s, c, :], xnT[:, c, blk],
                                         start=(c == 0), stop=(c == HC - 1))
                    last.then_inc(r_ok, 1)
                pe.wait_ge(rs_ok, 2 * b + 1)
                for u in range(4):
                    n = 4 * b + u
                    if n >= 2:
                        pe.wait_ge(hi_ok, n - 1)
                        pe.wait_ge(rem_ok, n - 1)
                    w = (wq, wk)[u // 2]
                    pe.matmul(psum[:, 6 + u % 2, :], w[:, P * (u % 2):P * (u % 2 + 1)], rt[:, b % 2, :],
                              start=True, stop=True).then_inc(qk_ok, 1)
                pe.wait_ge(rs_ok, 2 * b + 2)
                for i in range(2):
                    for t in range(2):
                        tt = 2 * i + t
                        last = pe.matmul(psum[:, 4 + i, HID * t:HID * (t + 1)], rvo[:, P * tt:P * (tt + 1)],
                                         wv[:, :], start=True, stop=True)
                    last.then_inc(v_ok, 1)
            pe.wait_ge(vec_in, 48)
            pe.wait_ge(xnT_ok, 2 * BLK)
            pe.wait_ge(xfT_ok, 2 * BLK)
            for t in range(TILES):
                for c in range(HC):
                    last = pe.matmul(psum[:, t // 8, 64 * (t % 8):64 * (t % 8) + EXPERTS + 1],
                                     xfT[:, c, P * t:P * (t + 1)], wr[:, c, :], start=(c == 0), stop=(c == HC - 1))
            last.then_inc(logit_ok, 1)
            pe.wait_ge(mask_ok, 1)
            mb = mask_b[:, :, :].rearrange("p t e -> p (t e)")
            pe.matmul(psum[:, 2, :], before[:, :], mb, start=True, stop=True).then_inc(count_ok, 1)
            pe.matmul(psum[:, 3, :], ones_b[:, :], mb, start=True, stop=True).then_inc(count_ok, 1)

        @block.vector
        def _(dve):
            steps = [0]

            def link(ins):
                steps[0] += 1
                ins.then_inc(dve_step, 1)
                dve.wait_ge(dve_step, steps[0])

            link(dve.memset(v_stage[:, :, :, :, HD:32], 1.0))
            dve.memset(bo_pad, 0.0)
            dve.memset(wq[64:128, :], 0.0)
            dve.memset(wk[0:64, :], 0.0)
            dve.memset(wv[64:128, :], 0.0)
            dve.memset(wo[0:64, :], 0.0)
            dve.memset(eps[:, 0:1], LN_EPS)
            link(dve.memset(eps[:, 1:2], RMS_EPS))
            dve.wait_ge(holo_in, 16 * HOLO)
            link(dve.tensor_scalar(turn, phase, INV_TWO_PI, 0.25, ALU.mult, ALU.add))
            link(dve.tensor_scalar(turn, turn, ROUND, ROUND, ALU.add, ALU.subtract))
            link(dve.scalar_tensor_tensor(ang, turn, -TWO_PI_HI, phase, ALU.mult, ALU.add))
            link(dve.scalar_tensor_tensor(ang, turn, -TWO_PI_LO, ang, ALU.mult, ALU.add))
            link(dve.tensor_scalar(ang, ang, PI / 2, PI, ALU.add, ALU.min))
            dve.tensor_scalar(ang, ang, -PI, None, ALU.max).then_inc(ang_ok, 1)
            for b in range(BLK):
                dve.wait_ge(x_in[b], 16)
                for t in range(TPB * b, TPB * (b + 1)):
                    last = dve.bn_stats(bn[:, t, :], res[:, t, :])
            link(last)
            for t in range(TILES):
                last = dve.bn_aggr(mv[:, t, :], bn[:, t, :])
            last.then_inc(var_ok, 1)
            dve.wait_ge(sin_ok, 1)
            dve.tensor_tensor(wmat, wmat, amp, ALU.mult).then_inc(wmat_ok, 1)
            dve.tensor_copy(bo_pad[64:128, :, :, 0:HD],
                            basis[64:128, 1, :].rearrange("p (g j d) -> p g j d", g=HG, j=GH)).then_inc(wmat_ok, 1)

            def inverse_root(var, root, e, tmp, y):
                link(dve.reciprocal(y, root))
                link(dve.tensor_tensor(tmp, y, y, ALU.mult))
                link(dve.scalar_tensor_tensor(tmp, var, e, tmp, ALU.add, ALU.mult))
                link(dve.tensor_scalar(tmp, tmp, -0.5, 1.5, ALU.mult, ALU.add))
                link(dve.tensor_tensor(y, y, tmp, ALU.mult))

            dve.wait_ge(sqrt_ok, 1)
            inverse_root(mv[:, :, 1], small[:, 0, :], LN_EPS, small[:, 1, :], small[:, 2, :])
            for t in range(TILES):
                dve.tensor_scalar(xn[:, t, :], res[:, t, :], mv[:, t, 0:1], small[:, 2, t:t + 1],
                                  ALU.subtract, ALU.mult).then_inc(xn_ok, 1)
            dve.wait_ge(wtr_ok, 3)
            dve.tensor_copy(bT[:, :, :, :].rearrange("p s c h -> p (s c h)"), psum[:, 0, :]).then_inc(wT_ok, 1)
            for w, lo, col in ((wq, 0, 0), (wk, 64, 0)):
                dve.tensor_copy(w[lo:lo + 64, :].rearrange("p (g d j) -> p g d j", g=HG, d=HD),
                                psum[lo:lo + 64, 1, 0:HID].rearrange("p (g j d) -> p g d j", g=HG, j=GH)).then_inc(wT_ok, 1)
            dve.tensor_copy(wv[0:64, :], psum[0:64, 1, HID:2 * HID]).then_inc(wT_ok, 1)
            dve.tensor_copy(wo[64:128, :], psum[64:128, 1, HID:2 * HID]).then_inc(wT_ok, 1)
            dve.tensor_copy(boT[:, :, :].rearrange("p g h -> p (g h)"), psum[:, 2, :]).then_inc(wT_ok, 1)
            dve.wait_ge(sqrt_ok, 2)
            dve.wait_ge(vec_in, 48)
            inverse_root(small[:, 4, :], small[:, 5, :], RMS_EPS, small[:, 6, :], small[:, 7, :])
            for t in range(TILES):
                dve.scalar_tensor_tensor(xf[:, t, :], xn[:, t, :], small[:, 7, t:t + 1], wn[:, :],
                                         ALU.mult, ALU.mult).then_inc(xf_ok, 1)
            for b in range(BLK):
                blk = slice(N * b, N * (b + 1))
                for c in range(HC):
                    dve.wait_ge(tr_ok, 4 * b + 2 + c + 1)
                    dve.tensor_copy(xfT[:, c, blk], psum[:, 2 + c, :]).then_inc(xfT_ok, 1)
                for u in range(4):
                    n = 4 * b + u
                    half = slice(N * (b % 2), N * (b % 2 + 1))
                    dve.wait_ge(hi_ok, n + 1)
                    dve.tensor_tensor(rem[:, n % 2, :], psum[:, 6 + u % 2, :], parts[:, u, 0, half],
                                      ALU.subtract).then_inc(rem_ok, 1)
                    dve.wait_ge(mid_ok, n + 1)
                    dve.tensor_tensor(parts[:, u, 2, half], rem[:, n % 2, :], parts[:, u, 1, half],
                                      ALU.subtract).then_inc(low_ok, 1)
            dve.wait_ge(logit_ok, 1)
            dve.wait_ge(const_ok, 6)
            lg = psum[:, 0:2, :].rearrange("p b (t e) -> p (b t) e", e=64)
            link(dve.tensor_copy(probs, lg[:, :, 0:EXPERTS]))
            link(dve.tensor_copy(small[:, 9, :], lg[:, :, EXPERTS]))
            link(dve.tensor_reduce(small[:, 8, :], probs, AX.X, ALU.max))
            dve.tensor_tensor(probs, probs, small[:, 8, :].unsqueeze(2).broadcast_to([P, TILES, EXPERTS]),
                              ALU.subtract).then_inc(exp_in, 1)
            dve.wait_ge(exp_ok, 2)
            link(dve.tensor_reduce(small[:, 11, :], probs, AX.X, ALU.add))
            link(dve.reciprocal(small[:, 12, :], small[:, 11, :]))
            link(dve.tensor_tensor(probs, probs, small[:, 12, :].unsqueeze(2).broadcast_to([P, TILES, EXPERTS]), ALU.mult))
            dve.tensor_scalar(sgate[:, :], small[:, 10, :], 0.5, 0.5, ALU.mult, ALU.add)
            for t in range(TILES):
                last = dve.max(top8[:, t, :], probs[:, t, :])
            link(last)
            for t in range(TILES):
                last = dve.max_index(idx8[:, t, :], top8[:, t, :], probs[:, t, :])
            link(last)
            link(dve.tensor_copy(idxf[:, :, :], idx8[:, :, :]))
            ie = iota_e[:, :].unsqueeze(1).broadcast_to([P, TILES, EXPERTS])
            for k in range(TOPK):
                last = dve.tensor_tensor(onehot[:, k, :, :], ie,
                                         idxf[:, :, k:k + 1].broadcast_to([P, TILES, EXPERTS]), ALU.is_equal)
            link(last)
            link(dve.tensor_tensor(rtmp, onehot[:, 0, :, :], onehot[:, 1, :, :], ALU.add))
            link(dve.tensor_tensor(rtmp, rtmp, onehot[:, 2, :, :], ALU.add))
            dve.tensor_tensor(mask_b[:, :, :], rtmp, onehot[:, 3, :, :], ALU.add).then_inc(mask_ok, 1)
            dve.wait_ge(count_ok, 2)
            tot = psum[:, 3, :].rearrange("p (t e) -> p t e", t=TILES)
            link(dve.tensor_copy(cum[:, 0, :, :], tot))
            cur, sh = 0, 1
            while sh < TILES:
                dve.tensor_copy(cum[:, 1 - cur, 0:sh, :], cum[:, cur, 0:sh, :])
                link(dve.tensor_tensor(cum[:, 1 - cur, sh:, :], cum[:, cur, sh:, :], cum[:, cur, 0:TILES - sh, :], ALU.add))
                cur, sh = 1 - cur, 2 * sh
            link(dve.tensor_tensor(pos, cum[:, cur, :, :], tot, ALU.subtract))
            link(dve.tensor_tensor(pos, pos, psum[:, 2, :].rearrange("p (t e) -> p t e", t=TILES), ALU.add))
            for k in range(TOPK):
                link(dve.tensor_tensor(rtmp, onehot[:, k, :, :], pos, ALU.mult))
                link(dve.tensor_reduce(small[:, 13, :], rtmp, AX.X, ALU.add))
                link(dve.tensor_scalar(small[:, 14, :], small[:, 13, :], float(CAP), None, ALU.is_lt))
                link(dve.tensor_tensor(wsel[:, k, :], top8[:, :, k], small[:, 14, :], ALU.mult))
                link(dve.scalar_tensor_tensor(small[:, 13, :], idxf[:, :, k], float(CAP), small[:, 13, :], ALU.mult, ALU.add))
                link(dve.scalar_tensor_tensor(small[:, 15, :], small[:, 13, :], float(-SLOTS), small[:, 14, :], ALU.add, ALU.mult))
                link(dve.tensor_scalar(slot[:, k, :], small[:, 15, :], float(SLOTS), None, ALU.add))


def attention(nc, sem, v):
    psum, mx, nm, nmT, prob, attT = v["psum"], v["mx"], v["nm"], v["nmT"], v["prob"], v["attT"]
    q_stack, k_stack, v_stack = v["q_stack"], v["k_stack"], v["v_stack"]
    stack_in = [sem(f"stack_in{i}") for i in range(3)]
    ones_ok = sem("ones_ok")
    mbank_full = sem("mbank_full")
    mbank_free = sem("mbank_free")
    nm_step = sem("nm_step")
    bias_in = [sem(f"bias_in{h}") for h in range(2)]
    score_ok = sem("score_ok")
    exp_done = sem("exp_done")
    av_done = sem("av_done")
    evac_done = sem("evac_done")
    scattered = sem("scattered")

    LAST_M = 13
    order = [("unit", w) for w in range(UNITS // 2 + 3)] + [("turn", 0)]
    order += [("unit", w) for w in range(UNITS // 2 + 3, UNITS)] + [("turn", 1)]

    def unit_matmuls(pe, buf, w, use, kh):
        j, qt = w // KT, w % KT
        return pe.matmul(psum[:, 2 * (use % 2) + kh, :], q_stack[0:SROWS, buf, j, P * qt:P * (qt + 1)],
                         k_stack[0:SROWS, buf, j, N * kh:N * (kh + 1)], start=True, stop=True)

    def pe_use(pe, G, buf, use, first=False):
        kind, w = order[use]

        def begin():
            if not first or use >= 2:
                pe.wait_ge(mbank_free, MBANK * G + (use - 1))

        def piece(kh):
            def go():
                if kh == 0:
                    begin()
                ins = unit_matmuls(pe, buf, w, use, kh)
                if kh == QH - 1:
                    ins.then_inc(mbank_full, 1)
            return go

        def turn():
            begin()
            pe.wait_ge(nm_step, 4 * G + (2 * w + 2))
            src = nm[:, w, :, :, :].rearrange("p j s t -> p (j s t)")
            pe.matmul(psum[0:32, 2 * (use % 2), 0:P], src, v["ident_b"][:, :], start=True,
                      stop=True).then_inc(mbank_full, 1)

        return [turn] if kind == "turn" else [piece(kh) for kh in range(QH)]

    def dve_use(dve, G, use, first):
        kind, w = order[use]
        dve.wait_ge(mbank_full, MBANK * G + (use + 1))
        if kind == "turn":
            if not first:
                dve.wait_ge(bias_in[w], 16 * BIAS_DMAS * G)
            dve.tensor_copy(nmT[:, w, :], psum[0:32, 2 * (use % 2), 0:P]).then_inc(mbank_free, 1)
            return
        pair = psum[:, 2 * (use % 2):2 * (use % 2) + 2, :].rearrange("p b n -> p (b n)")
        dve.tensor_reduce(mx[:, w:w + 1], pair, AX.X, ALU.max).then_inc(mbank_free, 1)
        if w % (2 * KT) == 2 * KT - 1:
            h = w // (2 * KT)
            m2 = mx[:, 2 * KT * h:2 * KT * (h + 1)].rearrange("p (j t) -> p j t", j=2)
            dve.wait_ge(mbank_free, MBANK * G + (use + 1))
            dve.tensor_scalar(nm[:, h, :, 0, :], m2, -1.0, None, ALU.mult).then_inc(nm_step, 1)
            dve.wait_ge(nm_step, 4 * G + (2 * h + 1))
            dve.scalar_tensor_tensor(nm[:, h, :, 1, :], m2, -1.0, nm[:, h, :, 0, :],
                                     ALU.mult, ALU.subtract).then_inc(nm_step, 1)

    def load(sp, G, buf):
        for st, dram, side in ((q_stack, v["q_parts"], 1), (k_stack, v["k_parts"], 0)):
            flat = dram.rearrange("g s (d j) t -> g s d (j t)", j=GH)
            for i, pair in enumerate(PAIRS):
                sp.dma_start(st[HD * i:HD * (i + 1), buf, :, :].rearrange("p j t -> p (j t)"),
                             flat[bass.ds(G, 1), pair[side], :, :].rearrange("g d n -> (g d) n")).then_inc(stack_in[buf], 16)
        vw = v["v_wide"].rearrange("g (t p) n -> g p t n", p=P)
        sp.dma_start(v_stack[:, buf, :, :, :].rearrange("p t j d -> p t (j d)"),
                     vw[bass.ds(G, 1), :, :, :].rearrange("g p t n -> (g p) t n")).then_inc(stack_in[buf], 16)

    def bias(sp, G, buf):
        for h in range(2):
            sp.wait_ge(mbank_free, MBANK * G + (order.index(("turn", h)) + 1))
            for j in range(2):
                for s in range(2):
                    r = (2 * j + s) * KT
                    sp.dma_start(q_stack[SROWS + s:SROWS + s + 1, buf, 2 * h + j, :].rearrange("a (t c) -> a t c", t=KT),
                                 nmT[r:r + KT, h, :]).then_inc(bias_in[h], 16)

    def pe_group(pe, G, off, it, peel):
        buf, nxt = off % 3, (off + 1) % 3
        uses = []
        if peel != "last":
            for use in range(MBANK):
                uses += pe_use(pe, G + 1, nxt, use)
            pe.wait_ge(stack_in[nxt], 16 * STACK_DMAS * (it + ((off + 1) // 3 + 1)))
        for h in range(2):
            pe.wait_ge(bias_in[h], 16 * BIAS_DMAS * (G + 1))
        at = 0
        for s in range(STEPS):
            qh, kt = s // KT, s % KT
            for j in range(GH):
                u = GH * s + j
                if not (peel == "first" and u < 2):
                    pe.wait_ge(exp_done, GH * STEPS * G + (u - 1))
                pe.matmul(psum[:, 4 + u % 2, :], k_stack[0:KROWS, buf, j, P * kt:P * (kt + 1)],
                          q_stack[0:KROWS, buf, j, N * qh:N * (qh + 1)], start=True, stop=True).then_inc(score_ok, 1)
                want = -(-len(uses) * (u + 1) // (LAST_M * GH))
                want = len(uses) if u >= GH * (LAST_M + 1) else min(want, len(uses) - 1)
                while at < want:
                    uses[at]()
                    at += 1
            if not (peel == "first" and s == 0):
                av_step(pe, G, off, s - 1, peel)

    def av_step(pe, G, off, s, peel):
        buf = (off + s // STEPS) % 3
        qh, kt = s % STEPS // KT, s % KT
        pe.wait_ge(exp_done, GH * STEPS * G + GH * (s + 1))
        if kt == 0 and peel != "first":
            pe.wait_ge(evac_done, QH * G + (qh - 1))
        for j in range(GH):
            last = pe.matmul(psum[32 * j:32 * (j + 1), 6 + qh, :], v_stack[:, buf, kt, j, :],
                             prob[:, (off * STEPS + s) % 3, j, :], start=(kt == 0), stop=(kt == KT - 1))
        last.then_inc(av_done, 1)

    def act_group(act, G, off, it, peel):
        for s in range(STEPS):
            for j in range(GH):
                u = GH * s + j
                act.wait_ge(score_ok, GH * STEPS * G + (u + 1))
                if j == 0 and not (peel == "first" and s < 3):
                    act.wait_ge(av_done, STEPS * G + (s - 2))
                act.activation(prob[:, (off * STEPS + s) % 3, j, :], psum[:, 4 + u % 2, :], ACT.Exp,
                               scale=SCALE).then_inc(exp_done, 1)
            if s == 1 and peel != "first":
                evac(act, G - 1, 1)
            if s == KT + 1:
                evac(act, G, 0)

    def evac(act, G, qh):
        act.wait_ge(av_done, STEPS * G + KT * (qh + 1))
        act.copy(attT[:, bass.ds(G, 1), N * qh:N * (qh + 1)], psum[:, 6 + qh:7 + qh, :]).then_inc(evac_done, 1)

    def groups(eng, run):
        run(0, 0, 0, "first")
        with eng.Fori(0, (GROUPS - 2) // 3) as it:
            for off in range(1, 4):
                run(it * 3 + off, off, it, None)
        run(GROUPS - 1, (GROUPS - 1) % 3, (GROUPS - 1) // 3, "last")

    with nc.Block() as block:
        @block.sync
        def _(sp):
            load(sp, 0, 0)
            load(sp, 1, 1)
            bias(sp, 0, 0)
            with sp.Fori(0, (GROUPS - 2) // 3) as it:
                for off in range(3):
                    G = it * 3 + off
                    sp.wait_ge(av_done, STEPS * G + 1)
                    load(sp, G + 2, (off + 2) % 3)
                    bias(sp, G + 1, (off + 1) % 3)
            bias(sp, GROUPS - 1, (GROUPS - 1) % 3)

        @block.gpsimd
        def _(pool):
            for t in range(TILES):
                for k in range(TOPK):
                    pool.indirect_dma_start(out=v["slot_x"],
                                            out_offset=bass.IndirectOffsetOnAxis(ap=v["slot"][:, k, t:t + 1], axis=0),
                                            in_=v["xf"][:, t, :], in_offset=None, bounds_check=SLOTS - 1,
                                            oob_is_err=False).then_inc(scattered, 16)
            pool.wait_ge(scattered, 16 * TOPK * TILES)

        @block.scalar
        def _(act):
            groups(act, lambda *a: act_group(act, *a))
            evac(act, GROUPS - 1, 1)

        @block.tensor
        def _(pe):
            pe.wait_ge(ones_ok, 3)
            pe.wait_ge(stack_in[0], 16 * STACK_DMAS)
            for use in range(MBANK):
                for piece in pe_use(pe, 0, 0, use, first=True):
                    piece()
            groups(pe, lambda *a: pe_group(pe, *a))
            av_step(pe, GROUPS - 1, (GROUPS - 1) % 3, STEPS - 1, "last")

        @block.vector
        def _(dve):
            for buf in range(3):
                dve.memset(k_stack[SROWS:KROWS, buf, :, :], 1.0).then_inc(ones_ok, 1)
            for use in range(MBANK):
                dve_use(dve, 0, use, True)

            def run(G, off, it, peel):
                if peel != "last":
                    for use in range(MBANK):
                        dve_use(dve, G + 1, use, False)

            groups(dve, run)


def experts(nc, sem, v):
    psum, attT, ident = v["psum"], v["attT"], v["ident"]
    expert_in = [sem(f"expert_in{i}") for i in range(4)]
    bufT_ps = sem("bufT_ps")
    bufT_ok = sem("bufT_ok")
    gu_ok = sem("gu_ok")
    tanh_ok = sem("tanh_ok")
    gate_ok = sem("gate_ok")
    hid_ok = sem("hid_ok")
    hidT_ps = sem("hidT_ps")
    hidT_ok = sem("hidT_ok")
    y_ps = sem("y_ps")
    y_ok = sem("y_ok")
    y_out = [sem(f"y_out{i}") for i in range(2)]
    norm_step = sem("norm_step")
    den_ok = sem("den_ok")
    qm, km = v["q_mem"], v["k_mem"]
    per = HID + HC * 2 * FF + 2 * HID
    xb = [qm[:, per * i:per * i + HID] for i in range(4)]
    wgu = [qm[:, per * i + HID:per * i + HID + HC * 2 * FF].rearrange("p (c s f) -> p c s f", c=HC, s=2) for i in range(4)]
    wdn = [qm[0:FHALF, per * (i + 1) - 2 * HID:per * (i + 1)].rearrange("p (c h) -> p c h", c=2) for i in range(4)]
    o = [0]

    def take(n):
        o[0] += n
        return km[:, o[0] - n:o[0]]

    xbT = [take(HID).rearrange("p (c t) -> p c t", c=HC) for _ in range(2)]
    th = [take(FF) for _ in range(2)]
    gt = [take(FF) for _ in range(2)]
    hid = [take(FF) for _ in range(2)]
    hidT = [take(2 * P)[0:FHALF, :].rearrange("p (c t) -> p c t", c=2) for _ in range(2)]
    ysb = [take(HID) for _ in range(2)]
    den = [take(SEQ) for _ in range(2)]
    ET = EXPERTS // 4

    def turns(eng, run):
        run(0, "first")
        with eng.Fori(1, ET - 1) as it:
            run(it, None)
        run(ET - 1, "last")

    def gate_up(pe, it, r, peel):
        e = it * 4 + r
        pe.wait_ge(bufT_ok, e + 1)
        if not (peel == "first" and r < 2):
            pe.wait_ge(hid_ok, e - 1)
        for c in range(HC):
            last = pe.matmul(psum[:, 2 + r % 2, 0:2 * FF], xbT[r % 2][:, c, :],
                             wgu[r][:, c, :, :].rearrange("p s f -> p (s f)"), start=(c == 0), stop=(c == HC - 1))
        last.then_inc(gu_ok, 1)

    def tokens_T(pe, it, r, lap, peel_first):
        e = it * 4 + r
        pe.wait_ge(expert_in[r], 16 * 4 * (lap + 1))
        if not peel_first:
            pe.wait_ge(bufT_ok, e - 1)
        for c in range(HC):
            last = pe.transpose(psum[:, r % 2, P * c:P * (c + 1)], xb[r][:, P * c:P * (c + 1)], ident[:, :])
        last.then_inc(bufT_ps, 1)

    def down(pe, e, rr, skip_free):
        pe.wait_ge(hidT_ok, e + 1)
        if not skip_free:
            pe.wait_ge(y_ok, e - 1)
        for c in range(2):
            last = pe.matmul(psum[:, 6 + rr % 2, 0:HID], hidT[rr % 2][:, c, :], wdn[rr][:, c, :],
                             start=(c == 0), stop=(c == 1))
        last.then_inc(y_ps, 1)

    def hidden_T(pe, it, r, peel):
        e = it * 4 + r
        pe.wait_ge(hid_ok, e + 1)
        if not (peel == "first" and r < 2):
            pe.wait_ge(hidT_ok, e - 1)
        for c in range(2):
            last = pe.transpose(psum[0:FHALF, 4 + r % 2, P * c:P * (c + 1)], hid[r % 2][:, FHALF * c:FHALF * (c + 1)], ident[:, :])
        last.then_inc(hidT_ps, 1)

    with nc.Block() as block:
        @block.sync
        def _(sp):
            def load(it, r, wait):
                e = it * 4 + r
                if wait:
                    sp.wait_ge(y_ps, e - 3)
                sp.dma_start(xb[r], v["slot_x"].rearrange("(e p) h -> e p h", p=P)[bass.ds(e, 1), :, :]
                             .rearrange("a p h -> (a p) h")).then_inc(expert_in[r], 16)
                for s, w in enumerate((v["w_gate"], v["w_up"])):
                    sp.dma_start(wgu[r][:, :, s, :], w.rearrange("e (c p) f -> e p c f", p=P)[bass.ds(e, 1), :, :, :]
                                 .rearrange("a p c f -> (a p) c f")).then_inc(expert_in[r], 16)
                sp.dma_start(wdn[r], v["w_down"].rearrange("e (c p) h -> e p c h", p=FHALF)[bass.ds(e, 1), :, :, :]
                             .rearrange("a p c h -> (a p) c h")).then_inc(expert_in[r], 16)

            for r in range(4):
                load(0, r, False)
            with sp.Fori(1, ET) as it:
                for r in range(4):
                    load(it, r, True)

        @block.gpsimd
        def _(pool):
            yv = v["slot_y"][0:SLOTS, :].rearrange("(e p) h -> e p h", p=P)

            def run(it):
                pool.tensor_copy(den[0], attT[:, bass.ds(it, 1), :].rearrange("p a t -> p (a t)")).then_inc(den_ok, 1)
                for r in range(4):
                    pool.wait_ge(y_ok, it * 4 + (r + 1))
                    pool.dma_start(yv[bass.ds(it * 4 + r, 1), :, :].rearrange("a p h -> (a p) h"),
                                   ysb[r % 2]).then_inc(y_out[r % 2], 16)

            run(0)
            with pool.Fori(1, ET) as it:
                pool.wait_ge(norm_step, it * 3)
                run(it)
            for i in range(2):
                pool.wait_ge(y_out[i], 16 * EXPERTS // 2)

        @block.scalar
        def _(act):
            def tokens(e, rr):
                act.wait_ge(bufT_ps, e + 1)
                act.copy(xbT[rr % 2].rearrange("p c t -> p (c t)"), psum[:, rr % 2, 0:HID]).then_inc(bufT_ok, 1)

            def rows(e, rr, wait):
                act.wait_ge(y_ps, e + 1)
                if wait is not None:
                    act.wait_ge(y_out[rr % 2], wait)
                act.copy(ysb[rr % 2], psum[:, 6 + rr % 2, 0:HID]).then_inc(y_ok, 1)

            def run(it, peel):
                for r in range(4):
                    e = it * 4 + r
                    act.wait_ge(gu_ok, e + 1)
                    act.activation(th[r % 2], psum[:, 2 + r % 2, 0:FF], ACT.Tanh, scale=0.5).then_inc(tanh_ok, 1)
                    if not (peel == "last" and r == 3):
                        tokens(e + 1, r + 1)
                    if not (peel == "first" and r == 0):
                        n = None if (peel == "first" and r <= 2) else (it * 2 + ((r + 1) // 2 - 1)) * 16
                        rows(e - 1, r - 1, n)

            tokens(0, 0)
            turns(act, run)
            rows(EXPERTS - 1, EXPERTS - 1, 16 * (EXPERTS // 2 - 1))

        @block.tensor
        def _(pe):
            def run(it, peel):
                for r in range(4):
                    gate_up(pe, it, r, peel)
                    if not (peel == "last" and r == 3):
                        if r < 3:
                            tokens_T(pe, it, r + 1, it, peel == "first" and r == 0)
                        else:
                            tokens_T(pe, it + 1, 0, it + 1, False)
                    if not (peel == "first" and r == 0):
                        down(pe, it * 4 + (r - 1), (r - 1) % 4, peel == "first" and r <= 2)
                    hidden_T(pe, it, r, peel)

            tokens_T(pe, 0, 0, 0, True)
            turns(pe, run)
            down(pe, EXPERTS - 1, 3, False)

        @block.vector
        def _(dve):
            def run(it, peel):
                for r in range(4):
                    e = it * 4 + r
                    g, u = psum[:, 2 + r % 2, 0:FF], psum[:, 2 + r % 2, FF:2 * FF]
                    if r == 1:
                        dve.wait_ge(den_ok, it + 1)
                    dve.wait_ge(tanh_ok, e + 1)
                    dve.scalar_tensor_tensor(gt[r % 2], th[r % 2], 1.0, g, ALU.add, ALU.mult).then_inc(gate_ok, 1)
                    dve.wait_ge(gate_ok, e + 1)
                    dve.scalar_tensor_tensor(hid[r % 2], gt[r % 2], 0.5, u, ALU.mult, ALU.mult).then_inc(hid_ok, 1)
                    a = attT[:, bass.ds(it, 1), :].rearrange("p a t -> p (a t)")
                    if r == 1:
                        dve.stream_shuffle(den[1], den[0], [HD] * 32).then_inc(norm_step, 1)
                    elif r == 2:
                        dve.wait_ge(norm_step, it * 3 + 1)
                        dve.reciprocal(den[1], den[1]).then_inc(norm_step, 1)
                    elif r == 3:
                        dve.wait_ge(norm_step, it * 3 + 2)
                        dve.tensor_tensor(a, a, den[1], ALU.mult).then_inc(norm_step, 1)
                    dve.wait_ge(hidT_ps, e + 1)
                    if not (peel == "first" and r < 2):
                        dve.wait_ge(y_ps, e - 1)
                    dve.tensor_copy(hidT[r % 2].rearrange("p c t -> p (c t)"), psum[0:FHALF, 4 + r % 2, 0:2 * P]).then_inc(hidT_ok, 1)

            turns(dve, run)


def shared(nc, sem, v):
    psum, attT, xfT, res, slot = v["psum"], v["attT"], v["xfT"], v["res"], v["slot"]
    boT, wo, wsel, sgate = v["boT"], v["wo"], v["wsel"], v["sgate"]
    sw_gu, sw_dn = v["sw_gu"], v["sw_dn"]
    gathered = [sem(f"gathered{i}") for i in range(3)]
    ro_ps = sem("ro_ps")
    ro_ok = sem("ro_ok")
    att_ps = sem("att_ps")
    att_ok = sem("att_ok")
    sgu_ps = sem("sgu_ps")
    stanh_ok = sem("stanh_ok")
    sgate_ok = sem("sgate_ok")
    shid_ok = sem("shid_ok")
    sh_ps = sem("sh_ps")
    sh_ok = sem("sh_ok")
    mix_step = sem("mix_step")
    tile_ok = sem("tile_ok")
    stored = sem("stored")
    NF = len(FCH)
    shid = v["prob"][0:FCH[0], :, :, :].rearrange("p a b n -> p (a b) n")
    qm, km = v["q_mem"], v["k_mem"]
    rows = [qm[:, 1024 * i:1024 * (i + 1)].rearrange("p (k h) -> p k h", k=TOPK) for i in range(3)]
    ro = km[:, 0:N]
    sth = [km[0:FCH[0], N * (1 + i):N * (2 + i)] for i in range(2)]
    sgt = [km[0:FCH[0], N * (3 + i):N * (4 + i)] for i in range(2)]
    out_v = v["out"].rearrange("b s h -> (b s) h").rearrange("(t p) h -> p t h", p=P)

    with nc.Block() as block:
        @block.gpsimd
        def _(pool):
            for t in range(TILES):
                if t >= 3:
                    pool.wait_ge(tile_ok, t - 2)
                for k in range(TOPK):
                    pool.indirect_dma_start(out=rows[t % 3][:, k, :], out_offset=None, in_=v["slot_y"],
                                            in_offset=bass.IndirectOffsetOnAxis(ap=slot[:, k, t:t + 1], axis=0),
                                            bounds_check=SLOTS, oob_is_err=False).then_inc(gathered[t % 3], 16)

        @block.sync
        def _(sp):
            for t in range(TILES):
                sp.wait_ge(tile_ok, t + 1)
                sp.dma_start(out_v[:, t, :], res[:, t, :]).then_inc(stored, 16)
            sp.wait_ge(stored, 16 * TILES)

        @block.scalar
        def _(act):
            for b in range(BLK):
                for f in range(NF):
                    i = NF * b + f
                    act.wait_ge(sgu_ps, i + 1)
                    if i >= 2:
                        act.wait_ge(sgate_ok, i - 1)
                    act.activation(sth[i % 2][0:FCH[f], :], psum[0:FCH[f], 2 * (i % 2), :], ACT.Tanh,
                                   scale=0.5).then_inc(stanh_ok, 1)
                if True:
                    act.wait_ge(ro_ps, b + 1)
                    if b:
                        act.wait_ge(att_ps, 2 * b)
                    act.copy(ro, psum[:, 4, :]).then_inc(ro_ok, 1)

        @block.tensor
        def _(pe):
            def gate_up(b):
                for f in range(NF):
                    i = NF * b + f
                    if i >= 2:
                        pe.wait_ge(shid_ok, i - 1)
                    for s in range(2):
                        for c in range(HC):
                            last = pe.matmul(psum[0:FCH[f], 2 * (i % 2) + s, :], sw_gu[:, c, s, FOFF[f]:FOFF[f] + FCH[f]],
                                             xfT[:, c, N * b:N * (b + 1)], start=(c == 0), stop=(c == HC - 1))
                    last.then_inc(sgu_ps, 1)
                if b:
                    pe.wait_ge(ro_ok, b)
                for g in range(HG):
                    last = pe.matmul(psum[:, 4, :], boT[:, g, :],
                                     attT[:, HG * (b // 2) + g, N * (b % 2):N * (b % 2 + 1)], start=(g == 0), stop=(g == HG - 1))
                last.then_inc(ro_ps, 1)

            def tail(b):
                pe.wait_ge(shid_ok, NF * (b + 1))
                for i in range(2):
                    n = 2 * b + i
                    if n:
                        pe.wait_ge(att_ok, n)
                    if i == 0:
                        pe.wait_ge(ro_ok, b + 1)
                    for t in range(2):
                        tt = 2 * i + t
                        last = pe.matmul(psum[:, 5, HID * t:HID * (t + 1)], ro[:, P * tt:P * (tt + 1)], wo[:, :], start=True, stop=True)
                    last.then_inc(att_ps, 1)
                    if n >= 2:
                        pe.wait_ge(sh_ok, n - 1)
                    for t in range(2):
                        tt = 2 * i + t
                        for f in range(NF):
                            last = pe.matmul(psum[:, 6 + i, HID * t:HID * (t + 1)],
                                             shid[0:FCH[f], NF * (b % 2) + f, P * tt:P * (tt + 1)], sw_dn[0:FCH[f], f, :],
                                             start=(f == 0), stop=(f == NF - 1))
                    last.then_inc(sh_ps, 1)

            gate_up(0)
            for b in range(1, BLK):
                gate_up(b)
                tail(b - 1)
            tail(BLK - 1)

        @block.vector
        def _(dve):
            steps = [0]

            def link(ins):
                steps[0] += 1
                ins.then_inc(mix_step, 1)
                dve.wait_ge(mix_step, steps[0])

            def hidden(b):
                for f in range(NF):
                    i = NF * b + f
                    n = FCH[f]
                    dve.wait_ge(stanh_ok, i + 1)
                    dve.scalar_tensor_tensor(sgt[i % 2][0:n, :], sth[i % 2][0:n, :], 1.0, psum[0:n, 2 * (i % 2), :],
                                             ALU.add, ALU.mult).then_inc(sgate_ok, 1)
                    dve.wait_ge(sgate_ok, i + 1)
                    if b >= 2:
                        dve.wait_ge(sh_ps, 2 * (b - 1))
                    dve.scalar_tensor_tensor(shid[0:n, NF * (b % 2) + f, :], sgt[i % 2][0:n, :], 0.5,
                                             psum[0:n, 2 * (i % 2) + 1, :], ALU.mult, ALU.mult).then_inc(shid_ok, 1)

            def mix(b):
                for i in range(2):
                    n = 2 * b + i
                    r2 = res[:, 2 * n:2 * n + 2, :].rearrange("p t h -> p (t h)")
                    dve.wait_ge(att_ps, n + 1)
                    dve.tensor_tensor(r2, r2, psum[:, 5, :], ALU.add).then_inc(att_ok, 1)
                    dve.wait_ge(att_ok, n + 1)
                    dve.wait_ge(sh_ps, n + 1)
                    for t in range(2):
                        tile = 2 * n + t
                        ins = dve.scalar_tensor_tensor(res[:, tile, :], psum[:, 6 + i, HID * t:HID * (t + 1)], sgate[:, tile:tile + 1],
                                                       res[:, tile, :], ALU.mult, ALU.add)
                        if t:
                            ins.then_inc(sh_ok, 1)
                            dve.wait_ge(sh_ok, n + 1)
                        else:
                            link(ins)
                    for t in range(2):
                        tile = 2 * n + t
                        dve.wait_ge(gathered[tile % 3], 16 * TOPK * (tile // 3 + 1))
                        for k in range(TOPK):
                            ins = dve.scalar_tensor_tensor(res[:, tile, :], rows[tile % 3][:, k, :], wsel[:, k, tile:tile + 1],
                                                           res[:, tile, :], ALU.mult, ALU.add)
                            if k == TOPK - 1:
                                ins.then_inc(tile_ok, 1)
                            else:
                                link(ins)

            hidden(0)
            for b in range(1, BLK):
                hidden(b)
                mix(b - 1)
            mix(BLK - 1)


_INS = ['L0_attn_hidden_states', 'L0_attn_basis_q', 'L0_attn_phase_q', 'L0_attn_amp_q', 'L0_attn_basis_k',
        'L0_attn_phase_k', 'L0_attn_amp_k', 'L0_attn_basis_v', 'L0_attn_phase_v', 'L0_attn_amp_v',
        'L0_attn_basis_o', 'L0_attn_phase_o', 'L0_attn_amp_o', 'L0_ffn_w_norm', 'L0_ffn_w_router', 'L0_ffn_w_gate',
        'L0_ffn_w_up', 'L0_ffn_w_down', 'L0_ffn_sw_gate', 'L0_ffn_sw_up', 'L0_ffn_sw_down', 'L0_ffn_w_shared_gate']
_OUTS = [((2, 1024, 256), 'float32')]


def kernel(**inputs):
    import numpy as _np
    import concourse.bacc as _bacc
    from concourse import mybir as _mybir
    from concourse.bass_utils import run_bass_kernel_spmd as _run

    nc = _bacc.Bacc("TRN2", target_bir_lowering=False, num_devices=1)
    arrays, args = {}, []
    for name in _INS:
        a = _np.ascontiguousarray(inputs[name])
        arrays[f"in_{name}_dram"] = a
        args.append(nc.dram_tensor(f"in_{name}_dram", a.shape, _mybir.dt.from_np(a.dtype), kind="ExternalInput").ap())
    for i, (shape, dtype) in enumerate(_OUTS):
        dt = _mybir.dt.from_np(_np.dtype(dtype))
        args.append(nc.dram_tensor(f"out_{i}_dram", shape, dt, kind="ExternalOutput").ap())
    build(nc, *args)
    r = _run(nc, [arrays], core_ids=[0])
    got = tuple(r.results[0][f"out_{i}_dram"] for i in range(len(_OUTS)))
    return got[0]
```

```python
from contextlib import ExitStack

import concourse.bass as bass
from concourse import mybir

FP32 = mybir.dt.float32
BF16 = mybir.dt.bfloat16
U32 = mybir.dt.uint32
ALU = mybir.AluOpType
ACT = mybir.ActivationFunctionType
AX = mybir.AxisListType

P = 128
BATCH, SEQ, HID = 2, 1024, 256
TOK = BATCH * SEQ
TILES = TOK // P
HC = HID // P
HEADS, HD, HARM = 16, 16, 64
GH = 4
HG = HEADS // GH
GROUPS = BATCH * HG
KT = SEQ // P
N = 512
QH = SEQ // N
STEPS = QH * KT
EXPERTS, TOPK, FF, CAP = 32, 4, 176, 128
SLOTS = EXPERTS * CAP
FS = 704
FCH = [118] * 5 + [114]
FOFF = [118 * i for i in range(6)]
FHALF = FF // 2
BLK = TOK // N
TPB = N // P
LN_EPS, RMS_EPS = 1e-5, 1e-6
SCALE = HD ** -0.5
TWO_PI_HI, TWO_PI_LO = 6.28125, 0.0019353071795864769
INV_TWO_PI = 0.15915494309189535
ROUND = 1.5 * 2.0 ** 23
PI = 3.1415925
PAIRS = [(0, 0), (0, 1), (0, 2), (1, 0), (1, 1), (2, 0)]
SROWS = HD * len(PAIRS)
KROWS = SROWS + 2
STACK_DMAS = 2 * len(PAIRS) + 1
BIAS_DMAS = 4
UNITS = GH * KT
MBANK = UNITS + 2


def build(nc, x, bq, pq, aq, bk, pk, ak, bv, pv, av, bo, po, ao, w_norm, w_router, w_gate, w_up,
          w_down, sw_gate, sw_up, sw_down, w_sg, out):
    ctx = ExitStack()
    with ctx:
        def sb(name, shape, dt=FP32):
            return ctx.enter_context(nc.sbuf_tensor(name, shape, dt))

        def sem(name):
            return ctx.enter_context(nc.semaphore(name))

        q_parts = nc.dram_tensor("q_parts", (GROUPS, 3, HD * GH, SEQ), BF16).ap()
        k_parts = nc.dram_tensor("k_parts", (GROUPS, 3, HD * GH, SEQ), BF16).ap()
        v_wide = nc.dram_tensor("v_wide", (GROUPS, SEQ, GH * 32), FP32).ap()
        slot_x = nc.dram_tensor("slot_x", (SLOTS, HID), FP32).ap()
        slot_y = nc.dram_tensor("slot_y", (SLOTS + 1, HID), FP32).ap()

        res = sb("res", [P, TILES, HID])
        wide = sb("wide", [P, GROUPS * SEQ])
        xn = wide[:, 0:TILES * HID].rearrange("p (t h) -> p t h", t=TILES)
        xnT = wide[:, TILES * HID:2 * TILES * HID].rearrange("p (c t) -> p c t", c=HC)
        attT = wide[:, :].rearrange("p (g t) -> p g t", g=GROUPS)
        xf = sb("xf", [P, TILES, HID])
        xfT = sb("xfT", [P, HC, TOK])
        q_mem = sb("q_mem", [P, 3 * GH * SEQ // 2])
        k_mem = sb("k_mem", [P, 3 * GH * SEQ // 2])
        q_stack = q_mem[:, :].bitcast(BF16).rearrange("p (b j t) -> p b j t", b=3, j=GH)
        k_stack = k_mem[:, :].bitcast(BF16).rearrange("p (b j t) -> p b j t", b=3, j=GH)
        v_stack = sb("v_stack", [P, 3, KT, GH, 32])
        prob = sb("prob", [P, 3, GH, N])
        sw_gu = sb("sw_gu", [P, HC, 2, FS])
        sw_dn = sb("sw_dn", [FCH[0], len(FCH), HID])
        ident = sb("ident", [P, P])
        ident_b = sb("ident_b", [P, P], BF16)
        before = sb("before", [P, P], BF16)
        ones_b = sb("ones_b", [P, P], BF16)
        bT = sb("bT", [P, 2, HC, P])
        wq = sb("wq", [P, HID])
        wk = sb("wk", [P, HID])
        wv = sb("wv", [P, HID])
        wo = sb("wo", [P, HID])
        boT = sb("boT", [P, HG, P])
        wr = sb("wr", [P, HC, EXPERTS + 1])
        rt = sb("rt", [P, 2, N])
        rvo = sb("rvo", [P, N])
        mx = sb("mx", [P, UNITS])
        nm = sb("nm", [P, 2, 2, 2, KT], BF16)
        nmT = sb("nmT", [32, 2, P], BF16)
        slot = sb("slot", [P, TOPK, TILES], U32)
        wsel = sb("wsel", [P, TOPK, TILES])
        sgate = sb("sgate", [P, TILES])
        small = sb("small", [P, 16, TILES])
        bn = sb("bn", [P, TILES, 6])
        mv = sb("mv", [P, TILES, 2])
        top8 = sb("top8", [P, TILES, 8])
        idx8 = sb("idx8", [P, TILES, 8], U32)
        idxf = sb("idxf", [P, TILES, 8])
        wn = sb("wn", [P, HID])
        iota_e = sb("iota_e", [P, EXPERTS])
        mask_b = sb("mask_b", [P, TILES, EXPERTS], BF16)
        eps = sb("eps", [P, 2])

        psum = ctx.enter_context(nc.psum_tensor("psum", [P, 8, N], FP32))

        probf = prob[:, :, :, :].rearrange("p a b c -> p (a b c)")
        zeros = probf[:, 0:2048]
        phase = probf[:, 2048:2560].rearrange("p (c m h) -> p c m h", c=2, m=4)
        amp = probf[:, 2560:3072].rearrange("p (c m h) -> p c m h", c=2, m=4)
        turn = probf[:, 3072:3584].rearrange("p (c m h) -> p c m h", c=2, m=4)
        ang = probf[:, 3584:4096].rearrange("p (c m h) -> p c m h", c=2, m=4)
        wmat = probf[:, 4096:4608].rearrange("p (c m h) -> p c m h", c=2, m=4)
        rem = probf[:, 4608:5632].rearrange("p (b n) -> p b n", b=2)
        bo_pad = probf[:, 5632:6144].rearrange("p (g j d) -> p g j d", g=HG, j=GH)
        basis = k_mem[:, 5120:5632].rearrange("p (s h) -> p s h", s=2)
        parts = q_mem[:, :].bitcast(BF16).rearrange("p (u s t) -> p u s t", u=4, s=3)
        v_stage = k_mem[:, 0:4096].rearrange("p (b t h d) -> p b t h d", b=4, t=2, h=HEADS)
        vsf = v_stack[:, :, :, :, :].rearrange("p a b c d -> p (a b c d)")
        probs = vsf[:, 0:512].rearrange("p (t e) -> p t e", t=TILES)
        onehot = vsf[:, 512:2560].rearrange("p (k t e) -> p k t e", k=TOPK, t=TILES)
        rtmp = vsf[:, 2560:3072].rearrange("p (t e) -> p t e", t=TILES)
        cum = k_mem[:, 4096:5120].rearrange("p (b t e) -> p b t e", b=2, t=TILES)
        pos = k_mem[:, 5632:6144].rearrange("p (t e) -> p t e", t=TILES)

        prologue(nc, sem, locals())
        attention(nc, sem, locals())
        feed_forward(nc, sem, locals())


def prologue(nc, sem, v):
    (x, res, xn, xnT, xf, xfT, psum, ident, ident_b, before, ones_b, bT, wq, wk, wv, wo, boT, wr, rt, rvo) = (
        v["x"], v["res"], v["xn"], v["xnT"], v["xf"], v["xfT"], v["psum"], v["ident"], v["ident_b"], v["before"],
        v["ones_b"], v["bT"], v["wq"], v["wk"], v["wv"], v["wo"], v["boT"], v["wr"], v["rt"], v["rvo"])
    (zeros, phase, amp, turn, ang, wmat, rem, bo_pad, basis, parts, v_stage, probs, onehot, rtmp, cum, pos) = (
        v["zeros"], v["phase"], v["amp"], v["turn"], v["ang"], v["wmat"], v["rem"], v["bo_pad"], v["basis"],
        v["parts"], v["v_stage"], v["probs"], v["onehot"], v["rtmp"], v["cum"], v["pos"])
    (bn, mv, small, eps, wn, top8, idx8, idxf, iota_e, mask_b, slot, wsel, sgate, k_stack) = (
        v["bn"], v["mv"], v["small"], v["eps"], v["wn"], v["top8"], v["idx8"], v["idxf"], v["iota_e"],
        v["mask_b"], v["slot"], v["wsel"], v["sgate"], v["k_stack"])
    slot_x, slot_y, v_wide = v["slot_x"], v["slot_y"], v["v_wide"]

    x_in = [sem(f"x_in{i}") for i in range(BLK)]
    holo_in = sem("holo_in")
    vec_in = sem("vec_in")
    late_in = sem("late_in")
    zero_out = sem("zero_out")
    const_ok = sem("const_ok")
    pool_step = sem("pool_step")
    dve_step = sem("dve_step")
    var_ok = sem("var_ok")
    sqrt_ok = sem("sqrt_ok")
    xn_ok = sem("xn_ok")
    ms_ok = sem("ms_ok")
    xf_ok = sem("xf_ok")
    ang_ok = sem("ang_ok")
    sin_ok = sem("sin_ok")
    wmat_ok = sem("wmat_ok")
    wtr_ok = sem("wtr_ok")
    wT_ok = sem("wT_ok")
    tr_ok = sem("tr_ok")
    xnT_ok = sem("xnT_ok")
    xfT_ok = sem("xfT_ok")
    r_ok = sem("r_ok")
    rs_ok = sem("rs_ok")
    qk_ok = sem("qk_ok")
    hi_ok = sem("hi_ok")
    rem_ok = sem("rem_ok")
    mid_ok = sem("mid_ok")
    low_ok = sem("low_ok")
    part_out = [sem(f"part_out{u}") for u in range(4)]
    v_ok = sem("v_ok")
    vs_ok = sem("vs_ok")
    v_out = [sem(f"v_out{i}") for i in range(4)]
    logit_ok = sem("logit_ok")
    exp_in = sem("exp_in")
    exp_ok = sem("exp_ok")
    mask_ok = sem("mask_ok")
    count_ok = sem("count_ok")

    mats = [(v["pq"], v["aq"]), (v["pk"], v["ak"]), (v["pv"], v["av"]), (v["po"], v["ao"])]
    HOLO = 2 * len(mats) + 4
    VDMAS = 2

    with nc.Block() as block:
        @block.sync
        def _(sp):
            xr = x.rearrange("b s h -> (b s) h").rearrange("(t p) h -> p t h", p=P)
            for i in range(BLK):
                sp.dma_start(res[:, TPB * i:TPB * (i + 1), :], xr[:, TPB * i:TPB * (i + 1), :]).then_inc(x_in[i], 16)
            sp.wait_ge(const_ok, 5)
            sp.wait_ge(holo_in, 16 * HOLO)
            for i in range(4):
                sp.dma_start(slot_x[1024 * i:1024 * (i + 1), :].rearrange("(p r) h -> p (r h)", p=P),
                             zeros).then_inc(zero_out, 16)
            sp.dma_start(slot_y[SLOTS:SLOTS + 1, :], zeros[0:1, 0:HID]).then_inc(zero_out, 16)
            sgu = v["sw_gu"]
            sp.dma_start(sgu[:, :, 0, :], v["sw_gate"].rearrange("(c p) f -> p c f", p=P)).then_inc(late_in, 16)
            sp.dma_start(sgu[:, :, 1, :], v["sw_up"].rearrange("(c p) f -> p c f", p=P)).then_inc(late_in, 16)
            for i, (o, n) in enumerate(zip(FOFF, FCH)):
                sp.dma_start(v["sw_dn"][0:n, i, :], v["sw_down"][o:o + n, :]).then_inc(late_in, 16)
            for b in range(BATCH):
                for u in range(4):
                    dst = (v["q_parts"], v["k_parts"])[u // 2]
                    sp.wait_ge(low_ok, 8 * b + 4 + u + 1)
                    for i in range(2):
                        sp.dma_start(dst[HG * b + 2 * (u % 2) + i, :, :, :].rearrange("s p t -> p s t"),
                                     parts[64 * i:64 * (i + 1), u, :, :]).then_inc(part_out[u], 16)
            for u in range(4):
                sp.wait_ge(part_out[u], 16 * 2 * BATCH)
            sp.wait_ge(zero_out, 16 * 5)
            sp.wait_ge(late_in, 16 * 8)

        @block.gpsimd
        def _(pool):
            pool.memset(ident[:, :], 0.0).then_inc(pool_step, 1)
            pool.memset(ident_b[:, :], 0.0).then_inc(pool_step, 1)
            pool.memset(before[:, :], 1.0).then_inc(pool_step, 1)
            pool.wait_ge(pool_step, 3)
            for m in (ident, ident_b):
                pool.affine_select(out=m[:, :], in_=m[:, :], compare_op=ALU.not_equal, fill=1.0, base=0,
                                   pattern=[[-1, P]], channel_multiplier=1).then_inc(const_ok, 1)
            pool.affine_select(out=before[:, :], in_=before[:, :], compare_op=ALU.is_gt, fill=0.0, base=0,
                               pattern=[[1, P]], channel_multiplier=-1).then_inc(const_ok, 1)
            pool.memset(ones_b[:, :], 1.0).then_inc(const_ok, 1)
            pool.memset(zeros, 0.0).then_inc(const_ok, 1)
            pool.iota(iota_e[:, :], pattern=[[1, EXPERTS]], base=0, channel_multiplier=0,
                      allow_small_or_imprecise_dtypes=True).then_inc(const_ok, 1)
            for b in range(BLK):
                pool.wait_ge(xn_ok, TPB * (b + 1))
                sl = slice(TPB * b, TPB * (b + 1))
                pool.tensor_tensor(res[:, sl, :], res[:, sl, :], xn[:, sl, :], ALU.add).then_inc(pool_step, 1)

        @block.scalar
        def _(act):
            act.dma_start(basis[0:64, 0, :], v["bq"]).then_inc(holo_in, 16)
            act.dma_start(basis[64:128, 0, :], v["bk"]).then_inc(holo_in, 16)
            act.dma_start(basis[0:64, 1, :], v["bv"]).then_inc(holo_in, 16)
            act.dma_start(basis[64:128, 1, :], v["bo"]).then_inc(holo_in, 16)
            for m, (ph, am) in enumerate(mats):
                act.dma_start(phase[:, :, m, :], ph.rearrange("(c p) h -> p c h", p=P)).then_inc(holo_in, 16)
                act.dma_start(amp[:, :, m, :], am.rearrange("(c p) h -> p c h", p=P)).then_inc(holo_in, 16)
            wn_src = v["w_norm"].rearrange("(a h) -> a h", a=1)
            act.dma_start(wn[:, :], wn_src.broadcast_to([P, HID])).then_inc(vec_in, 16)
            act.dma_start(wr[:, :, 0:EXPERTS], v["w_router"].rearrange("(c p) e -> p c e", p=P)).then_inc(vec_in, 16)
            with nc.allow_non_contiguous_dma(reason="one column of 256 weights"):
                act.dma_start(wr[:, :, EXPERTS:EXPERTS + 1],
                              v["w_sg"].rearrange("(c p) e -> p c e", p=P)).then_inc(vec_in, 16)
            act.wait_ge(ang_ok, 1)
            act.activation(wmat, ang, ACT.Sin).then_inc(sin_ok, 1)
            act.wait_ge(var_ok, 1)
            act.activation(small[:, 0, :], mv[:, :, 1], ACT.Sqrt, bias=eps[:, 0:1]).then_inc(sqrt_ok, 1)
            for t in range(TILES):
                act.wait_ge(xn_ok, t + 1)
                act.activation(xf[:, t, :], xn[:, t, :], ACT.Square, scale=1.0 / 16.0,
                               accum_out=small[:, 4, t:t + 1]).then_inc(ms_ok, 1)
            act.wait_ge(ms_ok, TILES)
            act.activation(small[:, 5, :], small[:, 4, :], ACT.Sqrt, bias=eps[:, 1:2]).then_inc(sqrt_ok, 1)
            for b in range(BLK):
                blk = slice(N * b, N * (b + 1))
                for c in range(HC):
                    act.wait_ge(tr_ok, 4 * b + c + 1)
                    act.copy(xnT[:, c, blk], psum[:, c, :]).then_inc(xnT_ok, 1)
                for i, dst in enumerate((rt[:, b % 2, :], rvo[:, :])):
                    act.wait_ge(r_ok, 2 * b + i + 1)
                    if i == 0 and b >= 2:
                        act.wait_ge(qk_ok, 4 * (b - 1))
                    if i == 1 and b >= 1:
                        act.wait_ge(v_ok, 2 * b)
                    act.copy(dst, psum[:, 4, :] if i == 0 else psum[:, 5, :]).then_inc(rs_ok, 1)
                for u in range(4):
                    n = 4 * b + u
                    half = slice(N * (b % 2), N * (b % 2 + 1))
                    act.wait_ge(qk_ok, n + 1)
                    if b >= 2:
                        act.wait_ge(part_out[u], 32)
                    act.copy(parts[:, u, 0, half], psum[:, 6 + u % 2, :]).then_inc(hi_ok, 1)
                    act.wait_ge(rem_ok, n + 1)
                    act.copy(parts[:, u, 1, half], rem[:, n % 2, :]).then_inc(mid_ok, 1)
                for i in range(2):
                    n = 2 * b + i
                    act.wait_ge(v_ok, n + 1)
                    act.wait_ge(dve_step, 1)
                    if n >= 4:
                        act.wait_ge(v_out[n % 4], VDMAS * 16 * (n // 4))
                    act.copy(v_stage[:, n % 4, :, :, 0:HD],
                             psum[:, 4 + i, :].rearrange("p (t h d) -> p t h d", t=2, h=HEADS)).then_inc(vs_ok, 1)
                    act.wait_ge(vs_ok, n + 1)
                    for t in range(2):
                        tile = 2 * n + t
                        row = P * (tile % KT)
                        act.dma_start(v_wide[HG * (tile // KT):HG * (tile // KT + 1), row:row + P, :].rearrange("g p n -> p g n"),
                                      v_stage[:, n % 4, t, :, :].rearrange("p (g j) d -> p g (j d)", g=HG)).then_inc(v_out[n % 4], 16)
            act.wait_ge(exp_in, 1)
            act.activation(probs, probs, ACT.Exp).then_inc(exp_ok, 1)
            act.activation(small[:, 10, :], small[:, 9, :], ACT.Tanh, scale=0.5).then_inc(exp_ok, 1)
            for i in range(4):
                act.wait_ge(v_out[i], VDMAS * 16 * 2)

        @block.tensor
        def _(pe):
            pe.wait_ge(const_ok, 2)
            pe.wait_ge(holo_in, 16 * HOLO - 16 * 0)
            for s in range(2):
                for c in range(HC):
                    last = pe.transpose(psum[:, 0, P * (2 * s + c):P * (2 * s + c + 1)],
                                        basis[:, s, P * c:P * (c + 1)], ident[:, :])
            last.then_inc(wtr_ok, 1)
            pe.wait_ge(wmat_ok, 2)
            for s in range(2):
                for c in range(HC):
                    last = pe.transpose(psum[:, 1, P * (2 * s + c):P * (2 * s + c + 1)],
                                        wmat[:, c, 2 * s:2 * s + 2, :], ident[:, :])
            last.then_inc(wtr_ok, 1)
            for g in range(HG):
                last = pe.transpose(psum[:, 2, P * g:P * (g + 1)], bo_pad[:, g, :, :], ident[:, :])
            last.then_inc(wtr_ok, 1)
            pe.wait_ge(wT_ok, 6)
            for b in range(BLK):
                blk = slice(N * b, N * (b + 1))
                for src, ok, free, bank in ((xn, xn_ok, xnT_ok, 0), (xf, xf_ok, xfT_ok, 2)):
                    pe.wait_ge(ok, TPB * (b + 1))
                    for c in range(HC):
                        if b:
                            pe.wait_ge(free, 2 * (b - 1) + c + 1)
                        for t in range(TPB):
                            last = pe.transpose(psum[:, bank + c, P * t:P * (t + 1)],
                                                src[:, TPB * b + t, P * c:P * (c + 1)], ident[:, :])
                        last.then_inc(tr_ok, 1)
                pe.wait_ge(xnT_ok, 2 * (b + 1))
                for s in range(2):
                    if b:
                        pe.wait_ge(vs_ok, 2 * (b - 1) + s + 1)
                    for c in range(HC):
                        last = pe.matmul(psum[:, 4 + s, :], bT[:, s, c, :], xnT[:, c, blk],
                                         start=(c == 0), stop=(c == HC - 1))
                    last.then_inc(r_ok, 1)
                pe.wait_ge(rs_ok, 2 * b + 1)
                for u in range(4):
                    n = 4 * b + u
                    if n >= 2:
                        pe.wait_ge(hi_ok, n - 1)
                        pe.wait_ge(rem_ok, n - 1)
                    w = (wq, wk)[u // 2]
                    pe.matmul(psum[:, 6 + u % 2, :], w[:, P * (u % 2):P * (u % 2 + 1)], rt[:, b % 2, :],
                              start=True, stop=True).then_inc(qk_ok, 1)
                pe.wait_ge(rs_ok, 2 * b + 2)
                for i in range(2):
                    for t in range(2):
                        tt = 2 * i + t
                        last = pe.matmul(psum[:, 4 + i, HID * t:HID * (t + 1)], rvo[:, P * tt:P * (tt + 1)],
                                         wv[:, :], start=True, stop=True)
                    last.then_inc(v_ok, 1)
            pe.wait_ge(vec_in, 48)
            pe.wait_ge(xnT_ok, 2 * BLK)
            pe.wait_ge(xfT_ok, 2 * BLK)
            for t in range(TILES):
                for c in range(HC):
                    last = pe.matmul(psum[:, t // 8, 64 * (t % 8):64 * (t % 8) + EXPERTS + 1],
                                     xfT[:, c, P * t:P * (t + 1)], wr[:, c, :], start=(c == 0), stop=(c == HC - 1))
            last.then_inc(logit_ok, 1)
            pe.wait_ge(mask_ok, 1)
            mb = mask_b[:, :, :].rearrange("p t e -> p (t e)")
            pe.matmul(psum[:, 2, :], before[:, :], mb, start=True, stop=True).then_inc(count_ok, 1)
            pe.matmul(psum[:, 3, :], ones_b[:, :], mb, start=True, stop=True).then_inc(count_ok, 1)

        @block.vector
        def _(dve):
            steps = [0]

            def link(ins):
                steps[0] += 1
                ins.then_inc(dve_step, 1)
                dve.wait_ge(dve_step, steps[0])

            link(dve.memset(v_stage[:, :, :, :, HD:32], 1.0))
            dve.memset(bo_pad, 0.0)
            dve.memset(wq[64:128, :], 0.0)
            dve.memset(wk[0:64, :], 0.0)
            dve.memset(wv[64:128, :], 0.0)
            dve.memset(wo[0:64, :], 0.0)
            dve.memset(eps[:, 0:1], LN_EPS)
            link(dve.memset(eps[:, 1:2], RMS_EPS))
            dve.wait_ge(holo_in, 16 * HOLO)
            link(dve.tensor_scalar(turn, phase, INV_TWO_PI, 0.25, ALU.mult, ALU.add))
            link(dve.tensor_scalar(turn, turn, ROUND, ROUND, ALU.add, ALU.subtract))
            link(dve.scalar_tensor_tensor(ang, turn, -TWO_PI_HI, phase, ALU.mult, ALU.add))
            link(dve.scalar_tensor_tensor(ang, turn, -TWO_PI_LO, ang, ALU.mult, ALU.add))
            link(dve.tensor_scalar(ang, ang, PI / 2, PI, ALU.add, ALU.min))
            dve.tensor_scalar(ang, ang, -PI, None, ALU.max).then_inc(ang_ok, 1)
            for b in range(BLK):
                dve.wait_ge(x_in[b], 16)
                for t in range(TPB * b, TPB * (b + 1)):
                    last = dve.bn_stats(bn[:, t, :], res[:, t, :])
            link(last)
            for t in range(TILES):
                last = dve.bn_aggr(mv[:, t, :], bn[:, t, :])
            last.then_inc(var_ok, 1)
            dve.wait_ge(sin_ok, 1)
            dve.tensor_tensor(wmat, wmat, amp, ALU.mult).then_inc(wmat_ok, 1)
            dve.tensor_copy(bo_pad[64:128, :, :, 0:HD],
                            basis[64:128, 1, :].rearrange("p (g j d) -> p g j d", g=HG, j=GH)).then_inc(wmat_ok, 1)

            def inverse_root(var, root, e, tmp, y):
                link(dve.reciprocal(y, root))
                link(dve.tensor_tensor(tmp, y, y, ALU.mult))
                link(dve.scalar_tensor_tensor(tmp, var, e, tmp, ALU.add, ALU.mult))
                link(dve.tensor_scalar(tmp, tmp, -0.5, 1.5, ALU.mult, ALU.add))
                link(dve.tensor_tensor(y, y, tmp, ALU.mult))

            dve.wait_ge(sqrt_ok, 1)
            inverse_root(mv[:, :, 1], small[:, 0, :], LN_EPS, small[:, 1, :], small[:, 2, :])
            for t in range(TILES):
                dve.tensor_scalar(xn[:, t, :], res[:, t, :], mv[:, t, 0:1], small[:, 2, t:t + 1],
                                  ALU.subtract, ALU.mult).then_inc(xn_ok, 1)
            dve.wait_ge(wtr_ok, 3)
            dve.tensor_copy(bT[:, :, :, :].rearrange("p s c h -> p (s c h)"), psum[:, 0, :]).then_inc(wT_ok, 1)
            for w, lo, col in ((wq, 0, 0), (wk, 64, 0)):
                dve.tensor_copy(w[lo:lo + 64, :].rearrange("p (g d j) -> p g d j", g=HG, d=HD),
                                psum[lo:lo + 64, 1, 0:HID].rearrange("p (g j d) -> p g d j", g=HG, j=GH)).then_inc(wT_ok, 1)
            dve.tensor_copy(wv[0:64, :], psum[0:64, 1, HID:2 * HID]).then_inc(wT_ok, 1)
            dve.tensor_copy(wo[64:128, :], psum[64:128, 1, HID:2 * HID]).then_inc(wT_ok, 1)
            dve.tensor_copy(boT[:, :, :].rearrange("p g h -> p (g h)"), psum[:, 2, :]).then_inc(wT_ok, 1)
            dve.wait_ge(sqrt_ok, 2)
            dve.wait_ge(vec_in, 48)
            inverse_root(small[:, 4, :], small[:, 5, :], RMS_EPS, small[:, 6, :], small[:, 7, :])
            for t in range(TILES):
                dve.scalar_tensor_tensor(xf[:, t, :], xn[:, t, :], small[:, 7, t:t + 1], wn[:, :],
                                         ALU.mult, ALU.mult).then_inc(xf_ok, 1)
            for b in range(BLK):
                blk = slice(N * b, N * (b + 1))
                for c in range(HC):
                    dve.wait_ge(tr_ok, 4 * b + 2 + c + 1)
                    dve.tensor_copy(xfT[:, c, blk], psum[:, 2 + c, :]).then_inc(xfT_ok, 1)
                for u in range(4):
                    n = 4 * b + u
                    half = slice(N * (b % 2), N * (b % 2 + 1))
                    dve.wait_ge(hi_ok, n + 1)
                    dve.tensor_tensor(rem[:, n % 2, :], psum[:, 6 + u % 2, :], parts[:, u, 0, half],
                                      ALU.subtract).then_inc(rem_ok, 1)
                    dve.wait_ge(mid_ok, n + 1)
                    dve.tensor_tensor(parts[:, u, 2, half], rem[:, n % 2, :], parts[:, u, 1, half],
                                      ALU.subtract).then_inc(low_ok, 1)
            dve.wait_ge(logit_ok, 1)
            dve.wait_ge(const_ok, 6)
            lg = psum[:, 0:2, :].rearrange("p b (t e) -> p (b t) e", e=64)
            link(dve.tensor_copy(probs, lg[:, :, 0:EXPERTS]))
            link(dve.tensor_copy(small[:, 9, :], lg[:, :, EXPERTS]))
            link(dve.tensor_reduce(small[:, 8, :], probs, AX.X, ALU.max))
            dve.tensor_tensor(probs, probs, small[:, 8, :].unsqueeze(2).broadcast_to([P, TILES, EXPERTS]),
                              ALU.subtract).then_inc(exp_in, 1)
            dve.wait_ge(exp_ok, 2)
            link(dve.tensor_reduce(small[:, 11, :], probs, AX.X, ALU.add))
            link(dve.reciprocal(small[:, 12, :], small[:, 11, :]))
            link(dve.tensor_tensor(probs, probs, small[:, 12, :].unsqueeze(2).broadcast_to([P, TILES, EXPERTS]), ALU.mult))
            dve.tensor_scalar(sgate[:, :], small[:, 10, :], 0.5, 0.5, ALU.mult, ALU.add)
            for t in range(TILES):
                last = dve.max(top8[:, t, :], probs[:, t, :])
            link(last)
            for t in range(TILES):
                last = dve.max_index(idx8[:, t, :], top8[:, t, :], probs[:, t, :])
            link(last)
            link(dve.tensor_copy(idxf[:, :, :], idx8[:, :, :]))
            ie = iota_e[:, :].unsqueeze(1).broadcast_to([P, TILES, EXPERTS])
            for k in range(TOPK):
                last = dve.tensor_tensor(onehot[:, k, :, :], ie,
                                         idxf[:, :, k:k + 1].broadcast_to([P, TILES, EXPERTS]), ALU.is_equal)
            link(last)
            link(dve.tensor_tensor(rtmp, onehot[:, 0, :, :], onehot[:, 1, :, :], ALU.add))
            link(dve.tensor_tensor(rtmp, rtmp, onehot[:, 2, :, :], ALU.add))
            dve.tensor_tensor(mask_b[:, :, :], rtmp, onehot[:, 3, :, :], ALU.add).then_inc(mask_ok, 1)
            dve.wait_ge(count_ok, 2)
            tot = psum[:, 3, :].rearrange("p (t e) -> p t e", t=TILES)
            link(dve.tensor_copy(cum[:, 0, :, :], tot))
            cur, sh = 0, 1
            while sh < TILES:
                dve.tensor_copy(cum[:, 1 - cur, 0:sh, :], cum[:, cur, 0:sh, :])
                link(dve.tensor_tensor(cum[:, 1 - cur, sh:, :], cum[:, cur, sh:, :], cum[:, cur, 0:TILES - sh, :], ALU.add))
                cur, sh = 1 - cur, 2 * sh
            link(dve.tensor_tensor(pos, cum[:, cur, :, :], tot, ALU.subtract))
            link(dve.tensor_tensor(pos, pos, psum[:, 2, :].rearrange("p (t e) -> p t e", t=TILES), ALU.add))
            for k in range(TOPK):
                link(dve.tensor_tensor(rtmp, onehot[:, k, :, :], pos, ALU.mult))
                link(dve.tensor_reduce(small[:, 13, :], rtmp, AX.X, ALU.add))
                link(dve.tensor_scalar(small[:, 14, :], small[:, 13, :], float(CAP), None, ALU.is_lt))
                link(dve.tensor_tensor(wsel[:, k, :], top8[:, :, k], small[:, 14, :], ALU.mult))
                link(dve.scalar_tensor_tensor(small[:, 13, :], idxf[:, :, k], float(CAP), small[:, 13, :], ALU.mult, ALU.add))
                link(dve.scalar_tensor_tensor(small[:, 15, :], small[:, 13, :], float(-SLOTS), small[:, 14, :], ALU.add, ALU.mult))
                link(dve.tensor_scalar(slot[:, k, :], small[:, 15, :], float(SLOTS), None, ALU.add))


def attention(nc, sem, v):
    psum, mx, nm, nmT, prob, attT = v["psum"], v["mx"], v["nm"], v["nmT"], v["prob"], v["attT"]
    q_stack, k_stack, v_stack = v["q_stack"], v["k_stack"], v["v_stack"]
    stack_in = [sem(f"stack_in{i}") for i in range(3)]
    ones_ok = sem("ones_ok")
    mbank_full = sem("mbank_full")
    mbank_free = sem("mbank_free")
    nm_step = sem("nm_step")
    bias_in = [sem(f"bias_in{h}") for h in range(2)]
    score_ok = sem("score_ok")
    exp_done = sem("exp_done")
    av_done = sem("av_done")
    evac_done = sem("evac_done")
    scattered = sem("scattered")

    SBANKS = 3
    LAG, EARLY = 3, 6
    units = [("unit", 0, w) for w in range(UNITS)]
    half = UNITS // 2
    ORDER = units[:LAG] + [("turn", -1, 1)] + units[LAG:half + LAG] + [("turn", 0, 0)] + units[half + LAG:]
    START = [u for u in ORDER if u[1] == 0]

    def number(k, use):
        return MBANK * k + (use - 1)

    def stream(G, off):
        return ([(G + 1, off + 1, use) for use in range(EARLY, MBANK)] + [(G + 2, off + 2, use) for use in range(EARLY)])

    def pe_use(pe, k, mod, num, what, fill=None):
        kind, back, w = what
        bank = 2 * (num[1] % 2)

        def begin():
            if num[0] is not None:
                pe.wait_ge(mbank_free, num[0])

        def piece(kh):
            def go():
                if kh == 0:
                    if fill is not None:
                        pe.wait_ge(stack_in[mod % 3], 16 * STACK_DMAS * fill)
                    begin()
                j, qt = w // KT, w % KT
                ins = pe.matmul(psum[:, bank + kh, :], q_stack[0:SROWS, mod % 3, j, P * qt:P * (qt + 1)],
                                k_stack[0:SROWS, mod % 3, j, N * kh:N * (kh + 1)], start=True, stop=True)
                if kh == QH - 1:
                    ins.then_inc(mbank_full, 1)
            return go

        def turn():
            begin()
            pe.wait_ge(nm_step, 4 * (k + back) + (2 * w + 2))
            src = nm[:, w, :, :, :].rearrange("p j s t -> p (j s t)")
            pe.matmul(psum[0:32, bank, 0:P], src, v["ident_b"][:, :], start=True, stop=True).then_inc(mbank_full, 1)

        return [(kind, turn)] if kind == "turn" else [(kind, piece(kh)) for kh in range(QH)]

    def dve_use(dve, k, num, what, first=False):
        kind, back, w = what
        bank = 2 * (num[1] % 2)
        dve.wait_ge(mbank_full, num[0] + 1)
        if kind == "turn":
            if not first:
                dve.wait_ge(bias_in[w], 16 * BIAS_DMAS * (k + back))
            dve.tensor_copy(nmT[:, w, :], psum[0:32, bank, 0:P]).then_inc(mbank_free, 1)
            return
        pair = psum[:, bank:bank + 2, :].rearrange("p b n -> p (b n)")
        dve.tensor_reduce(mx[:, w:w + 1], pair, AX.X, ALU.max).then_inc(mbank_free, 1)
        if w % half == half - 1:
            h = w // half
            m2 = mx[:, half * h:half * (h + 1)].rearrange("p (j t) -> p j t", j=2)
            dve.wait_ge(mbank_free, num[0] + 1)
            dve.tensor_scalar(nm[:, h, :, 0, :], m2, -1.0, None, ALU.mult).then_inc(nm_step, 1)
            dve.wait_ge(nm_step, 4 * k + (2 * h + 1))
            dve.scalar_tensor_tensor(nm[:, h, :, 1, :], m2, -1.0, nm[:, h, :, 0, :],
                                     ALU.mult, ALU.subtract).then_inc(nm_step, 1)

    def load(sp, G, buf):
        for st, dram, side in ((q_stack, v["q_parts"], 1), (k_stack, v["k_parts"], 0)):
            flat = dram.rearrange("g s (d j) t -> g s d (j t)", j=GH)
            for i, pair in enumerate(PAIRS):
                sp.dma_start(st[HD * i:HD * (i + 1), buf, :, :].rearrange("p j t -> p (j t)"),
                             flat[bass.ds(G, 1), pair[side], :, :].rearrange("g d n -> (g d) n")).then_inc(stack_in[buf], 16)
        vw = v["v_wide"].rearrange("g (t p) n -> g p t n", p=P)
        sp.dma_start(v_stack[:, buf, :, :, :].rearrange("p t j d -> p t (j d)"),
                     vw[bass.ds(G, 1), :, :, :].rearrange("g p t n -> (g p) t n")).then_inc(stack_in[buf], 16)

    def bias(sp, G, buf):
        for h in range(2):
            use = ORDER.index(("turn", 0, 0)) if h == 0 else MBANK + ORDER.index(("turn", -1, 1))
            sp.wait_ge(mbank_free, number(G, use) + 1)
            for j in range(2):
                for s in range(2):
                    r = (2 * j + s) * KT
                    sp.dma_start(q_stack[SROWS + s:SROWS + s + 1, buf, 2 * h + j, :].rearrange("a (t c) -> a t c", t=KT),
                                 nmT[r:r + KT, h, :]).then_inc(bias_in[h], 16)

    def pe_group(pe, G, off, it, peel):
        buf = off % 3
        uses = []
        if peel != "last":
            for k, mod, use in stream(G, off):
                fill = it + (mod // 3 + 1) if use == 0 else None
                uses += pe_use(pe, k, mod, (number(k, use - 1), (use + 1) % 2), ORDER[use], fill)
        for h in range(2):
            pe.wait_ge(bias_in[h], 16 * BIAS_DMAS * (G + 1))
        for s in range(STEPS):
            qh, kt = s // KT, s % KT
            for j in range(GH):
                u = GH * s + j
                if not (peel == "first" and u < SBANKS):
                    pe.wait_ge(exp_done, GH * STEPS * G + (u - SBANKS + 1))
                pe.matmul(psum[:, 4 + (off + u) % SBANKS, :], k_stack[0:KROWS, buf, j, P * kt:P * (kt + 1)],
                          q_stack[0:KROWS, buf, j, N * qh:N * (qh + 1)], start=True, stop=True).then_inc(score_ok, 1)
                if uses:
                    uses.pop(0)[1]()
                if uses and uses[0][0] == "turn":
                    uses.pop(0)[1]()
                if j == 1 and not (peel == "first" and s == 0):
                    av_step(pe, G, off, s - 1, peel)

    def av_step(pe, G, off, s, peel):
        buf = (off + s // STEPS) % 3
        qh, kt = s % STEPS // KT, s % KT
        pe.wait_ge(exp_done, GH * STEPS * G + GH * (s + 1))
        if kt == 0 and not (peel == "first" and qh == 0):
            pe.wait_ge(evac_done, QH * G + qh)
        for j in range(GH):
            last = pe.matmul(psum[32 * j:32 * (j + 1), 4 + SBANKS, :], v_stack[:, buf, kt, j, :],
                             prob[:, (off * STEPS + s) % 3, j, :], start=(kt == 0), stop=(kt == KT - 1))
        last.then_inc(av_done, 1)

    def act_group(act, G, off, it, peel):
        for s in range(STEPS):
            for j in range(GH):
                u = GH * s + j
                act.wait_ge(score_ok, GH * STEPS * G + (u + 1))
                if j == 0 and not (peel == "first" and s < 3):
                    act.wait_ge(av_done, STEPS * G + (s - 2))
                act.activation(prob[:, (off * STEPS + s) % 3, j, :], psum[:, 4 + (off + u) % SBANKS, :], ACT.Exp,
                               scale=SCALE).then_inc(exp_done, 1)
                if j == 1 and s == 0 and peel != "first":
                    evac(act, G - 1, 1)
                if j == 1 and s == KT:
                    evac(act, G, 0)

    def evac(act, G, qh):
        act.wait_ge(av_done, STEPS * G + KT * (qh + 1))
        act.copy(attT[:, bass.ds(G, 1), N * qh:N * (qh + 1)], psum[:, 4 + SBANKS:5 + SBANKS, :]).then_inc(evac_done, 1)

    def groups(eng, run):
        run(0, 0, 0, "first")
        with eng.Fori(0, (GROUPS - 2) // 3) as it:
            for off in range(1, 4):
                run(it * 3 + off, off, it, None)
        run(GROUPS - 1, (GROUPS - 1) % 3, (GROUPS - 1) // 3, "last")

    with nc.Block() as block:
        @block.sync
        def _(sp):
            for G in range(3):
                load(sp, G, G)
            bias(sp, 0, 0)
            bias(sp, 1, 1)
            with sp.Fori(0, (GROUPS - 2) // 3) as it:
                for off in range(1, 4):
                    G = it * 3 + off
                    sp.wait_ge(av_done, STEPS * G + 1)
                    load(sp, (G + 2) % GROUPS, (off + 2) % 3)
                    bias(sp, G + 1, (off + 1) % 3)

        @block.gpsimd
        def _(pool):
            for t in range(TILES):
                for k in range(TOPK):
                    pool.indirect_dma_start(out=v["slot_x"],
                                            out_offset=bass.IndirectOffsetOnAxis(ap=v["slot"][:, k, t:t + 1], axis=0),
                                            in_=v["xf"][:, t, :], in_offset=None, bounds_check=SLOTS - 1,
                                            oob_is_err=False).then_inc(scattered, 16)
            pool.wait_ge(scattered, 16 * TOPK * TILES)

        @block.scalar
        def _(act):
            groups(act, lambda *a: act_group(act, *a))
            evac(act, GROUPS - 1, 1)

        @block.tensor
        def _(pe):
            pe.wait_ge(ones_ok, 3)
            pe.wait_ge(stack_in[0], 16 * STACK_DMAS)
            for n, what in enumerate(START):
                for _, piece in pe_use(pe, 0, 0, (n - 1 if n >= 2 else None, n), what):
                    piece()
            for use in range(EARLY):
                for _, piece in pe_use(pe, 1, 1, (number(1, use - 1), use + 1), ORDER[use], 1 if use == 0 else None):
                    piece()
            groups(pe, lambda *a: pe_group(pe, *a))
            av_step(pe, GROUPS - 1, (GROUPS - 1) % 3, STEPS - 1, "last")

        @block.vector
        def _(dve):
            for buf in range(3):
                dve.memset(k_stack[SROWS:KROWS, buf, :, :], 1.0).then_inc(ones_ok, 1)
            for n, what in enumerate(START):
                dve_use(dve, 0, (n, n), what, True)
            for use in range(EARLY):
                dve_use(dve, 1, (number(1, use), use + 1), ORDER[use], True)

            def run(G, off, it, peel):
                if peel != "last":
                    for k, mod, use in stream(G, off):
                        dve_use(dve, k, (number(k, use), use + 1), ORDER[use])

            groups(dve, run)


def feed_forward(nc, sem, v):
    psum, attT, ident, xfT, res, slot = v["psum"], v["attT"], v["ident"], v["xfT"], v["res"], v["slot"]
    boT, wo, wsel, sgate, sw_gu, sw_dn = v["boT"], v["wo"], v["wsel"], v["sgate"], v["sw_gu"], v["sw_dn"]
    up_in = [sem(f"up_in{i}") for i in range(4)]
    down_in = [sem(f"down_in{i}") for i in range(4)]
    bufT_ps = sem("bufT_ps")
    bufT_ok = sem("bufT_ok")
    gu_ok = sem("gu_ok")
    silu_ok = sem("silu_ok")
    hid_ok = sem("hid_ok")
    hidT_ps = sem("hidT_ps")
    hidT_ok = sem("hidT_ok")
    y_ps = sem("y_ps")
    y_ok = sem("y_ok")
    y_out = [sem(f"y_out{i}") for i in range(2)]
    sums_in = sem("sums_in")
    recip_ok = sem("recip_ok")
    recips_in = sem("recips_in")
    den_ok = sem("den_ok")
    spread_ok = sem("spread_ok")
    norm_ok = sem("norm_ok")
    gathered = [sem(f"gathered{i}") for i in range(3)]
    ro_ps = sem("ro_ps")
    ro_ok = sem("ro_ok")
    att_ps = sem("att_ps")
    att_ok = sem("att_ok")
    sgu_ps = sem("sgu_ps")
    ssilu_ok = sem("ssilu_ok")
    shid_ok = sem("shid_ok")
    sh_ps = sem("sh_ps")
    sh_ok = sem("sh_ok")
    mix_step = sem("mix_step")
    tile_ok = sem("tile_ok")
    stored = sem("stored")

    qm, km = v["q_mem"], v["k_mem"]
    per = HID + HC * 2 * FF + 2 * HID
    xb = [qm[:, per * i:per * i + HID] for i in range(4)]
    wgu = [qm[:, per * i + HID:per * i + HID + HC * 2 * FF].rearrange("p (c s f) -> p c s f", c=HC, s=2) for i in range(4)]
    wdn = [qm[0:FHALF, per * (i + 1) - 2 * HID:per * (i + 1)].rearrange("p (c h) -> p c h", c=2) for i in range(4)]
    o = [0]

    def take(n):
        o[0] += n
        return km[:, o[0] - n:o[0]]

    xbT = [take(HID).rearrange("p (c t) -> p c t", c=HC) for _ in range(2)]
    silu = [take(FF) for _ in range(2)]
    hid = [take(FF) for _ in range(2)]
    hidT = [take(2 * P)[0:FHALF, :].rearrange("p (c t) -> p c t", c=2) for _ in range(2)]
    ysb = [take(HID) for _ in range(2)]
    den = [take(SEQ) for _ in range(2)]
    rc = take(GROUPS * SEQ // 32)
    ssilu = [take(N)[0:FCH[0], :] for _ in range(2)]
    ET = EXPERTS // 4
    NF = len(FCH)
    shid = v["prob"][0:FCH[0], :, :, :].rearrange("p a b n -> p (a b) n")
    rows = [qm[:, 1024 * i:1024 * (i + 1)].rearrange("p (k h) -> p k h", k=TOPK) for i in range(3)]
    ro = den[0][:, 0:N]
    out_v = v["out"].rearrange("b s h -> (b s) h").rearrange("(t p) h -> p t h", p=P)

    def turns(eng, run):
        run(0, "first")
        with eng.Fori(1, ET - 1) as it:
            run(it, None)
        run(ET - 1, "last")

    def tokens_T(pe, e, r, lap):
        pe.wait_ge(up_in[r], 16 * 3 * (lap + 1))
        if not (isinstance(e, int) and e < 2):
            pe.wait_ge(bufT_ok, e - 1)
        for c in range(HC):
            last = pe.transpose(psum[:, r % 2, P * c:P * (c + 1)], xb[r][:, P * c:P * (c + 1)], ident[:, :])
        last.then_inc(bufT_ps, 1)

    def gate_up(pe, e, r):
        pe.wait_ge(bufT_ok, e + 1)
        if not (isinstance(e, int) and e < 2):
            pe.wait_ge(hid_ok, e - 1)
        for c in range(HC):
            last = pe.matmul(psum[:, 2 + r % 2, 0:2 * FF], xbT[r % 2][:, c, :],
                             wgu[r][:, c, :, :].rearrange("p s f -> p (s f)"), start=(c == 0), stop=(c == HC - 1))
        last.then_inc(gu_ok, 1)

    def hidden_T(pe, e, r):
        pe.wait_ge(hid_ok, e + 1)
        if not (isinstance(e, int) and e < 2):
            pe.wait_ge(hidT_ok, e - 1)
        for c in range(2):
            last = pe.transpose(psum[0:FHALF, 4 + r % 2, P * c:P * (c + 1)],
                                hid[r % 2][:, FHALF * c:FHALF * (c + 1)], ident[:, :])
        last.then_inc(hidT_ps, 1)

    def down(pe, e, r, lap):
        pe.wait_ge(down_in[r], 16 * (lap + 1))
        pe.wait_ge(hidT_ok, e + 1)
        if not (isinstance(e, int) and e < 2):
            pe.wait_ge(y_ok, e - 1)
        for c in range(2):
            last = pe.matmul(psum[:, 6 + r % 2, 0:HID], hidT[r % 2][:, c, :], wdn[r][:, c, :],
                             start=(c == 0), stop=(c == 1))
        last.then_inc(y_ps, 1)

    def shared_gate_up(pe, b):
        for f in range(NF):
            i = NF * b + f
            if i >= 2:
                pe.wait_ge(shid_ok, i - 1)
            for s in range(2):
                for c in range(HC):
                    last = pe.matmul(psum[0:FCH[f], 2 * (i % 2) + s, :], sw_gu[:, c, s, FOFF[f]:FOFF[f] + FCH[f]],
                                     xfT[:, c, N * b:N * (b + 1)], start=(c == 0), stop=(c == HC - 1))
            last.then_inc(sgu_ps, 1)

    def shared_tail(pe, b):
        if b:
            pe.wait_ge(ro_ok, b)
        for g in range(HG):
            last = pe.matmul(psum[:, 4, :], boT[:, g, :],
                             attT[:, HG * (b // 2) + g, N * (b % 2):N * (b % 2 + 1)], start=(g == 0), stop=(g == HG - 1))
        last.then_inc(ro_ps, 1)
        pe.wait_ge(shid_ok, NF * (b + 1))
        for i in range(2):
            n = 2 * b + i
            if n >= 2:
                pe.wait_ge(sh_ok, n - 1)
            for t in range(2):
                tt = 2 * i + t
                for f in range(NF):
                    last = pe.matmul(psum[:, 6 + i, HID * t:HID * (t + 1)],
                                     shid[0:FCH[f], NF * (b % 2) + f, P * tt:P * (tt + 1)], sw_dn[0:FCH[f], f, :],
                                     start=(f == 0), stop=(f == NF - 1))
            last.then_inc(sh_ps, 1)
            if n:
                pe.wait_ge(att_ok, n)
            if i == 0:
                pe.wait_ge(ro_ok, b + 1)
            for t in range(2):
                tt = 2 * i + t
                last = pe.matmul(psum[:, 5, HID * t:HID * (t + 1)], ro[:, P * tt:P * (tt + 1)], wo[:, :],
                                 start=True, stop=True)
            last.then_inc(att_ps, 1)

    with nc.Block() as block:
        @block.sync
        def _(sp):
            xv = v["slot_x"].rearrange("(e p) h -> e p h", p=P)
            gv = v["w_gate"].rearrange("e (c p) f -> e p c f", p=P)
            uv = v["w_up"].rearrange("e (c p) f -> e p c f", p=P)
            dv = v["w_down"].rearrange("e (c p) h -> e p c h", p=FHALF)
            yv = v["slot_y"][0:SLOTS, :].rearrange("(e p) h -> e p h", p=P)

            def load_up(e, r):
                sp.dma_start(xb[r], xv[bass.ds(e, 1), :, :].rearrange("a p h -> (a p) h")).then_inc(up_in[r], 16)
                for s, w in enumerate((gv, uv)):
                    sp.dma_start(wgu[r][:, :, s, :], w[bass.ds(e, 1), :, :, :]
                                 .rearrange("a p c f -> (a p) c f")).then_inc(up_in[r], 16)

            def load_down(e, r):
                sp.dma_start(wdn[r], dv[bass.ds(e, 1), :, :, :].rearrange("a p c h -> (a p) c h")).then_inc(down_in[r], 16)

            def store(e, r):
                sp.wait_ge(y_ok, e + 1)
                sp.dma_start(yv[bass.ds(e, 1), :, :].rearrange("a p h -> (a p) h"), ysb[r % 2]).then_inc(y_out[r % 2], 16)

            flat = attT.rearrange("p g t -> p (g t)")
            for j in range(GH):
                sp.dma_start(rc[32 * j:32 * (j + 1), :],
                             flat[32 * j + HD:32 * j + HD + 1, :].rearrange("a (p n) -> a p n", p=32)).then_inc(sums_in, 16)
            for r in range(4):
                load_up(r, r)
                load_down(r, r)
            sp.wait_ge(recip_ok, 1)
            for j in range(GH):
                sp.dma_start(flat[32 * j + HD:32 * j + HD + 1, :].rearrange("a (p n) -> a p n", p=32),
                             rc[32 * j:32 * (j + 1), :]).then_inc(recips_in, 16)

            def run(it, peel):
                for r in range(4):
                    e = it * 4 + r
                    if peel != "last":
                        sp.wait_ge(gu_ok, e + 1)
                        load_up(e + 4, r)
                    if not (peel == "first" and r < 2):
                        store(e - 2, (r - 2) % 4)
                        if not (peel == "last" and r >= 2):
                            load_down(e + 2, (r + 2) % 4)

            turns(sp, run)
            store(EXPERTS - 2, 2)
            store(EXPERTS - 1, 3)
            for t in range(TILES):
                sp.wait_ge(tile_ok, t + 1)
                sp.dma_start(out_v[:, t, :], res[:, t, :]).then_inc(stored, 16)
            sp.wait_ge(stored, 16 * TILES)

        @block.gpsimd
        def _(pool):
            pool.wait_ge(recips_in, 16 * GH)
            for g in range(GROUPS):
                if g:
                    pool.wait_ge(spread_ok, g)
                pool.tensor_copy(den[0], attT[:, g, :]).then_inc(den_ok, 1)
                pool.wait_ge(spread_ok, g + 1)
                pool.tensor_tensor(attT[:, g, :], attT[:, g, :], den[1], ALU.mult).then_inc(norm_ok, 1)
            for i in range(2):
                pool.wait_ge(y_out[i], 16 * EXPERTS // 2)
            for t in range(TILES):
                if t >= 3:
                    pool.wait_ge(tile_ok, t - 2)
                for k in range(TOPK):
                    pool.indirect_dma_start(out=rows[t % 3][:, k, :], out_offset=None, in_=v["slot_y"],
                                            in_offset=bass.IndirectOffsetOnAxis(ap=slot[:, k, t:t + 1], axis=0),
                                            bounds_check=SLOTS, oob_is_err=False).then_inc(gathered[t % 3], 16)

        @block.scalar
        def _(act):
            def tokens(e, r):
                act.wait_ge(bufT_ps, e + 1)
                act.copy(xbT[r % 2].rearrange("p c t -> p (c t)"), psum[:, r % 2, 0:HID]).then_inc(bufT_ok, 1)

            def out_rows(e, r, stores):
                act.wait_ge(y_ps, e + 1)
                if stores is not None:
                    act.wait_ge(y_out[r % 2], 16 * stores)
                act.copy(ysb[r % 2], psum[:, 6 + r % 2, 0:HID]).then_inc(y_ok, 1)

            def run(it, peel):
                for r in range(4):
                    e = it * 4 + r
                    act.wait_ge(gu_ok, e + 1)
                    act.activation(silu[r % 2], psum[:, 2 + r % 2, 0:FF], ACT.Silu).then_inc(silu_ok, 1)
                    if not (peel == "last" and r == 3):
                        tokens(e + 1, r + 1)
                    if not (peel == "first" and r < 2):
                        out_rows(e - 2, r, None if peel == "first" else it * 2 + (r // 2 - 1))

            def shared_silu(b):
                for f in range(NF):
                    i = NF * b + f
                    act.wait_ge(sgu_ps, i + 1)
                    if i >= 2:
                        act.wait_ge(shid_ok, i - 1)
                    act.activation(ssilu[i % 2][0:FCH[f], :], psum[0:FCH[f], 2 * (i % 2), :], ACT.Silu).then_inc(ssilu_ok, 1)

            def out_resonance(b):
                act.wait_ge(ro_ps, b + 1)
                if b:
                    act.wait_ge(att_ps, 2 * b)
                act.copy(ro, psum[:, 4, :]).then_inc(ro_ok, 1)

            shared_silu(0)
            tokens(0, 0)
            turns(act, run)
            out_rows(EXPERTS - 2, 0, EXPERTS // 2 - 1)
            out_rows(EXPERTS - 1, 1, EXPERTS // 2 - 1)
            for b in range(1, BLK):
                shared_silu(b)
                out_resonance(b - 1)
            out_resonance(BLK - 1)

        @block.tensor
        def _(pe):
            def run(it, peel):
                for r in range(4):
                    e = it * 4 + r
                    gate_up(pe, e, r)
                    if not (peel == "last" and r == 3):
                        tokens_T(pe, e + 1, (r + 1) % 4, it + (r + 1) // 4)
                    if not (peel == "first" and r < 1):
                        hidden_T(pe, e - 1, (r - 1) % 4)
                    if not (peel == "first" and r < 2):
                        down(pe, e - 2, (r - 2) % 4, it + (r - 2) // 4)

            shared_gate_up(pe, 0)
            pe.wait_ge(shid_ok, NF)
            tokens_T(pe, 0, 0, 0)
            turns(pe, run)
            hidden_T(pe, EXPERTS - 1, 3)
            down(pe, EXPERTS - 2, 2, ET - 1)
            down(pe, EXPERTS - 1, 3, ET - 1)
            for b in range(1, BLK):
                shared_gate_up(pe, b)
                if b == 1:
                    pe.wait_ge(norm_ok, GROUPS)
                    pe.wait_ge(y_ok, EXPERTS)
                shared_tail(pe, b - 1)
            shared_tail(pe, BLK - 1)

        @block.vector
        def _(dve):
            steps = [0]

            def link(ins):
                steps[0] += 1
                ins.then_inc(mix_step, 1)
                dve.wait_ge(mix_step, steps[0])

            def shared_hidden(b):
                for f in range(NF):
                    i = NF * b + f
                    n = FCH[f]
                    dve.wait_ge(ssilu_ok, i + 1)
                    if b >= 2:
                        dve.wait_ge(sh_ps, 2 * (b - 1))
                    dve.tensor_tensor(shid[0:n, NF * (b % 2) + f, :], ssilu[i % 2][0:n, :],
                                      psum[0:n, 2 * (i % 2) + 1, :], ALU.mult).then_inc(shid_ok, 1)

            def hidden_out(e, r, drained):
                dve.wait_ge(hidT_ps, e + 1)
                if drained:
                    dve.wait_ge(y_ps, e - 1)
                dve.tensor_copy(hidT[r % 2].rearrange("p c t -> p (c t)"), psum[0:FHALF, 4 + r % 2, 0:2 * P]).then_inc(hidT_ok, 1)

            def run(it, peel):
                for r in range(4):
                    e = it * 4 + r
                    if r == 2:
                        dve.wait_ge(den_ok, it + 1)
                    dve.wait_ge(silu_ok, e + 1)
                    dve.tensor_tensor(hid[r % 2], silu[r % 2], psum[:, 2 + r % 2, FF:2 * FF], ALU.mult).then_inc(hid_ok, 1)
                    if r == 2:
                        dve.stream_shuffle(den[1], den[0], [HD] * 32).then_inc(spread_ok, 1)
                    if not (peel == "first" and r < 1):
                        hidden_out(e - 1, (r - 1) % 4, not (peel == "first" and r < 3))

            def mix(b):
                for i in range(2):
                    n = 2 * b + i
                    dve.wait_ge(sh_ps, n + 1)
                    for t in range(2):
                        tile = 2 * n + t
                        last = dve.scalar_tensor_tensor(res[:, tile, :], psum[:, 6 + i, HID * t:HID * (t + 1)],
                                                        sgate[:, tile:tile + 1], res[:, tile, :], ALU.mult, ALU.add)
                    last.then_inc(sh_ok, 1)
                    dve.wait_ge(sh_ok, n + 1)
                    r2 = res[:, 2 * n:2 * n + 2, :].rearrange("p t h -> p (t h)")
                    dve.wait_ge(att_ps, n + 1)
                    dve.tensor_tensor(r2, r2, psum[:, 5, :], ALU.add).then_inc(att_ok, 1)
                    dve.wait_ge(att_ok, n + 1)
                    for t in range(2):
                        tile = 2 * n + t
                        dve.wait_ge(gathered[tile % 3], 16 * TOPK * (tile // 3 + 1))
                        for k in range(TOPK):
                            ins = dve.scalar_tensor_tensor(res[:, tile, :], rows[tile % 3][:, k, :], wsel[:, k, tile:tile + 1],
                                                           res[:, tile, :], ALU.mult, ALU.add)
                            if k == TOPK - 1:
                                ins.then_inc(tile_ok, 1)
                            else:
                                link(ins)

            shared_hidden(0)
            dve.wait_ge(sums_in, 16 * GH)
            dve.reciprocal(rc, rc).then_inc(recip_ok, 1)
            turns(dve, run)
            hidden_out(EXPERTS - 1, 3, True)
            for b in range(1, BLK):
                shared_hidden(b)
                mix(b - 1)
            mix(BLK - 1)




_INS = ['L0_attn_hidden_states', 'L0_attn_basis_q', 'L0_attn_phase_q', 'L0_attn_amp_q', 'L0_attn_basis_k',
        'L0_attn_phase_k', 'L0_attn_amp_k', 'L0_attn_basis_v', 'L0_attn_phase_v', 'L0_attn_amp_v',
        'L0_attn_basis_o', 'L0_attn_phase_o', 'L0_attn_amp_o', 'L0_ffn_w_norm', 'L0_ffn_w_router', 'L0_ffn_w_gate',
        'L0_ffn_w_up', 'L0_ffn_w_down', 'L0_ffn_sw_gate', 'L0_ffn_sw_up', 'L0_ffn_sw_down', 'L0_ffn_w_shared_gate']
_OUTS = [((2, 1024, 256), 'float32')]


def kernel(**inputs):
    import numpy as _np
    import concourse.bacc as _bacc
    from concourse import mybir as _mybir
    from concourse.bass_utils import run_bass_kernel_spmd as _run

    nc = _bacc.Bacc("TRN2", target_bir_lowering=False, num_devices=1)
    arrays, args = {}, []
    for name in _INS:
        a = _np.ascontiguousarray(inputs[name])
        arrays[f"in_{name}_dram"] = a
        args.append(nc.dram_tensor(f"in_{name}_dram", a.shape, _mybir.dt.from_np(a.dtype), kind="ExternalInput").ap())
    for i, (shape, dtype) in enumerate(_OUTS):
        dt = _mybir.dt.from_np(_np.dtype(dtype))
        args.append(nc.dram_tensor(f"out_{i}_dram", shape, dt, kind="ExternalOutput").ap())
    build(nc, *args)
    r = _run(nc, [arrays], core_ids=[0])
    got = tuple(r.results[0][f"out_{i}_dram"] for i in range(len(_OUTS)))
    return got[0]
```

```python
from contextlib import ExitStack

import concourse.bass as bass
from concourse import mybir

FP32 = mybir.dt.float32
BF16 = mybir.dt.bfloat16
U32 = mybir.dt.uint32
ALU = mybir.AluOpType
ACT = mybir.ActivationFunctionType
AX = mybir.AxisListType

P = 128
BATCH, SEQ, HID = 2, 1024, 256
TOK = BATCH * SEQ
TILES = TOK // P
HC = HID // P
HEADS, HD, HARM = 16, 16, 64
GH = 4
HG = HEADS // GH
GROUPS = BATCH * HG
KT = SEQ // P
N = 512
QH = SEQ // N
STEPS = QH * KT
EXPERTS, TOPK, FF, CAP = 32, 4, 176, 128
SLOTS = EXPERTS * CAP
FS = 704
FCH = [118] * 5 + [114]
FOFF = [118 * i for i in range(6)]
FHALF = FF // 2
BLK = TOK // N
TPB = N // P
LN_EPS, RMS_EPS = 1e-5, 1e-6
SCALE = HD ** -0.5
TWO_PI_HI, TWO_PI_LO = 6.28125, 0.0019353071795864769
INV_TWO_PI = 0.15915494309189535
ROUND = 1.5 * 2.0 ** 23
PI = 3.1415925
PAIRS = [(0, 0), (0, 1), (0, 2), (1, 0), (1, 1), (2, 0)]
SROWS = HD * len(PAIRS)
KROWS = SROWS + 2
Q_RUNS = [(0, 0, 3), (3, 0, 2), (5, 0, 1)]
K_RUNS = [(0, 0, 1), (1, 0, 1), (2, 0, 1), (3, 1, 1), (4, 1, 1), (5, 2, 1)]
STACK_DMAS = len(Q_RUNS) + len(K_RUNS)
BIAS_DMAS = P // 32
UNITS = GH * KT
EARLY = 7


def build(nc, x, bq, pq, aq, bk, pk, ak, bv, pv, av, bo, po, ao, w_norm, w_router, w_gate, w_up,
          w_down, sw_gate, sw_up, sw_down, w_sg, out):
    ctx = ExitStack()
    with ctx:
        def sb(name, shape, dt=FP32):
            return ctx.enter_context(nc.sbuf_tensor(name, shape, dt))

        def sem(name):
            return ctx.enter_context(nc.semaphore(name))

        q_parts = nc.dram_tensor("q_parts", (GROUPS, 3, HD * GH, SEQ), BF16).ap()
        k_parts = nc.dram_tensor("k_parts", (GROUPS, 3, HD * GH, SEQ), BF16).ap()
        v_wide = nc.dram_tensor("v_wide", (GROUPS, SEQ, GH * 32), FP32).ap()
        slot_x = nc.dram_tensor("slot_x", (SLOTS, HID), FP32).ap()
        slot_y = nc.dram_tensor("slot_y", (SLOTS + 1, HID), FP32).ap()

        res = sb("res", [P, TILES, HID])
        wide = sb("wide", [P, GROUPS * SEQ])
        xn = wide[:, 0:TILES * HID].rearrange("p (t h) -> p t h", t=TILES)
        xnT = wide[:, TILES * HID:2 * TILES * HID].rearrange("p (c t) -> p c t", c=HC)
        attT = wide[:, :].rearrange("p (g t) -> p g t", g=GROUPS)
        xf = sb("xf", [P, TILES, HID])
        xfT = sb("xfT", [P, HC, TOK])
        q_mem = sb("q_mem", [P, 3 * GH * SEQ // 2])
        k_mem = sb("k_mem", [P, 3 * GH * SEQ // 2])
        q_stack = q_mem[:, :].bitcast(BF16).rearrange("p (b j t) -> p b j t", b=3, j=GH)
        k_stack = k_mem[:, :].bitcast(BF16).rearrange("p (b j t) -> p b j t", b=3, j=GH)
        v_stack = sb("v_stack", [P, 3, KT, GH, 32])
        prob = sb("prob", [P, 3, GH, N])
        sw_gu = sb("sw_gu", [P, HC, 2, FS])
        sw_dn = sb("sw_dn", [FCH[0], len(FCH), HID])
        ident = sb("ident", [P, P])
        before = sb("before", [P, P], BF16)
        ones_b = sb("ones_b", [P, P], BF16)
        bT = sb("bT", [P, 2, HC, P])
        wq = sb("wq", [P, HID])
        wk = sb("wk", [P, HID])
        wv = sb("wv", [P, HID])
        wo = sb("wo", [P, HID])
        boT = sb("boT", [P, HG, P])
        wr = sb("wr", [P, HC, EXPERTS + 1])
        rt = sb("rt", [P, 2, N])
        rvo = sb("rvo", [P, N])
        rem = sb("rem", [P, 2, N])
        mx = sb("mx", [P, UNITS])
        nm = sb("nm", [P, 2, 2, 2, KT], BF16)
        nmT = sb("nmT", [P, 2, 32], BF16)
        slot = sb("slot", [P, TOPK, TILES], U32)
        wsel = sb("wsel", [P, TOPK, TILES])
        sgate = sb("sgate", [P, TILES])
        small = sb("small", [P, 13, TILES])
        place = sb("place", [P, 2, TOPK, TILES])
        bn = sb("bn", [P, TILES, 6])
        mv = sb("mv", [P, TILES, 2])
        top8 = sb("top8", [P, TILES, 8])
        idx8 = sb("idx8", [P, TILES, 8], U32)
        idxf = sb("idxf", [P, TILES, 8], BF16)
        iota_e = sb("iota_e", [P, EXPERTS], BF16)
        eps = sb("eps", [P, 2])

        psum = ctx.enter_context(nc.psum_tensor("psum", [P, 8, N], FP32))

        probf = prob[:, :, :, :].rearrange("p a b c -> p (a b c)")

        def holo(i):
            return probf[:, N * i:N * (i + 1)].rearrange("p (c m h) -> p c m h", c=2, m=4)

        phase, amp, turn, ang, wmat = (holo(i) for i in range(5))
        bo_pad = probf[:, 5 * N:6 * N].rearrange("p (g j d) -> p g j d", g=HG, j=GH)
        basis = probf[:, 6 * N:7 * N].rearrange("p (s h) -> p s h", s=2)
        zeros = probf[:, 7 * N:9 * N]
        wn = probf[:, 9 * N:9 * N + HID]
        parts = [(q_mem, k_mem)[i // 2][:, :].bitcast(BF16)[:, 2 * GH * SEQ + 3 * N * (i % 2):
                                                            2 * GH * SEQ + 3 * N * (i % 2 + 1)]
                 .rearrange("p (s t) -> p s t", s=3) for i in range(4)]
        v_stage = v_stack[:, 1:3, :, :, :].rearrange("p b k j d -> p b (k j d)").rearrange(
            "p b (t h d) -> p b t h d", t=2, h=HEADS)
        rm = wide[:, TILES * HID:2 * TILES * HID]
        onehot = rm[:, 0:1024].bitcast(BF16).rearrange("p (k t e) -> p k t e", k=TOPK, t=TILES)

        def routing(i):
            return rm[:, 1024 + N * i:1024 + N * (i + 1)].rearrange("p (t e) -> p t e", t=TILES)

        probs, rtmp, pos, cum0, cum1 = (routing(i) for i in range(5))
        mask_b = rm[:, 1024 + 5 * N:1024 + 5 * N + N // 2].bitcast(BF16).rearrange("p (t e) -> p t e", t=TILES)

        sgu_ps = sem("sgu_ps")
        attend(nc, sem, locals())
        feed_forward(nc, sem, locals())


def schedule():
    plan = [("bases",), ("xT", 0, 0), ("xT", 0, 1), ("sin",), ("res_qk", 0), ("root",), ("res_v", 0),
            ("weights",), ("out_basis",), ("qk", 0), ("qk", 1), ("v", 0), ("qk", 2), ("qk", 3), ("v", 1), ("xT", 1, 0),
            ("xT", 1, 1), ("res_qk", 1), ("res_v", 1), ("qk", 4), ("qk", 5), ("v", 2), ("qk", 6), ("load", 0), ("qk", 7), ("v", 3),
            ("low", 7), ("load", 1), ("load_v", 0),
            ("xT", 2, 0), ("square", 0), ("xT", 2, 1), ("square", 1), ("square", 2), ("square", 3), ("rms",),
            ("res_qk", 2), ("res_v", 2), 1, ("xT", 3, 0), 1, ("xT", 3, 1), 1, ("v", 4), 1, ("v", 5), 1, ("res_qk", 3), 1,
            ("res_v", 3), 2, ("qk", 8), 1, ("qk", 9), 1, ("xfT", 0, 0), 1, ("xfT", 0, 1), 1, ("xfT", 1, 0), 1,
            ("xfT", 1, 1), 2, ("logits", 0), 1, ("logits", 1), ("v", 6), 1, ("xfT", 2, 0), 2, ("xfT", 2, 1), 1,
            ("logits", 2), ("xfT", 3, 0), 2, ("xfT", 3, 1), 1, ("logits", 3), 2, ("soft1",), ("qk", 10), 1, ("v", 7), 1, ("soft2",), ("qk", 11), 1,
            ("qk", 12), 1, ("soft3",), 2, ("qk", 13), 1, ("soft4",), ("qk", 14), 2, ("soft5",), ("qk", 15), ("low", 15),
            3, ("count", 0), ("count", 1), 2]
    out, at = [], 0
    for e in plan:
        if not isinstance(e, int):
            out.append(e)
            continue
        for _ in range(e):
            if at in (UNITS // 2, UNITS):
                out.append(("bias", at // UNITS))
            out.append(("use", at))
            at += 1
    assert at == UNITS + EARLY
    return out


JOBS = ("bases", "xT", "weights", "out_basis", "res_qk", "qk", "res_v", "v", "xfT", "logits", "count")


def shared_bank(b, f):
    return 2 * (0, 1, 2, 3, 2, 3)[f] if b == 0 else 2 * (f % 2)


def gate_up_piece(pe, psum, sw_gu, xfT, b, f, s, c, lo=0, n=N):
    return pe.matmul(psum[0:FCH[f], shared_bank(b, f) + s, lo:lo + n], sw_gu[:, c, s, FOFF[f]:FOFF[f] + FCH[f]],
                     xfT[:, c, N * b + lo:N * b + lo + n], start=(c == 0), stop=(c == HC - 1))


def attend(nc, sem, v):
    names = ("x res xn xnT attT xf xfT q_stack k_stack v_stack prob ident before ones_b bT wq wk wv wo "
             "boT wr rt rvo rem mx nm nmT slot wsel sgate small place bn mv top8 idx8 idxf iota_e eps psum phase amp "
             "turn ang wmat bo_pad basis zeros wn parts v_stage onehot probs rtmp pos cum0 cum1 mask_b slot_x slot_y "
             "v_wide q_parts k_parts")
    (x, res, xn, xnT, attT, xf, xfT, q_stack, k_stack, v_stack, prob, ident, before, ones_b, bT, wq, wk,
     wv, wo, boT, wr, rt, rvo, rem, mx, nm, nmT, slot, wsel, sgate, small, place, bn, mv, top8, idx8, idxf, iota_e, eps,
     psum, phase, amp, turn, ang, wmat, bo_pad, basis, zeros, wn, parts, v_stage, onehot, probs, rtmp, pos, cum0, cum1,
     mask_b, slot_x, slot_y, v_wide, q_parts, k_parts) = (v[n] for n in names.split())

    x_in = [sem(f"x_in{i}") for i in range(BLK)]
    phase_in = sem("phase_in")
    amp_in = sem("amp_in")
    basis_in = sem("basis_in")
    vec_in = sem("vec_in")
    late_in = sem("late_in")
    zero_out = sem("zero_out")
    pool_step = sem("pool_step")
    const_ok = sem("const_ok")
    dve_step = sem("dve_step")
    var_ok = sem("var_ok")
    sqrt_ok = sem("sqrt_ok")
    xn_ok = sem("xn_ok")
    ms_ok = sem("ms_ok")
    rms_ok = sem("rms_ok")
    xf_ok = sem("xf_ok")
    xn_free = sem("xn_free")
    ang_ok = sem("ang_ok")
    sin_ok = sem("sin_ok")
    wmat_ok = sem("wmat_ok")
    job_full = sem("job_full")
    job_free = sem("job_free")
    rem_ok = sem("rem_ok")
    mid_ok = sem("mid_ok")
    low_ok = sem("low_ok")
    part_out = [sem(f"part_out{i}") for i in range(4)]
    v_out = [sem(f"v_out{i}") for i in range(2)]
    top_ok = sem("top_ok")
    exp_in = sem("exp_in")
    exp_ok = sem("exp_ok")
    total_ok = sem("total_ok")
    probs_ok = sem("probs_ok")
    chosen_ok = sem("chosen_ok")
    mask_ok = sem("mask_ok")
    stack_in = [sem(f"stack_in{i}") for i in range(3)]
    v_in = [sem(f"v_in{i}") for i in range(3)]
    ones_ok = sem("ones_ok")
    mbank_full = sem("mbank_full")
    mbank_free = sem("mbank_free")
    nm_step = sem("nm_step")
    nmT_ok = sem("nmT_ok")
    bias_in = [sem(f"bias_in{h}") for h in range(2)]
    score_ok = sem("score_ok")
    exp_done = sem("exp_done")
    av_done = sem("av_done")
    evac_done = sem("evac_done")
    routed = sem("routed")
    scattered = sem("scattered")

    mats = [(v["pq"], v["aq"]), (v["pk"], v["ak"]), (v["pv"], v["av"]), (v["po"], v["ao"])]
    CONSTS = 11

    plan = schedule()
    jobs = [e for e in plan if e[0] in JOBS]
    J = {e: i for i, e in enumerate(jobs)}

    SBANKS = 3
    half = UNITS // 2

    def stream(off):
        return [(1, off + 1, w) for w in range(EARLY, UNITS)] + [(2, off + 2, w) for w in range(EARLY)]

    def pe_use(pe, mod, w, free, fill=None):
        bank = 2 * (w % 2)

        def piece(kh):
            def go():
                if kh == 0:
                    if fill is not None:
                        pe.wait_ge(stack_in[mod % 3], 16 * STACK_DMAS * fill)
                    if free is not None:
                        pe.wait_ge(mbank_free, free)
                j, qt = w // KT, w % KT
                ins = pe.matmul(psum[:, bank + kh, :], q_stack[0:SROWS, mod % 3, j, P * qt:P * (qt + 1)],
                                k_stack[0:SROWS, mod % 3, j, N * kh:N * (kh + 1)], start=True, stop=True)
                if kh == QH - 1:
                    ins.then_inc(mbank_full, 1)
            return go

        return [piece(kh) for kh in range(QH)]

    def dve_use(dve, k, w, first=False):
        done = UNITS * k + (w + 1)
        bank = 2 * (w % 2)
        dve.wait_ge(mbank_full, done)
        pair = psum[:, bank:bank + 2, :].rearrange("p b n -> p (b n)")
        dve.tensor_reduce(mx[:, w:w + 1], pair, AX.X, ALU.max).then_inc(mbank_free, 1)
        if w % half == half - 1:
            h = w // half
            m2 = mx[:, half * h:half * (h + 1)].rearrange("p (j t) -> p j t", j=2)
            dve.wait_ge(mbank_free, done)
            dve.tensor_scalar(nm[:, h, 0, :, :], m2, -1.0, None, ALU.mult).then_inc(nm_step, 1)
            dve.wait_ge(nm_step, 4 * k + (2 * h + 1))
            dve.scalar_tensor_tensor(nm[:, h, 1, :, :], m2, -1.0, nm[:, h, 0, :, :],
                                     ALU.mult, ALU.subtract).then_inc(nm_step, 1)
            dve.wait_ge(nm_step, 4 * k + (2 * h + 2))
            if not first:
                dve.wait_ge(bias_in[h], 16 * BIAS_DMAS * k)
            dve.transpose(nmT[:, h, :], nm[:, h, :, :, :].rearrange("p s j t -> p (s j t)")).then_inc(nmT_ok, 1)

    def load(sp, G, buf):
        for st, dram, runs in ((q_stack, q_parts, Q_RUNS), (k_stack, k_parts, K_RUNS)):
            flat = dram.rearrange("g s (d j) t -> g s d (j t)", j=GH)
            for at, lo, n in runs:
                sp.dma_start(st[HD * at:HD * (at + n), buf, :, :].rearrange("p j t -> p (j t)"),
                             flat[bass.ds(G, 1), lo:lo + n, :, :].rearrange("g s d n -> (g s d) n")).then_inc(stack_in[buf], 16)

    def load_v(sp, G, buf):
        vw = v_wide.rearrange("g (t p) n -> g p t n", p=P)
        sp.dma_start(v_stack[:, buf, :, :, :].rearrange("p t j d -> p t (j d)"),
                     vw[bass.ds(G, 1), :, :, :].rearrange("g p t n -> (g p) t n")).then_inc(v_in[buf], 16)

    def bias(sp, G, buf, h):
        sp.wait_ge(nmT_ok, 2 * G + (h + 1))
        for b in range(BIAS_DMAS):
            sp.dma_start(q_stack[SROWS:KROWS, buf, 2 * h:2 * h + 2, :]
                         .rearrange("s j (t b c) -> s (j t) b c", t=KT, b=BIAS_DMAS)[:, :, b, :],
                         nmT[32 * b:32 * (b + 1), h, :]).then_inc(bias_in[h], 16)

    def av_at(peel):
        return 2 if peel == "last" else 1

    def pe_group(pe, G, off, it, peel):
        buf = off % 3
        if off == 2:
            pe.wait_ge(ones_ok, 3)
        uses = []
        if peel != "last":
            for back, mod, w in stream(off):
                fill = it + (mod // 3 + 1) if w == 0 else None
                uses += pe_use(pe, mod, w, UNITS * G + (UNITS * back + (w - 1)), fill)
        pe.wait_ge(v_in[buf], 16 * (it + (off // 3 + 1)))
        for h in range(2):
            pe.wait_ge(bias_in[h], 16 * BIAS_DMAS * (G + 1))
        for s in range(STEPS):
            qh, kt = s // KT, s % KT
            for j in range(GH):
                u = GH * s + j
                if not (peel == "first" and u < SBANKS):
                    pe.wait_ge(exp_done, GH * STEPS * G + (u - SBANKS + 1))
                pe.matmul(psum[:, 4 + (off + u) % SBANKS, :], k_stack[0:KROWS, buf, j, P * kt:P * (kt + 1)],
                          q_stack[0:KROWS, buf, j, N * qh:N * (qh + 1)], start=True, stop=True).then_inc(score_ok, 1)
                if uses:
                    uses.pop(0)()
                if j == av_at(peel) and not (peel == "first" and s == 0):
                    av_step(pe, G, off, s - 1, peel)
                if j == 0 and peel == "last":
                    if s == 0:
                        pe.wait_ge(late_in, 16 * (2 + len(FCH)))
                        pe.wait_ge(mbank_free, UNITS * GROUPS + EARLY)
                    f, part, part_of_n, c = s // 8, s // 4 % 2, s // 2 % 2, s % 2
                    ins = gate_up_piece(pe, psum, v["sw_gu"], xfT, 0, f, part, c, N // 2 * part_of_n, N // 2)
                    if s % 8 == 7:
                        ins.then_inc(v["sgu_ps"], 1)

    def av_step(pe, G, off, s, peel):
        buf = (off + s // STEPS) % 3
        qh, kt = s % STEPS // KT, s % KT
        pe.wait_ge(exp_done, GH * STEPS * G + GH * (s + 1))
        if kt == 0 and not (peel == "first" and qh == 0):
            pe.wait_ge(evac_done, QH * G + qh)
        for j in range(GH):
            last = pe.matmul(psum[32 * j:32 * (j + 1), 4 + SBANKS, :], v_stack[:, buf, kt, j, :],
                             prob[:, (off * STEPS + s) % 3, j, :], start=(kt == 0), stop=(kt == KT - 1))
        last.then_inc(av_done, 1)

    def act_group(act, G, off, it, peel):
        for s in range(STEPS):
            for j in range(GH):
                u = GH * s + j
                act.wait_ge(score_ok, GH * STEPS * G + (u + 1))
                if j == 0 and not (peel == "first" and s < 3):
                    act.wait_ge(av_done, STEPS * G + (s - 2))
                act.activation(prob[:, (off * STEPS + s) % 3, j, :], psum[:, 4 + (off + u) % SBANKS, :], ACT.Exp,
                               scale=SCALE).then_inc(exp_done, 1)
                if j == av_at(peel) and s == 0 and peel != "first":
                    evac(act, G - 1, 1)
                if j == av_at(peel) and s == KT:
                    if peel == "first":
                        act.wait_ge(xn_free, BLK)
                    if off == 1:
                        act.wait_ge(routed, 1)
                    evac(act, G, 0)

    def evac(act, G, qh):
        act.wait_ge(av_done, STEPS * G + KT * (qh + 1))
        act.copy(attT[:, bass.ds(G, 1), N * qh:N * (qh + 1)], psum[:, 4 + SBANKS:5 + SBANKS, :]).then_inc(evac_done, 1)

    def groups(eng, run):
        run(0, 0, 0, "first")
        with eng.Fori(0, (GROUPS - 2) // 3) as it:
            for off in range(1, 4):
                run(it * 3 + off, off, it, None)
        run(GROUPS - 1, (GROUPS - 1) % 3, (GROUPS - 1) // 3, "last")

    def unit(n):
        return n // 4, (0, 2, 1, 3)[n % 4]

    with nc.Block() as block:
        @block.sync
        def _(sp):
            xr = x.rearrange("b s h -> (b s) h").rearrange("(t p) h -> p t h", p=P)
            for i in range(BLK):
                if i == BLK // 2:
                    for m, w in enumerate(("bq", "bk", "bv", "bo")):
                        sp.dma_start(basis[64 * (m % 2):64 * (m % 2 + 1), m // 2, :], v[w]).then_inc(basis_in, 16)
                sp.dma_start(res[:, TPB * i:TPB * (i + 1), :], xr[:, TPB * i:TPB * (i + 1), :]).then_inc(x_in[i], 16)
            for m, (_, am) in enumerate(mats):
                sp.dma_start(amp[:, :, m, :], am.rearrange("(c p) h -> p c h", p=P)).then_inc(amp_in, 16)
            wn_src = v["w_norm"].rearrange("(a h) -> a h", a=1)
            sp.dma_start(wn, wn_src.broadcast_to([P, HID])).then_inc(vec_in, 16)
            sp.dma_start(wr[:, :, 0:EXPERTS], v["w_router"].rearrange("(c p) e -> p c e", p=P)).then_inc(vec_in, 16)
            with nc.allow_non_contiguous_dma(reason="one column of 256 weights"):
                sp.dma_start(wr[:, :, EXPERTS:EXPERTS + 1],
                             v["w_sg"].rearrange("(c p) e -> p c e", p=P)).then_inc(vec_in, 16)
            sp.wait_ge(vec_in, 48)
            sp.wait_ge(const_ok, 1)
            for i in range(8):
                sp.dma_start(slot_x[N * i:N * (i + 1), :].rearrange("(p r) h -> p (r h)", p=P),
                             zeros).then_inc(zero_out, 16)
            sp.dma_start(slot_y[SLOTS:SLOTS + 1, :], zeros[0:1, 0:HID]).then_inc(zero_out, 16)
            for e in plan:
                if e[0] in ("qk", "low"):
                    n = e[1] - 1 if e[0] == "qk" else e[1]
                    if n < 0 or (e[0] == "qk" and n == 7):
                        continue
                    sp.wait_ge(low_ok, n + 1)
                    b, u = unit(n)
                    dst = (q_parts, k_parts)[u // 2]
                    for i in range(2):
                        sp.dma_start(dst[HG * (b // 2) + 2 * (u % 2) + i, :, :, N * (b % 2):N * (b % 2 + 1)]
                                     .rearrange("s p t -> p s t"),
                                     parts[n % 4][64 * i:64 * (i + 1), :, :]).then_inc(part_out[n % 4], 16)
                elif e[0] == "v":
                    n = e[1]
                    sp.wait_ge(job_free, J[e] + 1)
                    for t in range(2):
                        tile = 2 * n + t
                        row = P * (tile % KT)
                        sp.dma_start(v_wide[HG * (tile // KT):HG * (tile // KT + 1), row:row + P, :].rearrange("g p n -> p g n"),
                                     v_stage[:, n % 2, t, :, :]
                                     .rearrange("p (g j) d -> p g (j d)", g=HG)).then_inc(v_out[n % 2], 16)
                elif e[0] == "load":
                    if e[1] == 0:
                        for i in range(2):
                            sp.wait_ge(part_out[i], 64)
                    load(sp, e[1], e[1])
                elif e[0] == "load_v":
                    for i in range(2):
                        sp.wait_ge(v_out[i], 64)
                    load_v(sp, 0, 0)
                elif e[0] == "bias":
                    bias(sp, 0, 0, e[1])
            for i in range(4):
                sp.wait_ge(part_out[i], 128)
            load(sp, 2, 2)
            for i in range(2):
                sp.wait_ge(v_out[i], 128)
            load_v(sp, 1, 1)
            load_v(sp, 2, 2)
            sgu = v["sw_gu"]
            sp.dma_start(sgu[:, :, 0, :], v["sw_gate"].rearrange("(c p) f -> p c f", p=P)).then_inc(late_in, 16)
            sp.dma_start(sgu[:, :, 1, :], v["sw_up"].rearrange("(c p) f -> p c f", p=P)).then_inc(late_in, 16)
            for i, (o, n) in enumerate(zip(FOFF, FCH)):
                sp.dma_start(v["sw_dn"][0:n, i, :], v["sw_down"][o:o + n, :]).then_inc(late_in, 16)
            for h in range(2):
                bias(sp, 1, 1, h)
            with sp.Fori(0, (GROUPS - 2) // 3) as it:
                for off in range(1, 4):
                    G = it * 3 + off
                    sp.wait_ge(av_done, STEPS * G + 1)
                    load(sp, (G + 2) % GROUPS, (off + 2) % 3)
                    load_v(sp, (G + 2) % GROUPS, (off + 2) % 3)
                    for h in range(2):
                        bias(sp, G + 1, (off + 1) % 3, h)
            sp.wait_ge(late_in, 16 * 8)
            sp.wait_ge(zero_out, 16 * 9)
            sp.wait_ge(stack_in[GROUPS % 3], 16 * STACK_DMAS * (GROUPS // 3 + 1))
            sp.wait_ge(v_in[GROUPS % 3], 16 * (GROUPS // 3 + 1))

        @block.gpsimd
        def _(pool):
            count = [0]

            def link(ins):
                count[0] += 1
                ins.then_inc(pool_step, 1)
                pool.wait_ge(pool_step, count[0])

            pool.memset(zeros, 0.0).then_inc(const_ok, 1)
            pool.memset(ident[:, :], 0.0)
            link(pool.memset(before[:, :], 1.0))
            pool.affine_select(out=ident[:, :], in_=ident[:, :], compare_op=ALU.not_equal, fill=1.0, base=0,
                               pattern=[[-1, P]], channel_multiplier=1).then_inc(const_ok, 1)
            pool.affine_select(out=before[:, :], in_=before[:, :], compare_op=ALU.is_gt, fill=0.0, base=0,
                               pattern=[[1, P]], channel_multiplier=-1).then_inc(const_ok, 1)
            halves = ((wq, 64), (wk, 0), (wv, 64), (wo, 0))
            for i, (w, lo) in enumerate(halves):
                pool.wait_ge(const_ok, 3 + i)
                pool.memset(w[lo:lo + 64, :], 0.0).then_inc(const_ok, 1)
            pool.wait_ge(const_ok, 7)
            pool.memset(ones_b[:, :], 1.0).then_inc(const_ok, 1)
            pool.iota(iota_e[:, :], pattern=[[1, EXPERTS]], base=0, channel_multiplier=0,
                      allow_small_or_imprecise_dtypes=True).then_inc(const_ok, 1)
            for i in range(2):
                pool.memset(v_stage[:, i, :, :, HD:32], 1.0).then_inc(const_ok, 1)
            pool.wait_ge(const_ok, CONSTS)
            for buf in range(2):
                pool.memset(k_stack[SROWS:KROWS, buf, :, :], 1.0).then_inc(ones_ok, 1)
                pool.wait_ge(ones_ok, buf + 1)
            wide_te = [P, TILES, EXPERTS]

            def residual(b):
                pool.wait_ge(xn_ok, TPB * (b + 1))
                sl = slice(TPB * b, TPB * (b + 1))
                pool.tensor_tensor(res[:, sl, :], res[:, sl, :], xn[:, sl, :], ALU.add).then_inc(xn_free, 1)

            residual(0)
            residual(1)
            for e in plan:
                kind = e[0]
                if kind == "qk":
                    n = e[1]
                    pool.wait_ge(mid_ok, n + 1)
                    pool.tensor_tensor(parts[n % 4][:, 2, :], rem[:, n % 2, :], parts[n % 4][:, 1, :],
                                       ALU.subtract).then_inc(low_ok, 1)
                elif kind == "rms":
                    pool.wait_ge(rms_ok, 1)
                    pool.wait_ge(vec_in, 48)
                    for b in range(BLK):
                        sl = slice(TPB * b, TPB * (b + 1))
                        blk = [P, TPB, HID]
                        link(pool.tensor_tensor(xf[:, sl, :], xn[:, sl, :], small[:, 7, sl].unsqueeze(2).broadcast_to(blk),
                                                ALU.mult))
                        pool.tensor_tensor(xf[:, sl, :], xf[:, sl, :], wn.unsqueeze(1).broadcast_to(blk),
                                           ALU.mult).then_inc(xf_ok, 1)
                elif kind == "soft1":
                    pool.wait_ge(top_ok, 1)
                    pool.tensor_tensor(probs, probs, small[:, 8, :].unsqueeze(2).broadcast_to(wide_te),
                                       ALU.subtract).then_inc(exp_in, 1)
                elif kind == "soft3":
                    pool.wait_ge(total_ok, 1)
                    pool.tensor_tensor(probs, probs, small[:, 12, :].unsqueeze(2).broadcast_to(wide_te),
                                       ALU.mult).then_inc(probs_ok, 1)
                elif kind == "soft5":
                    pool.wait_ge(chosen_ok, 1)
                    link(pool.tensor_tensor(mask_b, onehot[:, 0, :, :], onehot[:, 1, :, :], ALU.add))
                    link(pool.tensor_tensor(mask_b, mask_b, onehot[:, 2, :, :], ALU.add))
                    pool.tensor_tensor(mask_b, mask_b, onehot[:, 3, :, :], ALU.add).then_inc(mask_ok, 1)
            residual(2)
            residual(3)
            for i in range(4):
                pool.wait_ge(part_out[i], 128)
            pool.wait_ge(xn_free, BLK)
            pool.memset(k_stack[SROWS:KROWS, 2, :, :], 1.0).then_inc(ones_ok, 1)
            pool.wait_ge(ones_ok, 3)
            pool.wait_ge(job_free, J[("count", 1)] + 1)
            cur, nxt, sh = cum0, cum1, 1
            while sh < TILES:
                link(pool.tensor_copy(nxt[:, 0:sh, :], cur[:, 0:sh, :]))
                link(pool.tensor_tensor(nxt[:, sh:, :], cur[:, sh:, :], cur[:, 0:TILES - sh, :], ALU.add))
                cur, nxt, sh = nxt, cur, 2 * sh
            link(pool.tensor_tensor(pos[:, 1:, :], pos[:, 1:, :], cur[:, 0:TILES - 1, :], ALU.add))
            one, two = place[:, 0, :, :], place[:, 1, :, :]
            for k in range(TOPK):
                link(pool.tensor_tensor(rtmp, onehot[:, k, :, :], pos, ALU.mult))
                n = EXPERTS // 2
                while n > 1:
                    link(pool.tensor_tensor(rtmp[:, :, 0:n], rtmp[:, :, 0:n], rtmp[:, :, n:2 * n], ALU.add))
                    n //= 2
                link(pool.tensor_tensor(one[:, k, :], rtmp[:, :, 0], rtmp[:, :, 1], ALU.add))
            link(pool.tensor_scalar(two, one, float(CAP), None, ALU.is_lt))
            link(pool.tensor_tensor(wsel[:, :, :], top8[:, :, 0:TOPK].rearrange("p t k -> p k t"), two, ALU.mult))
            ids = rtmp[:, 0:2, :].rearrange("p a e -> p (a e)").rearrange("p (k t) -> p k t", k=TOPK)
            link(pool.tensor_scalar(ids, idxf[:, :, 0:TOPK].rearrange("p t k -> p k t"), float(CAP), None, ALU.mult))
            link(pool.tensor_tensor(one, one, ids, ALU.add))
            link(pool.tensor_scalar(one, one, float(-SLOTS), None, ALU.add))
            link(pool.tensor_tensor(one, one, two, ALU.mult))
            pool.tensor_scalar(slot[:, :, :], one, float(SLOTS), None, ALU.add).then_inc(routed, 1)
            pool.wait_ge(routed, 1)
            pool.wait_ge(zero_out, 16 * 9)
            for t in range(TILES):
                for k in range(TOPK):
                    pool.indirect_dma_start(out=slot_x, out_offset=bass.IndirectOffsetOnAxis(ap=slot[:, k, t:t + 1], axis=0),
                                            in_=xf[:, t, :], in_offset=None, bounds_check=SLOTS - 1,
                                            oob_is_err=False).then_inc(scattered, 16)
            pool.wait_ge(scattered, 16 * TOPK * TILES)

        @block.scalar
        def _(act):
            for m, (ph, _) in enumerate(mats):
                act.dma_start(phase[:, :, m, :], ph.rearrange("(c p) h -> p c h", p=P)).then_inc(phase_in, 16)

            def root(i):
                act.wait_ge(var_ok, i + 1)
                act.activation(small[:, 0, 8 * i:8 * (i + 1)], mv[:, 8 * i:8 * (i + 1), 1], ACT.Sqrt,
                               bias=eps[:, 0:1]).then_inc(sqrt_ok, 1)

            root(0)

            def middle(n):
                act.wait_ge(rem_ok, n + 1)
                act.copy(parts[n % 4][:, 1, :], rem[:, n % 2, :]).then_inc(mid_ok, 1)

            late = []
            for e in plan:
                kind = e[0]
                if kind in JOBS:
                    j = J[e]
                    bank = psum[:, 4 + j % 4, :]
                    act.wait_ge(job_full, j + 1)
                if kind == "bases":
                    act.copy(bT[:, :, :, :].rearrange("p s c h -> p (s c h)"), bank).then_inc(job_free, 1)
                elif kind == "weights":
                    for w, lo in ((wq, 0), (wk, 64)):
                        act.copy(w[lo:lo + 64, :].rearrange("p (g d j) -> p g d j", g=HG, d=HD),
                                 psum[lo:lo + 64, 4 + j % 4, 0:HID].rearrange("p (g j d) -> p g d j", g=HG, j=GH))
                    act.copy(wv[0:64, :], psum[0:64, 4 + j % 4, HID:2 * HID])
                    act.copy(wo[64:128, :], psum[64:128, 4 + j % 4, HID:2 * HID]).then_inc(job_free, 1)
                elif kind == "out_basis":
                    act.copy(boT[:, :, :].rearrange("p g h -> p (g h)"), bank).then_inc(job_free, 1)
                elif kind in ("xT", "xfT"):
                    dst = (xnT if kind == "xT" else xfT)[:, e[2], N * e[1]:N * (e[1] + 1)]
                    act.copy(dst, bank).then_inc(job_free, 1)
                elif kind == "res_qk":
                    if e[1] >= 2:
                        act.wait_ge(job_full, J[("qk", 4 * (e[1] - 2) + 3)] + 1)
                    act.copy(rt[:, e[1] % 2, :], bank).then_inc(job_free, 1)
                elif kind == "res_v":
                    if e[1]:
                        act.wait_ge(job_full, J[("v", 2 * e[1] - 1)] + 1)
                    act.copy(rvo[:, :], bank).then_inc(job_free, 1)
                elif kind == "v":
                    n = e[1]
                    act.wait_ge(const_ok, CONSTS)
                    if n >= 2:
                        act.wait_ge(v_out[n % 2], 32 * (n // 2))
                    act.copy(v_stage[:, n % 2, :, :, 0:HD],
                             bank.rearrange("p (t h d) -> p t h d", t=2, h=HEADS)).then_inc(job_free, 1)
                elif kind == "qk":
                    if e[1] >= 4:
                        act.wait_ge(part_out[e[1] % 4], 32 * (e[1] // 4))
                    act.copy(parts[e[1] % 4][:, 0, :], bank).then_inc(job_free, 1)
                elif kind == "logits":
                    lg = bank.rearrange("p (t e) -> p t e", t=TPB)
                    sl = slice(TPB * e[1], TPB * (e[1] + 1))
                    act.copy(probs[:, sl, :], lg[:, :, 0:EXPERTS])
                    act.copy(small[:, 9, sl], lg[:, :, EXPERTS]).then_inc(job_free, 1)
                elif kind == "count":
                    act.copy(((pos, cum0)[e[1]]).rearrange("p t e -> p (t e)"), bank).then_inc(job_free, 1)
                elif kind == "square":
                    for t in range(TPB * e[1], TPB * (e[1] + 1)):
                        act.wait_ge(xn_ok, t + 1)
                        act.activation(xf[:, t, :], xn[:, t, :], ACT.Square, scale=1.0 / 16.0,
                                       accum_out=small[:, 4, t:t + 1]).then_inc(ms_ok, 1)
                    if e[1] == BLK - 1:
                        act.wait_ge(ms_ok, TILES)
                        act.activation(small[:, 5, :], small[:, 4, :], ACT.Sqrt, bias=eps[:, 1:2]).then_inc(sqrt_ok, 1)
                elif kind == "sin":
                    act.wait_ge(ang_ok, 1)
                    act.activation(wmat, ang, ACT.Sin).then_inc(sin_ok, 1)
                elif kind == "root":
                    root(1)
                elif kind == "soft2":
                    act.wait_ge(exp_in, 1)
                    act.activation(probs, probs, ACT.Exp).then_inc(exp_ok, 1)
                    act.activation(small[:, 10, :], small[:, 9, :], ACT.Tanh, scale=0.5).then_inc(exp_ok, 1)
                if late and kind != "use":
                    middle(late.pop())
                if kind == "qk" and e[1] >= 8:
                    late.append(e[1])
            act.wait_ge(zero_out, 16 * 9)
            act.wait_ge(xf_ok, BLK)
            groups(act, lambda *a: act_group(act, *a))
            evac(act, GROUPS - 1, 1)

        @block.tensor
        def _(pe):
            pe.wait_ge(const_ok, 7)
            for e in plan:
                kind = e[0]
                if kind == "use":
                    k, w = divmod(e[1], UNITS)
                    if e[1] == 0:
                        pe.wait_ge(stack_in[0], 16 * STACK_DMAS)
                        pe.wait_ge(ones_ok, 2)
                    for piece in pe_use(pe, k, w, e[1] - 1 if e[1] >= 2 else None, 1 if k == 1 and w == 0 else None):
                        piece()
                    continue
                if kind not in JOBS:
                    continue
                j = J[e]
                if j >= 4:
                    pe.wait_ge(job_free, j - 3)
                    if jobs[j - 4][0] == "qk":
                        pe.wait_ge(rem_ok, jobs[j - 4][1] + 1)
                bank = psum[:, 4 + j % 4, :]
                if kind == "bases":
                    pe.wait_ge(basis_in, 16 * 4)
                    for s in range(2):
                        for c in range(HC):
                            last = pe.transpose(bank[:, P * (2 * s + c):P * (2 * s + c + 1)],
                                                basis[:, s, P * c:P * (c + 1)], ident[:, :])
                elif kind == "weights":
                    pe.wait_ge(wmat_ok, 1)
                    for s in range(2):
                        for c in range(HC):
                            last = pe.transpose(bank[:, P * (2 * s + c):P * (2 * s + c + 1)],
                                                wmat[:, c, 2 * s:2 * s + 2, :], ident[:, :])
                elif kind == "out_basis":
                    pe.wait_ge(wmat_ok, 2)
                    for g in range(HG):
                        last = pe.transpose(bank[:, P * g:P * (g + 1)], bo_pad[:, g, :, :], ident[:, :])
                elif kind in ("xT", "xfT"):
                    src = xn if kind == "xT" else xf
                    if kind == "xT":
                        pe.wait_ge(xn_ok, TPB * (e[1] + 1))
                    else:
                        pe.wait_ge(xf_ok, e[1] + 1)
                    for t in range(TPB):
                        last = pe.transpose(bank[:, P * t:P * (t + 1)],
                                            src[:, TPB * e[1] + t, P * e[2]:P * (e[2] + 1)], ident[:, :])
                elif kind in ("res_qk", "res_v"):
                    pe.wait_ge(job_free, J[("xT", e[1], 1)] + 1)
                    for c in range(HC):
                        last = pe.matmul(bank, bT[:, int(kind == "res_v"), c, :], xnT[:, c, N * e[1]:N * (e[1] + 1)],
                                         start=(c == 0), stop=(c == HC - 1))
                elif kind == "qk":
                    b, u = unit(e[1])
                    pe.wait_ge(job_free, max(J[("res_qk", b)], J[("weights",)]) + 1)
                    last = pe.matmul(bank, (wq, wk)[u // 2][:, P * (u % 2):P * (u % 2 + 1)], rt[:, b % 2, :],
                                     start=True, stop=True)
                elif kind == "v":
                    pe.wait_ge(job_free, max(J[("res_v", e[1] // 2)], J[("weights",)]) + 1)
                    for t in range(2):
                        tt = 2 * (e[1] % 2) + t
                        last = pe.matmul(bank[:, HID * t:HID * (t + 1)], rvo[:, P * tt:P * (tt + 1)],
                                         wv[:, :], start=True, stop=True)
                elif kind == "logits":
                    pe.wait_ge(vec_in, 48)
                    pe.wait_ge(job_free, J[("xfT", e[1], 1)] + 1)
                    for t in range(TPB):
                        tt = TPB * e[1] + t
                        for c in range(HC):
                            last = pe.matmul(bank[:, P * t:P * t + EXPERTS + 1], xfT[:, c, P * tt:P * (tt + 1)],
                                             wr[:, c, :], start=(c == 0), stop=(c == HC - 1))
                elif kind == "count":
                    pe.wait_ge(mask_ok, 1)
                    pe.wait_ge(const_ok, 8)
                    last = pe.matmul(bank, (before, ones_b)[e[1]][:, :], mask_b.rearrange("p t e -> p (t e)"),
                                     start=True, stop=True)
                last.then_inc(job_full, 1)
            pe.wait_ge(job_free, len(jobs))
            groups(pe, lambda *a: pe_group(pe, *a))
            av_step(pe, GROUPS - 1, (GROUPS - 1) % 3, STEPS - 1, "last")

        @block.vector
        def _(dve):
            steps = [0]

            def link(ins):
                steps[0] += 1
                ins.then_inc(dve_step, 1)
                dve.wait_ge(dve_step, steps[0])

            def inverse_root(var, root, e, tmp, y):
                link(dve.reciprocal(y, root))
                link(dve.tensor_tensor(tmp, y, y, ALU.mult))
                link(dve.scalar_tensor_tensor(tmp, var, e, tmp, ALU.add, ALU.mult))
                link(dve.tensor_scalar(tmp, tmp, -0.5, 1.5, ALU.mult, ALU.add))
                link(dve.tensor_tensor(y, y, tmp, ALU.mult))

            def statistics(i):
                for b in range(2 * i, 2 * i + 2):
                    dve.wait_ge(x_in[b], 16)
                    for t in range(TPB * b, TPB * (b + 1)):
                        last = dve.bn_stats(bn[:, t, :], res[:, t, :])
                link(last)
                for t in range(8 * i, 8 * (i + 1)):
                    last = dve.bn_aggr(mv[:, t, :], bn[:, t, :])
                last.then_inc(var_ok, 1)

            def normalise(i):
                sl = slice(8 * i, 8 * (i + 1))
                dve.wait_ge(sqrt_ok, i + 1)
                inverse_root(mv[:, sl, 1], small[:, 0, sl], LN_EPS, small[:, 1, sl], small[:, 2, sl])
                for t in range(8 * i, 8 * (i + 1)):
                    dve.tensor_scalar(xn[:, t, :], res[:, t, :], mv[:, t, 0:1], small[:, 2, t:t + 1],
                                      ALU.subtract, ALU.mult).then_inc(xn_ok, 1)

            dve.memset(bo_pad, 0.0)
            dve.memset(eps[:, 0:1], LN_EPS)
            link(dve.memset(eps[:, 1:2], RMS_EPS))
            statistics(0)
            normalise(0)
            dve.wait_ge(phase_in, 16 * 4)
            link(dve.tensor_scalar(turn, phase, INV_TWO_PI, 0.25, ALU.mult, ALU.add))
            link(dve.tensor_scalar(turn, turn, ROUND, ROUND, ALU.add, ALU.subtract))
            link(dve.scalar_tensor_tensor(ang, turn, -TWO_PI_HI, phase, ALU.mult, ALU.add))
            link(dve.scalar_tensor_tensor(ang, turn, -TWO_PI_LO, ang, ALU.mult, ALU.add))
            link(dve.tensor_scalar(ang, ang, PI / 2, PI, ALU.add, ALU.min))
            dve.tensor_scalar(ang, ang, -PI, None, ALU.max).then_inc(ang_ok, 1)
            statistics(1)
            dve.wait_ge(amp_in, 16 * 4)
            dve.wait_ge(sin_ok, 1)
            dve.tensor_tensor(wmat, wmat, amp, ALU.mult).then_inc(wmat_ok, 1)
            dve.wait_ge(basis_in, 16 * 4)
            dve.tensor_copy(bo_pad[64:128, :, :, 0:HD],
                            basis[64:128, 1, :].rearrange("p (g j d) -> p g j d", g=HG, j=GH)).then_inc(wmat_ok, 1)
            normalise(1)

            for e in plan:
                kind = e[0]
                if kind == "use":
                    k, w = divmod(e[1], UNITS)
                    dve_use(dve, k, w, True)
                elif kind == "qk":
                    n = e[1]
                    dve.wait_ge(job_free, J[e] + 1)
                    if n >= 2:
                        dve.wait_ge(low_ok, n - 1)
                    dve.tensor_tensor(rem[:, n % 2, :], psum[:, 4 + J[e] % 4, :], parts[n % 4][:, 0, :],
                                      ALU.subtract).then_inc(rem_ok, 1)
                    if n < 8:
                        dve.wait_ge(rem_ok, n + 1)
                        dve.tensor_copy(parts[n % 4][:, 1, :], rem[:, n % 2, :]).then_inc(mid_ok, 1)
                elif kind == "rms":
                    dve.wait_ge(sqrt_ok, 3)
                    link(dve.reciprocal(small[:, 7, :], small[:, 5, :]))
                    link(dve.tensor_tensor(small[:, 6, :], small[:, 7, :], small[:, 7, :], ALU.mult))
                    link(dve.scalar_tensor_tensor(small[:, 6, :], small[:, 4, :], RMS_EPS, small[:, 6, :], ALU.add, ALU.mult))
                    link(dve.tensor_scalar(small[:, 6, :], small[:, 6, :], -0.5, 1.5, ALU.mult, ALU.add))
                    dve.tensor_tensor(small[:, 7, :], small[:, 7, :], small[:, 6, :], ALU.mult).then_inc(rms_ok, 1)
                elif kind == "soft1":
                    dve.wait_ge(job_free, J[("logits", BLK - 1)] + 1)
                    dve.tensor_reduce(small[:, 8, :], probs, AX.X, ALU.max).then_inc(top_ok, 1)
                elif kind == "soft3":
                    dve.wait_ge(exp_ok, 2)
                    link(dve.tensor_reduce(small[:, 11, :], probs, AX.X, ALU.add))
                    dve.reciprocal(small[:, 12, :], small[:, 11, :]).then_inc(total_ok, 1)
                    dve.tensor_scalar(sgate[:, :], small[:, 10, :], 0.5, 0.5, ALU.mult, ALU.add)
                elif kind == "soft4":
                    dve.wait_ge(probs_ok, 1)
                    for t in range(TILES):
                        last = dve.max(top8[:, t, :], probs[:, t, :])
                    link(last)
                    for t in range(TILES):
                        last = dve.max_index(idx8[:, t, :], top8[:, t, :], probs[:, t, :])
                    link(last)
                    link(dve.tensor_copy(idxf[:, :, :], idx8[:, :, :]))
                    dve.wait_ge(const_ok, 9)
                    blk = [P, TILES, EXPERTS]
                    ie = iota_e[:, :].unsqueeze(1).broadcast_to(blk)
                    for k in range(TOPK):
                        last = dve.tensor_tensor(onehot[:, k, :, :], ie, idxf[:, :, k:k + 1].broadcast_to(blk), ALU.is_equal)
                    last.then_inc(chosen_ok, 1)

            def run(G, off, it, peel):
                if peel != "last":
                    for back, _, w in stream(off):
                        dve_use(dve, G + back, w)

            groups(dve, run)


def feed_forward(nc, sem, v):
    psum, attT, ident, xfT, res, slot = v["psum"], v["attT"], v["ident"], v["xfT"], v["res"], v["slot"]
    boT, wo, wsel, sgate, sw_gu, sw_dn = v["boT"], v["wo"], v["wsel"], v["sgate"], v["sw_gu"], v["sw_dn"]
    up_in = [sem(f"up_in{i}") for i in range(2)]
    down_in = [sem(f"down_in{i}") for i in range(2)]
    bufT_ps = sem("bufT_ps")
    bufT_ok = sem("bufT_ok")
    gu_ok = sem("gu_ok")
    silu_ok = sem("silu_ok")
    hid_ok = sem("hid_ok")
    hidT_ps = sem("hidT_ps")
    hidT_ok = sem("hidT_ok")
    y_ps = sem("y_ps")
    y_ok = sem("y_ok")
    y_out = [sem(f"y_out{i}") for i in range(2)]
    sums_in = sem("sums_in")
    recip_ok = sem("recip_ok")
    recips_in = sem("recips_in")
    den_ok = sem("den_ok")
    spread_ok = sem("spread_ok")
    norm_ok = sem("norm_ok")
    gathered = [sem(f"gathered{i}") for i in range(3)]
    ro_ps = sem("ro_ps")
    ro_ok = sem("ro_ok")
    att_ps = sem("att_ps")
    att_ok = sem("att_ok")
    sgu_ps = v["sgu_ps"]
    ssilu_ok = sem("ssilu_ok")
    shid_ok = sem("shid_ok")
    sh_ps = sem("sh_ps")
    sh_ok = sem("sh_ok")
    mix_step = sem("mix_step")
    tile_ok = sem("tile_ok")
    stored = sem("stored")

    qm, km = v["q_mem"], v["k_mem"]
    at_gu, at_dn = 4 * HID, 4 * (HID + HC * 2 * FF)
    xb = qm[:, 0:at_gu].rearrange("p (e h) -> p e h", e=4)
    wgu = qm[:, at_gu:at_dn].rearrange("p (e c s f) -> p e c s f", e=4, c=HC, s=2)
    wdn = qm[0:FHALF, at_dn:at_dn + 4 * 2 * HID].rearrange("p (e c h) -> p e c h", e=4, c=2)
    o = [0]

    def take(n):
        o[0] += n
        return km[:, o[0] - n:o[0]]

    xbT = [take(HID).rearrange("p (c t) -> p c t", c=HC) for _ in range(2)]
    silu = [take(FF) for _ in range(2)]
    hid = [take(FF) for _ in range(2)]
    hidT = [take(2 * P)[0:FHALF, :].rearrange("p (c t) -> p c t", c=2) for _ in range(2)]
    ysb = [take(HID) for _ in range(2)]
    den = [take(SEQ) for _ in range(2)]
    rc = take(GROUPS * SEQ // 32)
    ssilu = [take(N)[0:FCH[0], :] for _ in range(2)]
    ET = EXPERTS // 4
    NF = len(FCH)
    shid = v["prob"][0:FCH[0], :, :, :].rearrange("p a b n -> p (a b) n")
    rows = [qm[:, 1024 * i:1024 * (i + 1)].rearrange("p (k h) -> p k h", k=TOPK) for i in range(3)]
    ro = den[0][:, 0:N]
    out_v = v["out"].rearrange("b s h -> (b s) h").rearrange("(t p) h -> p t h", p=P)

    def turns(eng, run):
        run(0, "first")
        with eng.Fori(1, ET - 1) as it:
            run(it, None)
        run(ET - 1, "last")

    def tokens_T(pe, e, r, lap):
        pe.wait_ge(up_in[r // 2], 16 * 3 * (lap + 1))
        if not (isinstance(e, int) and e < 2):
            pe.wait_ge(bufT_ok, e - 1)
        for c in range(HC):
            last = pe.transpose(psum[:, r % 2, P * c:P * (c + 1)], xb[:, r, P * c:P * (c + 1)], ident[:, :])
        last.then_inc(bufT_ps, 1)

    def gate_up(pe, e, r):
        pe.wait_ge(bufT_ok, e + 1)
        if not (isinstance(e, int) and e < 2):
            pe.wait_ge(hid_ok, e - 1)
        for c in range(HC):
            last = pe.matmul(psum[:, 2 + r % 2, 0:2 * FF], xbT[r % 2][:, c, :],
                             wgu[:, r, c, :, :].rearrange("p s f -> p (s f)"), start=(c == 0), stop=(c == HC - 1))
        last.then_inc(gu_ok, 1)

    def hidden_T(pe, e, r):
        pe.wait_ge(hid_ok, e + 1)
        if not (isinstance(e, int) and e < 2):
            pe.wait_ge(hidT_ok, e - 1)
        for c in range(2):
            last = pe.transpose(psum[0:FHALF, 4 + r % 2, P * c:P * (c + 1)],
                                hid[r % 2][:, FHALF * c:FHALF * (c + 1)], ident[:, :])
        last.then_inc(hidT_ps, 1)

    def down(pe, e, r, lap):
        pe.wait_ge(down_in[r // 2], 16 * (lap + 1))
        pe.wait_ge(hidT_ok, e + 1)
        if not (isinstance(e, int) and e < 2):
            pe.wait_ge(y_ok, e - 1)
        for c in range(2):
            last = pe.matmul(psum[:, 6 + r % 2, 0:HID], hidT[r % 2][:, c, :], wdn[:, r, c, :],
                             start=(c == 0), stop=(c == 1))
        last.then_inc(y_ps, 1)

    def shared_gate_up(pe, b, f):
        i = NF * b + f
        if i >= 4:
            pe.wait_ge(shid_ok, i - 1)
        for s in range(2):
            for c in range(HC):
                last = gate_up_piece(pe, psum, sw_gu, xfT, b, f, s, c)
        last.then_inc(sgu_ps, 1)

    def shared_tail(pe, b):
        if b:
            pe.wait_ge(ro_ok, b)
        for g in range(HG):
            last = pe.matmul(psum[:, 4, :], boT[:, g, :],
                             attT[:, HG * (b // 2) + g, N * (b % 2):N * (b % 2 + 1)], start=(g == 0), stop=(g == HG - 1))
        last.then_inc(ro_ps, 1)
        pe.wait_ge(shid_ok, NF * (b + 1))
        for i in range(2):
            n = 2 * b + i
            if n >= 2:
                pe.wait_ge(sh_ok, n - 1)
            for t in range(2):
                tt = 2 * i + t
                for f in range(NF):
                    last = pe.matmul(psum[:, 6 + i, HID * t:HID * (t + 1)],
                                     shid[0:FCH[f], NF * (b % 2) + f, P * tt:P * (tt + 1)], sw_dn[0:FCH[f], f, :],
                                     start=(f == 0), stop=(f == NF - 1))
            last.then_inc(sh_ps, 1)
            if n:
                pe.wait_ge(att_ok, n)
            if i == 0:
                pe.wait_ge(ro_ok, b + 1)
            for t in range(2):
                tt = 2 * i + t
                last = pe.matmul(psum[:, 5, HID * t:HID * (t + 1)], ro[:, P * tt:P * (tt + 1)], wo[:, :],
                                 start=True, stop=True)
            last.then_inc(att_ps, 1)

    with nc.Block() as block:
        @block.sync
        def _(sp):
            xv = v["slot_x"].rearrange("(g e p) h -> g p e h", e=2, p=P)
            gv = v["w_gate"].rearrange("(g e) (c p) f -> g p (e c) f", e=2, p=P)
            uv = v["w_up"].rearrange("(g e) (c p) f -> g p (e c) f", e=2, p=P)
            dv = v["w_down"].rearrange("(g e) (c p) h -> g p (e c) h", e=2, p=FHALF)
            yv = v["slot_y"][0:SLOTS, :].rearrange("(e p) h -> e p h", p=P)

            def load_up(g, i):
                sp.dma_start(xb[:, 2 * i:2 * i + 2, :], xv[bass.ds(g, 1), :, :, :]
                             .rearrange("a p e h -> (a p) e h")).then_inc(up_in[i], 16)
                for s, w in enumerate((gv, uv)):
                    sp.dma_start(wgu[:, 2 * i:2 * i + 2, :, s, :].rearrange("p e c f -> p (e c) f"),
                                 w[bass.ds(g, 1), :, :, :].rearrange("a p n f -> (a p) n f")).then_inc(up_in[i], 16)

            def load_down(g, i):
                sp.dma_start(wdn[:, 2 * i:2 * i + 2, :, :].rearrange("p e c h -> p (e c) h"),
                             dv[bass.ds(g, 1), :, :, :].rearrange("a p n h -> (a p) n h")).then_inc(down_in[i], 16)

            def store(e, r):
                sp.wait_ge(y_ok, e + 1)
                sp.dma_start(yv[bass.ds(e, 1), :, :].rearrange("a p h -> (a p) h"), ysb[r % 2]).then_inc(y_out[r % 2], 16)

            flat = attT.rearrange("p g t -> p (g t)")
            for j in range(GH):
                sp.dma_start(rc[32 * j:32 * (j + 1), :],
                             flat[32 * j + HD:32 * j + HD + 1, :].rearrange("a (p n) -> a p n", p=32)).then_inc(sums_in, 16)
            for i in range(2):
                load_up(i, i)
                load_down(i, i)
            sp.wait_ge(recip_ok, 1)
            for j in range(GH):
                sp.dma_start(flat[32 * j + HD:32 * j + HD + 1, :].rearrange("a (p n) -> a p n", p=32),
                             rc[32 * j:32 * (j + 1), :]).then_inc(recips_in, 16)

            def run(it, peel):
                for i in range(2):
                    e = it * 4 + 2 * i
                    if peel != "last":
                        sp.wait_ge(gu_ok, e + 2)
                        load_up(it * 2 + (i + 2), i)
                    if not (peel == "first" and i == 0):
                        for r in range(2):
                            store(e + (r - 2), r)
                        if not (peel == "last" and i == 1):
                            load_down(it * 2 + (i + 1), (i + 1) % 2)

            turns(sp, run)
            store(EXPERTS - 2, 2)
            store(EXPERTS - 1, 3)
            for t in range(TILES):
                sp.wait_ge(tile_ok, t + 1)
                sp.dma_start(out_v[:, t, :], res[:, t, :]).then_inc(stored, 16)
            sp.wait_ge(stored, 16 * TILES)

        @block.gpsimd
        def _(pool):
            pool.wait_ge(recips_in, 16 * GH)
            for g in range(GROUPS):
                if g:
                    pool.wait_ge(spread_ok, g)
                pool.tensor_copy(den[0], attT[:, g, :]).then_inc(den_ok, 1)
                pool.wait_ge(spread_ok, g + 1)
                pool.tensor_tensor(attT[:, g, :], attT[:, g, :], den[1], ALU.mult).then_inc(norm_ok, 1)
            for i in range(2):
                pool.wait_ge(y_out[i], 16 * EXPERTS // 2)
            for t in range(TILES):
                if t >= 3:
                    pool.wait_ge(tile_ok, t - 2)
                for k in range(TOPK):
                    pool.indirect_dma_start(out=rows[t % 3][:, k, :], out_offset=None, in_=v["slot_y"],
                                            in_offset=bass.IndirectOffsetOnAxis(ap=slot[:, k, t:t + 1], axis=0),
                                            bounds_check=SLOTS, oob_is_err=False).then_inc(gathered[t % 3], 16)

        @block.scalar
        def _(act):
            def tokens(e, r):
                act.wait_ge(bufT_ps, e + 1)
                act.copy(xbT[r % 2].rearrange("p c t -> p (c t)"), psum[:, r % 2, 0:HID]).then_inc(bufT_ok, 1)

            def out_rows(e, r, stores):
                act.wait_ge(y_ps, e + 1)
                if stores is not None:
                    act.wait_ge(y_out[r % 2], 16 * stores)
                act.copy(ysb[r % 2], psum[:, 6 + r % 2, 0:HID]).then_inc(y_ok, 1)

            def run(it, peel):
                for r in range(4):
                    e = it * 4 + r
                    act.wait_ge(gu_ok, e + 1)
                    act.activation(silu[r % 2], psum[:, 2 + r % 2, 0:FF], ACT.Silu).then_inc(silu_ok, 1)
                    if not (peel == "last" and r == 3):
                        tokens(e + 1, r + 1)
                    if not (peel == "first" and r < 2):
                        out_rows(e - 2, r, None if peel == "first" else it * 2 + (r // 2 - 1))

            def shared_silu(b):
                for f in range(NF):
                    i = NF * b + f
                    if i == NF - 1:
                        tokens(0, 0)
                    act.wait_ge(sgu_ps, i + 1)
                    if i >= 2:
                        act.wait_ge(shid_ok, i - 1)
                    act.activation(ssilu[i % 2][0:FCH[f], :], psum[0:FCH[f], shared_bank(b, f), :], ACT.Silu).then_inc(ssilu_ok, 1)

            def out_resonance(b):
                act.wait_ge(ro_ps, b + 1)
                if b:
                    act.wait_ge(att_ps, 2 * b)
                act.copy(ro, psum[:, 4, :]).then_inc(ro_ok, 1)

            shared_silu(0)
            turns(act, run)
            out_rows(EXPERTS - 2, 0, EXPERTS // 2 - 1)
            out_rows(EXPERTS - 1, 1, EXPERTS // 2 - 1)
            for b in range(1, BLK):
                shared_silu(b)
                out_resonance(b - 1)
            out_resonance(BLK - 1)

        @block.tensor
        def _(pe):
            def run(it, peel):
                for r in range(4):
                    e = it * 4 + r
                    gate_up(pe, e, r)
                    if not (peel == "last" and r == 3):
                        tokens_T(pe, e + 1, (r + 1) % 4, it + (r + 1) // 4)
                    if peel == "first" and r == 1:
                        pe.wait_ge(shid_ok, NF)
                    if not (peel == "first" and r < 1):
                        hidden_T(pe, e - 1, (r - 1) % 4)
                    if not (peel == "first" and r < 2):
                        down(pe, e - 2, (r - 2) % 4, it + (r - 2) // 4)

            for f in range(2, NF):
                if f == NF - 1:
                    pe.wait_ge(shid_ok, 2)
                    tokens_T(pe, 0, 0, 0)
                shared_gate_up(pe, 0, f)
            turns(pe, run)
            hidden_T(pe, EXPERTS - 1, 3)
            down(pe, EXPERTS - 2, 2, ET - 1)
            down(pe, EXPERTS - 1, 3, ET - 1)
            for b in range(1, BLK):
                for f in range(NF):
                    shared_gate_up(pe, b, f)
                if b == 1:
                    pe.wait_ge(norm_ok, GROUPS)
                    pe.wait_ge(y_ok, EXPERTS)
                shared_tail(pe, b - 1)
            shared_tail(pe, BLK - 1)

        @block.vector
        def _(dve):
            steps = [0]

            def link(ins):
                steps[0] += 1
                ins.then_inc(mix_step, 1)
                dve.wait_ge(mix_step, steps[0])

            def shared_hidden(b):
                for f in range(NF):
                    i = NF * b + f
                    n = FCH[f]
                    if i == 3:
                        dve.wait_ge(sums_in, 16 * GH)
                        dve.reciprocal(rc, rc).then_inc(recip_ok, 1)
                    dve.wait_ge(ssilu_ok, i + 1)
                    if b >= 2:
                        dve.wait_ge(sh_ps, 2 * (b - 1))
                    dve.tensor_tensor(shid[0:n, NF * (b % 2) + f, :], ssilu[i % 2][0:n, :],
                                      psum[0:n, shared_bank(b, f) + 1, :], ALU.mult).then_inc(shid_ok, 1)

            def hidden_out(e, r, drained):
                dve.wait_ge(hidT_ps, e + 1)
                if drained:
                    dve.wait_ge(y_ps, e - 1)
                dve.tensor_copy(hidT[r % 2].rearrange("p c t -> p (c t)"), psum[0:FHALF, 4 + r % 2, 0:2 * P]).then_inc(hidT_ok, 1)

            def run(it, peel):
                for r in range(4):
                    e = it * 4 + r
                    if r == 2:
                        dve.wait_ge(den_ok, it + 1)
                    dve.wait_ge(silu_ok, e + 1)
                    dve.tensor_tensor(hid[r % 2], silu[r % 2], psum[:, 2 + r % 2, FF:2 * FF], ALU.mult).then_inc(hid_ok, 1)
                    if r == 2:
                        dve.stream_shuffle(den[1], den[0], [HD] * 32).then_inc(spread_ok, 1)
                    if not (peel == "first" and r < 1):
                        hidden_out(e - 1, (r - 1) % 4, not (peel == "first" and r < 3))

            def mix(b):
                for i in range(2):
                    n = 2 * b + i
                    dve.wait_ge(sh_ps, n + 1)
                    for t in range(2):
                        tile = 2 * n + t
                        last = dve.scalar_tensor_tensor(res[:, tile, :], psum[:, 6 + i, HID * t:HID * (t + 1)],
                                                        sgate[:, tile:tile + 1], res[:, tile, :], ALU.mult, ALU.add)
                    last.then_inc(sh_ok, 1)
                    dve.wait_ge(sh_ok, n + 1)
                    r2 = res[:, 2 * n:2 * n + 2, :].rearrange("p t h -> p (t h)")
                    dve.wait_ge(att_ps, n + 1)
                    dve.tensor_tensor(r2, r2, psum[:, 5, :], ALU.add).then_inc(att_ok, 1)
                    dve.wait_ge(att_ok, n + 1)
                    for t in range(2):
                        tile = 2 * n + t
                        dve.wait_ge(gathered[tile % 3], 16 * TOPK * (tile // 3 + 1))
                        for k in range(TOPK):
                            ins = dve.scalar_tensor_tensor(res[:, tile, :], rows[tile % 3][:, k, :], wsel[:, k, tile:tile + 1],
                                                           res[:, tile, :], ALU.mult, ALU.add)
                            if k == TOPK - 1:
                                ins.then_inc(tile_ok, 1)
                            else:
                                link(ins)

            shared_hidden(0)
            turns(dve, run)
            hidden_out(EXPERTS - 1, 3, True)
            for b in range(1, BLK):
                shared_hidden(b)
                mix(b - 1)
            mix(BLK - 1)




_INS = ['L0_attn_hidden_states', 'L0_attn_basis_q', 'L0_attn_phase_q', 'L0_attn_amp_q', 'L0_attn_basis_k',
        'L0_attn_phase_k', 'L0_attn_amp_k', 'L0_attn_basis_v', 'L0_attn_phase_v', 'L0_attn_amp_v',
        'L0_attn_basis_o', 'L0_attn_phase_o', 'L0_attn_amp_o', 'L0_ffn_w_norm', 'L0_ffn_w_router', 'L0_ffn_w_gate',
        'L0_ffn_w_up', 'L0_ffn_w_down', 'L0_ffn_sw_gate', 'L0_ffn_sw_up', 'L0_ffn_sw_down', 'L0_ffn_w_shared_gate']
_OUTS = [((2, 1024, 256), 'float32')]


def kernel(**inputs):
    import numpy as _np
    import concourse.bacc as _bacc
    from concourse import mybir as _mybir
    from concourse.bass_utils import run_bass_kernel_spmd as _run

    nc = _bacc.Bacc("TRN2", target_bir_lowering=False, num_devices=1)
    arrays, args = {}, []
    for name in _INS:
        a = _np.ascontiguousarray(inputs[name])
        arrays[f"in_{name}_dram"] = a
        args.append(nc.dram_tensor(f"in_{name}_dram", a.shape, _mybir.dt.from_np(a.dtype), kind="ExternalInput").ap())
    for i, (shape, dtype) in enumerate(_OUTS):
        dt = _mybir.dt.from_np(_np.dtype(dtype))
        args.append(nc.dram_tensor(f"out_{i}_dram", shape, dt, kind="ExternalOutput").ap())
    build(nc, *args)
    r = _run(nc, [arrays], core_ids=[0])
    got = tuple(r.results[0][f"out_{i}_dram"] for i in range(len(_OUTS)))
    return got[0]
```
